# Optimizing a Trainium2 kernel written in Bass

```python
import numpy as np
import jax
import jax.numpy as jnp

def _softmax(x, axis=-1):
    return jax.nn.softmax(x, axis=axis)

def _gelu(x):
    return jax.nn.gelu(x, approximate=True)

def _silu(x):
    return jax.nn.silu(x)

def _sigmoid(x):
    return jax.nn.sigmoid(x)

def _layernorm(x, axis=-1, eps=1e-05):
    m = jnp.mean(x, axis=axis, keepdims=True)
    v = jnp.var(x, axis=axis, keepdims=True)
    return (x - m) / jnp.sqrt(v + eps)

def _scatter_add(tgt, idx, src, axis=0):
    return tgt.at[idx].add(src)

def _segment_sum(src, seg, n):
    return jax.ops.segment_sum(src, seg, n)
kernel_name = 'mk_prb_d1_jaxref_r4_0816fc'

def setup_inputs(seed: int=0):
    np.random.seed(seed)
    _w = jnp.asarray

    def _L0_attn_setup():
        import jax, jax.numpy as jnp
        import numpy as np
        B, L, DM = (2, 256, 512)
        DIN, N, DTR, K = (512, 16, 128, 4)
        key = jax.random.key(seed)
        ks = jax.random.split(key, 8)
        s = lambda k, sh: jax.random.normal(k, sh, jnp.float32) * 0.02
        A = jnp.tile(jnp.arange(1, N + 1, dtype=jnp.float32)[None, :], (DIN, 1))
        return {'x': jax.random.normal(ks[0], (B, L, DM), jnp.float32), 'W_in': s(ks[1], (DM, 2 * DIN)), 'conv_w': s(ks[2], (DIN, DIN, K)), 'conv_b': jnp.zeros((DIN,), jnp.float32), 'W_x': s(ks[3], (DIN, DTR + 2 * N)), 'W_dt': s(ks[4], (DTR, DIN)), 'b_dt': jnp.zeros((DIN,), jnp.float32), 'A_log': jnp.log(A), 'D': jnp.ones((DIN,), jnp.float32), 'W_out': s(ks[5], (DIN, DM))}
    _L0_attn_in = _L0_attn_setup()

    def _L0_ffn_setup():
        import jax, jax.numpy as jnp
        import numpy as np
        E = 8
        TOP_K = 2
        D = 512
        M = 1792
        B, S = (2, 512)
        key = jax.random.key(seed)
        kx, kg, k1, k2, k3 = jax.random.split(key, 5)
        x = jax.random.normal(kx, (B, S, D), dtype=jnp.float32)
        gate_w = jax.random.normal(kg, (D, E), dtype=jnp.float32) / np.sqrt(D)
        w1 = jax.random.normal(k1, (E, D, M), dtype=jnp.float32) / np.sqrt(D)
        w2 = jax.random.normal(k2, (E, M, D), dtype=jnp.float32) / np.sqrt(M)
        w3 = jax.random.normal(k3, (E, D, M), dtype=jnp.float32) / np.sqrt(D)
        return {'x': x, 'gate_w': gate_w, 'w1': w1, 'w2': w2, 'w3': w3}
    _L0_ffn_in = _L0_ffn_setup()
    _d = {'L0_attn_x': _L0_attn_in['x'], 'L0_attn_W_in': _L0_attn_in['W_in'], 'L0_attn_conv_w': _L0_attn_in['conv_w'], 'L0_attn_conv_b': _L0_attn_in['conv_b'], 'L0_attn_W_x': _L0_attn_in['W_x'], 'L0_attn_W_dt': _L0_attn_in['W_dt'], 'L0_attn_b_dt': _L0_attn_in['b_dt'], 'L0_attn_A_log': _L0_attn_in['A_log'], 'L0_attn_D': _L0_attn_in['D'], 'L0_attn_W_out': _L0_attn_in['W_out'], 'L0_ffn_gate_w': _L0_ffn_in['gate_w'], 'L0_ffn_w1': _L0_ffn_in['w1'], 'L0_ffn_w2': _L0_ffn_in['w2'], 'L0_ffn_w3': _L0_ffn_in['w3']}
    _x0 = _d['L0_attn_x']
    _d['L0_attn_x'] = jax.random.normal(jax.random.fold_in(jax.random.key(seed), 1), (4, 1024, 512), dtype=_x0.dtype)
    del _x0
    return _d

def reference(L0_attn_x, L0_attn_W_in, L0_attn_conv_w, L0_attn_conv_b, L0_attn_W_x, L0_attn_W_dt, L0_attn_b_dt, L0_attn_A_log, L0_attn_D, L0_attn_W_out, L0_ffn_gate_w, L0_ffn_w1, L0_ffn_w2, L0_ffn_w3):

    def _L0_attn_ref(x, W_in, conv_w, conv_b, W_x, W_dt, b_dt, A_log, D, W_out):
        import jax, jax.numpy as jnp
        import numpy as np
        B, L, DM = (2, 256, 512)
        DIN, N, DTR, K = (512, 16, 128, 4)
        b, l, _ = x.shape
        n = A_log.shape[1]
        dtr = W_dt.shape[0]
        xz = x @ W_in
        xc, r = jnp.split(xz, 2, axis=-1)
        xt = xc.transpose(0, 2, 1)
        xconv = jax.lax.conv_general_dilated(xt, conv_w, (1,), [(conv_w.shape[2] - 1, 0)], dimension_numbers=('NCH', 'OIH', 'NCH'))
        xs = (xconv + conv_b[None, :, None]).transpose(0, 2, 1)
        u = jax.nn.silu(xs)
        A = -jnp.exp(A_log)
        dbc = u @ W_x
        delta = jax.nn.softplus(dbc[..., :dtr] @ W_dt + b_dt)
        Bm = dbc[..., dtr:dtr + n]
        Cm = dbc[..., dtr + n:]
        deltaA = jnp.exp(jnp.einsum('bld,dn->lbdn', delta, A))
        deltaBu = jnp.einsum('bld,bln->lbdn', delta * u, Bm)

        def step(h, inp):
            dA, dBu, c = inp
            h = dA * h + dBu
            return (h, jnp.einsum('bdn,bn->bd', h, c))
        h0 = jnp.zeros((b, u.shape[-1], n), u.dtype)
        _, ys = jax.lax.scan(step, h0, (deltaA, deltaBu, Cm.transpose(1, 0, 2)))
        y = ys.transpose(1, 0, 2) + u * D
        out = y * jax.nn.silu(r)
        return out @ W_out + xs

    def _L0_ffn_ref(x, gate_w, w1, w2, w3):
        import jax, jax.numpy as jnp
        import numpy as np
        E = 8
        TOP_K = 2
        D = 512
        M = 1792
        B, S = (2, 512)
        b, s, d = x.shape
        x_flat = x.reshape(-1, d)
        router_logits = x_flat @ gate_w
        router_probs = jax.nn.softmax(router_logits, axis=-1)
        topk_w, topk_idx = jax.lax.top_k(router_probs, TOP_K)
        topk_w = topk_w / jnp.sum(topk_w, axis=-1, keepdims=True)
        idx_flat = topk_idx.reshape(-1)
        sort_idx = jnp.argsort(idx_flat)
        x_rep_sort = jnp.take(x_flat, sort_idx // TOP_K, axis=0)
        group_sizes = jnp.bincount(idx_flat, length=E).astype(jnp.int32)
        h = jax.lax.ragged_dot(x_rep_sort, w1, group_sizes)
        h = jax.nn.silu(h) * jax.lax.ragged_dot(x_rep_sort, w3, group_sizes)
        out_sort = jax.lax.ragged_dot(h, w2, group_sizes)
        inv_sort_idx = jnp.argsort(sort_idx)
        out_rep = jnp.take(out_sort, inv_sort_idx, axis=0).reshape(-1, TOP_K, d)
        out = jnp.einsum('tkd,tk->td', out_rep, topk_w)
        return out.reshape(b, s, d)
    x = L0_attn_x
    xn = _layernorm(x, axis=-1)
    x = x + _L0_attn_ref(xn, L0_attn_W_in, L0_attn_conv_w, L0_attn_conv_b, L0_attn_W_x, L0_attn_W_dt, L0_attn_b_dt, L0_attn_A_log, L0_attn_D, L0_attn_W_out) + _L0_ffn_ref(xn, L0_ffn_gate_w, L0_ffn_w1, L0_ffn_w2, L0_ffn_w3)
    return x

_drawn_inputs = setup_inputs


def setup_inputs(seed=0):
    import zlib

    import numpy as np

    out = dict(_drawn_inputs(seed))
    spreads = {'L0_attn_conv_b': (0.0, 0.1), 'L0_attn_b_dt': (0.0, 2.0), 'L0_attn_D': (1.0, 0.6)}
    factors = {'L0_attn_W_x': 8.0, 'L0_attn_W_dt': 8.0, 'L0_attn_A_log': 41.875}
    for name, (base, spread) in spreads.items():
        noise = np.random.default_rng([zlib.crc32(name.encode()), seed]).standard_normal(out[name].shape)
        drawn = base * np.exp(spread * noise) if base else spread * noise
        out[name] = jnp.asarray(drawn.astype(out[name].dtype))
    for name, factor in factors.items():
        out[name] = (out[name] * factor).astype(out[name].dtype)
    return out
```

```python
from contextlib import ExitStack

import concourse.bass as bass
from concourse import mybir

F32 = mybir.dt.float32
I32 = mybir.dt.int32
U32 = mybir.dt.uint32
ACT = mybir.ActivationFunctionType
ALU = mybir.AluOpType
AX = mybir.AxisListType
ds = bass.ds

P = 128
BATCH, SEQ, DM = 4, 1024, 512
TOKENS = BATCH * SEQ
DC = DM // P
DIN, NST, DTR, KC = 512, 16, 128, 4
CC = DIN // P
NX = DTR + 2 * NST
HALF = 512
NH = SEQ // HALF
E, TOP = 8, 2
MH = 1792
TT = TOKENS // P
TPB = SEQ // P
SLOTS = 256
SH = SLOTS // P
SHIFT = 8
GROUP = 9
PLAIN = 4
NT = BATCH * GROUP + PLAIN
assert NT >= (TOKENS * TOP - E) // SLOTS + E
IDW = (NT + 1) * SH
NF = MH // P
NWC = NF // 2
EPS = 1e-5
LOG_MAX = 80.0


def dram(nc, name, shape, dt=F32):
    return nc.dram_tensor(name, shape, dt, kind="Internal").ap()


def bcast(ap, shape):
    return ap.broadcast_to(shape)


def norm_and_route_logits(nc, t, d):
    GT = 4
    NG = TT // GT
    with ExitStack() as ctx:
        sb = lambda n, s, dt=F32: ctx.enter_context(nc.sbuf_tensor(n, s, dt))
        sem = lambda n: ctx.enter_context(nc.semaphore(n))
        xin = [sb(f"xin{i}", [P, GT, DM]) for i in range(2)]
        xno = [sb(f"xno{i}", [P, GT, DM]) for i in range(2)]
        st = sb("ln_stats", [P, GT, 6])
        mv = sb("ln_mean_var", [P, GT, 2])
        ve = sb("ln_var_eps", [P, GT])
        sd = sb("ln_std", [P, GT])
        r0 = sb("ln_rstd0", [P, GT])
        r1 = sb("ln_newton", [P, GT])
        rs = sb("ln_rstd", [P, GT])
        ptr = [ctx.enter_context(nc.psum_tensor(f"ptr{i}", [P, HALF], F32)) for i in range(4)]
        x_in = [sem(f"x_in{i}") for i in range(2)]
        var_ready = sem("var_ready")
        std_ready = sem("std_ready")
        ln_step = sem("ln_step")
        ln_sync = sem("ln_sync")
        xn_ready = sem("xn_ready")
        xn_stored = [sem(f"xn_stored{i}") for i in range(2)]
        tr_ready = sem("tr_ready")
        tr_copied = sem("tr_copied")
        consts = sem("consts1")
        x_v = d["x"].rearrange("(g t p) c -> g p t c", p=P, t=GT)
        xn_v = d["xn"].rearrange("(g t p) c -> g p t c", p=P, t=GT)
        block = ctx.enter_context(nc.Block())

        @block.sync
        def _(eng):
            for i in range(2):
                eng.dma_start(xin[i][:, :, :], x_v[i]).then_inc(x_in[i], 16)
            eng.dma_start(t.gate[:, :, :], d["gate_w"].rearrange("(c p) e -> p c e", p=P)).then_inc(t.gate_in, 16)
            eng.dma_start(t.conv_b[:, :], d["conv_b"]).then_inc(t.small_in, 16)
            eng.dma_start(t.b_dt[:, :], d["b_dt"]).then_inc(t.small_in, 16)
            eng.dma_start(t.D[:, :], d["D"]).then_inc(t.small_in, 16)
            eng.dma_start(t.A_log[:, :, :], d["A_log"].rearrange("(c p) n -> p c n", p=P)).then_inc(t.small_in, 16)
            eng.dma_start(t.W_in[:, :, :], d["W_in"].rearrange("(c p) n -> p c n", p=P)).then_inc(t.w_in, 16)
            with eng.Fori(0, NG // 2 - 1) as g:
                for i in range(2):
                    eng.wait_ge(xn_ready, (g * 2 + i + 1) * GT)
                    eng.dma_start(xin[i][:, :, :], x_v[ds(g * 2 + i + 2, 1)].rearrange("o p t c -> (o p) t c")).then_inc(x_in[i], 16)
            eng.dma_start(t.conv_w[:, :, :, :], d["conv_w"].rearrange("k (c p) o -> p k c o", p=P)).then_inc(t.w_in, 16)
            eng.dma_start(t.W_x[:, :, :], d["W_x"].rearrange("(c p) n -> p c n", p=P)).then_inc(t.w_in, 16)
            eng.dma_start(t.W_dt[:, :], d["W_dt"]).then_inc(t.w_in, 16)

        @block.vector
        def _(eng):
            def group(g, i):
                base = g * (2 * (GT + 6)) + i * (GT + 6)
                eng.wait_ge(x_in[i], g * 16 + 16)
                for k in range(GT):
                    eng.bn_stats(st[:, k, :], xin[i][:, k, :]).then_inc(ln_step, 1)
                eng.wait_ge(ln_step, base + GT)
                eng.sem_inc(ln_sync, 1)
                for k in range(GT):
                    last = eng.bn_aggr(mv[:, k, :], st[:, k, :])
                last.then_inc(ln_step, 1)
                eng.wait_ge(ln_step, base + GT + 1)
                eng.tensor_scalar(ve[:, :], mv[:, :, 1], EPS, None, ALU.add).then_inc(var_ready, 1)
                eng.wait_ge(std_ready, g * 2 + i + 1)
                eng.reciprocal(r0[:, :], sd[:, :]).then_inc(ln_step, 1)
                eng.wait_ge(ln_step, base + GT + 2)
                eng.tensor_tensor(r1[:, :], r0[:, :], r0[:, :], ALU.mult).then_inc(ln_step, 1)
                eng.wait_ge(ln_step, base + GT + 3)
                eng.tensor_tensor(r1[:, :], r1[:, :], ve[:, :], ALU.mult).then_inc(ln_step, 1)
                eng.wait_ge(ln_step, base + GT + 4)
                eng.tensor_scalar(r1[:, :], r1[:, :], -0.5, 1.5, ALU.mult, ALU.add).then_inc(ln_step, 1)
                eng.wait_ge(ln_step, base + GT + 5)
                eng.tensor_tensor(rs[:, :], r1[:, :], r0[:, :], ALU.mult).then_inc(ln_step, 1)
                eng.wait_ge(ln_step, base + GT + 6)
                eng.wait_ge(xn_stored[i], g * 16 + 16)
                eng.wait_ge(tr_ready, (g * 2 + i) * 4 + 4)
                for k in range(GT):
                    last = eng.tensor_scalar(xno[i][:, k, :], xin[i][:, k, :], mv[:, k, 0:1], rs[:, k:k + 1],
                                             ALU.subtract, ALU.mult).then_inc(xn_ready, 1)

            with eng.Fori(0, NG // 2) as g:
                for i in range(2):
                    group(g, i)

        @block.gpsimd
        def _(eng):
            eng.memset(t.ident[:, :], 0.0).then_inc(consts, 1)
            eng.memset(t.tri[:, :], 1.0).then_inc(consts, 1)
            eng.memset(t.ones[:, :], 1.0).then_inc(consts, 1)
            eng.wait_ge(consts, 3)
            eng.affine_select(out=t.ident[:, :], in_=t.ident[:, :], compare_op=ALU.not_equal, fill=1.0,
                              base=0, pattern=[[-1, P]], channel_multiplier=1).then_inc(t.const_ready, 1)
            eng.affine_select(out=t.tri[:, :], in_=t.tri[:, :], compare_op=ALU.is_gt, fill=0.0,
                              base=0, pattern=[[1, P]], channel_multiplier=-1).then_inc(t.const_ready, 1)
            eng.iota(t.tok_id[:, :], pattern=[[P, TT]], base=0, channel_multiplier=1).then_inc(t.const_ready, 1)
            eng.iota(t.num_i[:, :], pattern=[[1, NT]], base=0, channel_multiplier=0).then_inc(t.const_ready, 1)
            eng.memset(t.zero_ids[:, :], 0).then_inc(t.const_ready, 1)
            eng.memset(t.xcT[:, :, 0:KC - 1], 0.0).then_inc(t.const_ready, 1)
            eng.wait_ge(t.const_ready, 6)
            eng.dma_start(d["ids"].rearrange("(p w) o -> p (w o)", p=P), t.zero_ids[:, :]).then_inc(t.ids_zeroed, 16)

        @block.scalar
        def _(eng):
            def group(g, i):
                eng.wait_ge(var_ready, g * 2 + i + 1)
                eng.activation(sd[:, :], ve[:, :], ACT.Sqrt).then_inc(std_ready, 1)
                eng.wait_ge(xn_ready, (g * 2 + i + 1) * GT)
                eng.dma_start(xn_v[ds(g * 2 + i, 1)].rearrange("o p t c -> (o p) t c"), xno[i][:, :, :]).then_inc(xn_stored[i], 16)
                for c in range(DC):
                    eng.wait_ge(tr_ready, (g * 2 + i) * 4 + c + 1 + 8)
                    eng.activation(t.xnT[:, c, ds((g * 2 + i) * HALF, HALF)], ptr[c][:, :], ACT.Copy).then_inc(tr_copied, 1)
            with eng.Fori(0, NG // 2) as g:
                for i in range(2):
                    group(g, i)
            for i in range(2):
                eng.wait_ge(xn_stored[i], NG * 8 + 16)

        @block.tensor
        def _(eng):
            for i in range(2):
                eng.sem_inc(xn_stored[i], 16)
            eng.sem_inc(tr_ready, 8)
            eng.sem_inc(tr_copied, 4)
            eng.wait_ge(t.const_ready, 6)
            eng.wait_ge(t.gate_in, 16)

            def group(g, i):
                eng.wait_ge(xn_ready, (g * 2 + i + 1) * GT)
                for c in range(DC):
                    eng.wait_ge(tr_copied, (g * 2 + i) * 4 + c + 1)
                    for k in range(GT):
                        last = eng.transpose(ptr[c][:, k * P:(k + 1) * P], xno[i][:, k, c * P:(c + 1) * P], t.ident[:, :])
                    last.then_inc(tr_ready, 1)

            with eng.Fori(0, NG // 2) as g:
                for i in range(2):
                    group(g, i)
            eng.wait_ge(tr_copied, NG * 4 + 4)
            for i in range(TT):
                for c in range(DC):
                    last = eng.matmul(t.ps_lg[:, i * E:(i + 1) * E], t.xnT[:, c, i * P:(i + 1) * P], t.gate[:, c, :],
                                      start=(c == 0), stop=(c == DC - 1), skip_group_check=True)
            last.then_inc(t.logits_ready, 1)


def mamba_front(nc, t, d):
    JOBS = 36
    RING = 6
    XC_X = 12
    with ExitStack() as ctx:
        sb = lambda n, s, dt=F32: ctx.enter_context(nc.sbuf_tensor(n, s, dt))
        sem = lambda n: ctx.enter_context(nc.semaphore(n))
        u2 = sb("u2", [P, CC, SEQ])
        din = sb("din", [P, SEQ])
        bcT = sb("bcT", [2 * NST, SEQ])
        th = [sb(f"th_r{i}", [P, HALF]) for i in range(2)]
        th2 = [sb(f"th_x{i}", [P, HALF]) for i in range(2)]
        srp = [sb(f"sr_piece{i}", [P, HALF]) for i in range(2)]
        xsp = [sb(f"xs_piece{i}", [P, HALF]) for i in range(2)]
        udp = [sb(f"ud_piece{i}", [P, HALF]) for i in range(2)]
        dlp = [sb(f"delta_piece{i}", [P, HALF]) for i in range(4)]
        dup = [sb(f"du_piece{i}", [P, HALF]) for i in range(4)]
        ez = th + th2
        w1m = t.hot[:, :, :, :].rearrange("p k i e -> p (k i e)")
        ring = [ctx.enter_context(nc.psum_tensor(f"front{i}", [P, HALF], F32)) for i in range(RING)]
        ps_rt = ctx.enter_context(nc.psum_tensor("ps_rt", [P, HALF], F32))
        bank_full = sem("bank_full")
        act_freed = sem("act_freed")
        th_r = sem("th_r")
        sr_ready = sem("sr_ready")
        sr_out = [sem(f"sr_out{i}") for i in range(2)]
        xs_ready = sem("xs_ready")
        xs_out = [sem(f"xs_out{i}") for i in range(2)]
        th_x = sem("th_x")
        u_ready = sem("u_ready")
        ud_ready = sem("ud_ready")
        ud_out = [sem(f"ud_out{i}") for i in range(2)]
        bc_out = sem("bc_out")
        abs_ready = sem("abs_ready")
        exp_ready = sem("exp_ready")
        z_ready = sem("z_ready")
        ln_ready = sem("ln_ready")
        sp_step = sem("softplus_step")
        delta_ready = sem("delta_ready")
        delta_out = [sem(f"delta_out{i}") for i in range(4)]
        du_ready = sem("du_ready")
        du_out = [sem(f"du_out{i}") for i in range(4)]
        r_step = sem("route_step")
        r_exp = sem("route_exp")
        r_max = sem("route_max")
        r_mask = sem("route_mask")
        r_count = sem("route_count")
        slots_ready = sem("slots_ready")
        block = ctx.enter_context(nc.Block())

        pieces = [(c, h) for c in range(CC) for h in range(NH)]

        def row(name, b, c, h):
            return d[name][ds(b, 1), :, c, h * HALF:(h + 1) * HALF].rearrange("o p n -> (o p) n")

        @block.tensor
        def _(eng):
            eng.wait_ge(r_mask, 1)
            eng.matmul(ps_rt[:, 0:TT * E], t.tri[:, :], t.mask[:, :, :].rearrange("p i e -> p (i e)"), start=True, stop=True)
            eng.matmul(ps_rt[:, TT * E:2 * TT * E], t.ones[:, :], t.mask[:, :, :].rearrange("p i e -> p (i e)"),
                       start=False, stop=True, skip_group_check=True).then_inc(r_count, 1)
            eng.wait_ge(t.w_in, 64)
            with eng.Fori(0, BATCH) as b:
                q = 0
                owner = ([(act_freed, XC_X, n + 1) for n in range(8)]
                         + [(sr_ready, 8, n + 1 + 2) for n in range(8)]
                         + [(xs_ready, 8, n + 1) for n in range(8)]
                         + [(act_freed, XC_X, n + 1) for n in range(8, 12)]
                         + [(z_ready, 8, n + 1 + 8) for n in range(8)])

                def bank():
                    s, per, n = owner[(q - RING) % JOBS]
                    eng.wait_ge(s, b * per + n - (per if q < RING else 0))
                    return ring[q % RING]

                for m in range(2 * CC):
                    for h in range(NH):
                        o = bank()
                        for c in range(DC):
                            last = eng.matmul(o[:, :], t.W_in[:, c, m * P:(m + 1) * P],
                                              t.xnT[:, c, ds(b * SEQ + h * HALF, HALF)], start=(c == 0), stop=(c == DC - 1))
                        last.then_inc(bank_full, 1)
                        q += 1
                for m, h in pieces:
                    o = bank()
                    if m == 0 and h == 0:
                        eng.wait_ge(act_freed, b * XC_X + 8)
                    for k in range(KC):
                        for c in range(CC):
                            last = eng.matmul(o[:, :], t.conv_w[:, k, c, m * P:(m + 1) * P],
                                              t.xcT[:, c, h * HALF + k:h * HALF + k + HALF],
                                              start=(k == 0 and c == 0), stop=(k == KC - 1 and c == CC - 1))
                    last.then_inc(bank_full, 1)
                    q += 1
                for part in range(2):
                    for h in range(NH):
                        o = bank()
                        eng.wait_ge(u_ready, b * 8 + 8 + 2)
                        lo, hi = (0, DTR) if part == 0 else (DTR, NX)
                        for c in range(CC):
                            last = eng.matmul(o[0:hi - lo, :], t.W_x[:, c, lo:hi], u2[:, c, h * HALF:(h + 1) * HALF],
                                              start=(c == 0), stop=(c == CC - 1))
                        last.then_inc(bank_full, 1)
                        q += 1
                for m, h in pieces:
                    o = bank()
                    eng.wait_ge(act_freed, b * XC_X + 10)
                    eng.matmul(o[:, :], t.W_dt[:, m * P:(m + 1) * P], din[:, h * HALF:(h + 1) * HALF],
                               start=True, stop=True).then_inc(bank_full, 1)
                    q += 1

        @block.scalar
        def _(eng):
            eng.wait_ge(t.a_step, 1)
            eng.activation(t.A[:, :, :], t.A_log[:, :, :], ACT.Exp).then_inc(t.a_step, 1)
            eng.wait_ge(t.a_step, 2)
            eng.activation(t.A[:, :, :], t.A[:, :, :], ACT.Copy, scale=-1.0).then_inc(t.a_step, 1)
            eng.wait_ge(r_max, 1)
            eng.activation(t.prob[:, :, :], t.prob[:, :, :], ACT.Exp).then_inc(r_exp, 1)
            with eng.Fori(0, BATCH) as b:
                q = 0
                for m, h in pieces:
                    eng.wait_ge(bank_full, b * JOBS + q + 1)
                    eng.activation(t.xcT[:, m, KC - 1 + h * HALF:KC - 1 + (h + 1) * HALF], ring[q % RING][:, :],
                                   ACT.Copy).then_inc(act_freed, 1)
                    q += 1
                eng.wait_ge(delta_ready, b * 8 + 4)
                for i in range(8):
                    eng.wait_ge(bank_full, b * JOBS + q + 1)
                    eng.wait_ge(sr_ready, b * 8 + i + 1)
                    eng.activation(th[i % 2][:, :], ring[q % RING][:, :], ACT.Tanh, scale=0.5).then_inc(th_r, 1)
                    q += 1
                for i in range(8):
                    eng.wait_ge(xs_ready, b * 8 + i + 1)
                    eng.wait_ge(u_ready, b * 8 + i + 1)
                    eng.activation(th2[i % 2][:, :], xsp[i % 2][:, :], ACT.Tanh, scale=0.5).then_inc(th_x, 1)
                    q += 1
                for h in range(NH):
                    eng.wait_ge(bank_full, b * JOBS + q + 1)
                    eng.activation(din[:, h * HALF:(h + 1) * HALF], ring[q % RING][:, :], ACT.Copy,
                                   scale=0.5).then_inc(act_freed, 1)
                    q += 1
                for h in range(NH):
                    eng.wait_ge(bank_full, b * JOBS + q + 1)
                    eng.wait_ge(bc_out, b * 32 + 32)
                    eng.activation(bcT[:, h * HALF:(h + 1) * HALF], ring[q % RING][0:2 * NST, :], ACT.Copy,
                                   scale=0.5).then_inc(act_freed, 1)
                    q += 1
                for quad in range(0, 8, 4):
                    for i in range(quad, quad + 4):
                        m = pieces[i][0]
                        eng.wait_ge(bank_full, b * JOBS + q + 1)
                        eng.wait_ge(delta_ready, b * 8 + i + 1)
                        eng.activation(ez[i % 4][:, :], ring[q % RING][:, :], ACT.Abs,
                                       bias=t.b_dt[:, m:m + 1]).then_inc(abs_ready, 1)
                        q += 1
                    for i in range(quad, quad + 4):
                        eng.wait_ge(abs_ready, b * 8 + i + 1)
                        eng.activation(ez[i % 4][:, :], ez[i % 4][:, :], ACT.Exp, scale=-1.0).then_inc(exp_ready, 1)
                    for i in range(quad, quad + 4):
                        eng.wait_ge(exp_ready, b * 8 + i + 1)
                        eng.wait_ge(delta_out[i % 4], (b * 2 + i // 4 + 1) * 16)
                        eng.wait_ge(du_ready, b * 8 + i + 1)
                        eng.activation(dlp[i % 4][:, :], ez[i % 4][:, :], ACT.Ln, bias=1.0).then_inc(ln_ready, 1)

        @block.vector
        def _(eng):
            for out in (sr_out, xs_out, ud_out, delta_out, du_out):
                for o in out:
                    eng.sem_inc(o, 16)
            eng.sem_inc(bc_out, 32)
            eng.sem_inc(sr_ready, 2)
            eng.sem_inc(du_ready, 4)
            eng.sem_inc(u_ready, 2)
            eng.sem_inc(z_ready, 8)
            eng.sem_inc(delta_ready, 4)
            eng.wait_ge(t.small_in, 64)
            eng.tensor_scalar(t.A_log[:, :, :], t.A_log[:, :, :], LOG_MAX, None, ALU.min).then_inc(t.a_step, 1)
            step = [0]

            def link(ins):
                step[0] += 1
                ins.then_inc(r_step, 1)
                eng.wait_ge(r_step, step[0])

            link(eng.tensor_copy(t.prob[:, :, :].rearrange("p i e -> p (i e)"), t.ps_lg[:, 0:TT * E]))
            link(eng.tensor_reduce(t.red[:, :], t.prob[:, :, :], AX.X, ALU.max))
            eng.tensor_tensor(t.prob[:, :, :], t.prob[:, :, :], bcast(t.red[:, :].unsqueeze(2), [P, TT, E]),
                              ALU.subtract).then_inc(r_max, 1)
            eng.wait_ge(r_exp, 1)
            link(eng.tensor_reduce(t.red[:, :], t.prob[:, :, :], AX.X, ALU.add))
            link(eng.reciprocal(t.red2[:, :], t.red[:, :]))
            link(eng.tensor_tensor(t.prob[:, :, :], t.prob[:, :, :], bcast(t.red2[:, :].unsqueeze(2), [P, TT, E]), ALU.mult))
            for i in range(TT):
                eng.max(t.top[:, i, :], t.prob[:, i, :]).then_inc(r_step, 1)
            step[0] += TT
            eng.wait_ge(r_step, step[0])
            for i in range(TT):
                eng.max_index(t.topi[:, i, :], t.top[:, i, :], t.prob[:, i, :]).then_inc(r_step, 1)
            step[0] += TT
            eng.wait_ge(r_step, step[0])
            link(eng.tensor_tensor(t.red[:, :], t.top[:, :, 0], t.top[:, :, 1], ALU.add))
            link(eng.reciprocal(t.red2[:, :], t.red[:, :]))
            for k in range(TOP):
                link(eng.tensor_tensor(t.wgt[:, k, :], t.top[:, :, k], t.red2[:, :], ALU.mult))
                link(eng.tensor_copy(t.topf[:, k, :], t.topi[:, :, k]))
            eng.wait_ge(t.const_ready, 6)
            link(eng.tensor_copy(t.num[:, :], t.num_i[:, :]))
            for k in range(TOP):
                link(eng.tensor_tensor(t.hot[:, k, :, :], bcast(t.num[:, 0:E].unsqueeze(1), [P, TT, E]),
                                       bcast(t.topf[:, k, :].unsqueeze(2), [P, TT, E]), ALU.is_equal))
            eng.tensor_tensor(t.mask[:, :, :], t.hot[:, 0, :, :], t.hot[:, 1, :, :], ALU.add).then_inc(r_mask, 1)
            eng.wait_ge(r_count, 1)
            rank = ps_rt[:, 0:TT * E].rearrange("p (i e) -> p i e", e=E)
            total = ps_rt[:, TT * E:2 * TT * E].rearrange("p (i e) -> p e i", e=E)
            link(eng.tensor_copy(t.tot[:, :, :], total))
            for e in range(E):
                link(eng.tensor_tensor_scan(t.cum[:, e, :], t.ones[:, 0:TT], t.tot[:, e, :], 0.0, ALU.mult, ALU.add))
            link(eng.tensor_scalar(t.cnt_i[:, :], t.cum[:, :, TT - 1], float(SLOTS - 1), None, ALU.add))
            link(eng.tensor_scalar(t.cnt_i[:, :], t.cnt_i[:, :], SHIFT, None, ALU.arith_shift_right))
            link(eng.tensor_copy(t.ntile[:, :], t.cnt_i[:, :]))
            link(eng.tensor_tensor_scan(t.last_tile[:, :], t.ones[:, 0:E], t.ntile[:, :], 0.0, ALU.mult, ALU.add))
            link(eng.tensor_tensor(t.base[:, :], t.last_tile[:, :], t.ntile[:, :], ALU.subtract))
            link(eng.tensor_scalar(t.base[:, :], t.base[:, :], float(SLOTS), None, ALU.mult))
            link(eng.tensor_tensor(t.cum[:, :, :], t.cum[:, :, :], t.tot[:, :, :], ALU.subtract))
            link(eng.tensor_tensor(t.cum[:, :, :], t.cum[:, :, :], bcast(t.base[:, :].unsqueeze(2), [P, E, TT]), ALU.add))
            link(eng.tensor_tensor(t.prob[:, :, :], t.cum[:, :, :].rearrange("p e i -> p i e"), rank, ALU.add))
            for k in range(TOP):
                link(eng.tensor_tensor(t.hot[:, k, :, :], t.hot[:, k, :, :], t.prob[:, :, :], ALU.mult))
                link(eng.tensor_reduce(t.topf[:, k, :], t.hot[:, k, :, :], AX.X, ALU.add))
            link(eng.tensor_copy(t.slot[:, :, :], t.topf[:, :, :]))
            link(eng.tensor_scalar(t.place[:, :, :], t.slot[:, :, :], P - 1, None, ALU.bitwise_and))
            link(eng.tensor_scalar(t.place2[:, :, :], t.slot[:, :, :], 7, None, ALU.logical_shift_right))
            eng.scalar_tensor_tensor(out=t.place[:, :, :], in0=t.place[:, :, :], scalar=float(IDW),
                                     in1=t.place2[:, :, :], op0=ALU.mult, op1=ALU.add).then_inc(slots_ready, 1)
            link(eng.tensor_tensor(t.cmp[:, :, :], bcast(t.num[:, :].unsqueeze(2), [P, NT, E - 1]),
                                   bcast(t.last_tile[:, 0:E - 1].unsqueeze(1), [P, NT, E - 1]), ALU.is_ge))
            link(eng.tensor_reduce(t.texp[:, :], t.cmp[:, :, :], AX.X, ALU.add))
            link(eng.tensor_copy(t.meta[:, 0, :], t.texp[:, :]))
            link(eng.memset(t.meta[:, 1, :], 1))
            link(eng.tensor_tensor(t.meta[:, 1, 1:NT], t.texp[:, 1:NT], t.texp[:, 0:NT - 1], ALU.not_equal))
            link(eng.tensor_tensor(t.meta[:, 2, :], t.num[:, :], bcast(t.last_tile[:, E - 1:E], [P, NT]), ALU.is_lt))

            eng.wait_ge(t.small_in, 64)
            with eng.Fori(0, BATCH) as b:
                q = 8
                for i in range(8):
                    eng.wait_ge(th_r, b * 8 + i + 1)
                    eng.wait_ge(sr_out[i % 2], (b * 4 + i // 2 + 1) * 16)
                    eng.scalar_tensor_tensor(out=srp[i % 2][:, :], in0=th[i % 2][:, :], scalar=1.0,
                                             in1=ring[q % RING][:, :], op0=ALU.add, op1=ALU.mult).then_inc(sr_ready, 1)
                    q += 1

                def silu(i):
                    m, h = pieces[i]
                    eng.wait_ge(th_x, b * 8 + i + 1)
                    eng.scalar_tensor_tensor(out=u2[:, m, h * HALF:(h + 1) * HALF], in0=th2[i % 2][:, :], scalar=1.0,
                                             in1=xsp[i % 2][:, :], op0=ALU.add, op1=ALU.mult).then_inc(u_ready, 1)
                    eng.wait_ge(u_ready, b * 8 + i + 1 + 2)
                    eng.wait_ge(ud_out[i % 2], (b * 4 + i // 2 + 1) * 16)
                    eng.tensor_scalar(udp[i % 2][:, :], u2[:, m, h * HALF:(h + 1) * HALF], t.D[:, m:m + 1], 0.5,
                                      ALU.mult, ALU.mult).then_inc(ud_ready, 1)

                for i, (m, h) in enumerate(pieces):
                    eng.wait_ge(bank_full, b * JOBS + q + 1)
                    eng.wait_ge(xs_out[i % 2], (b * 4 + i // 2 + 1) * 16)
                    eng.wait_ge(u_ready, b * 8 + i + 1)
                    eng.tensor_scalar(xsp[i % 2][:, :], ring[q % RING][:, :], t.conv_b[:, m:m + 1], None,
                                      ALU.add).then_inc(xs_ready, 1)
                    if i >= 1:
                        silu(i - 1)
                    q += 1
                silu(7)
                q = JOBS - 8
                for quad in range(0, 8, 4):
                    for i in range(quad, quad + 4):
                        m = pieces[i][0]
                        eng.wait_ge(abs_ready, b * 8 + i + 1)
                        eng.wait_ge(du_out[i % 4], (b * 2 + i // 4 + 1) * 16)
                        eng.tensor_scalar(dup[i % 4][:, :], ring[q % RING][:, :], t.b_dt[:, m:m + 1], 0.0,
                                          ALU.add, ALU.max).then_inc(z_ready, 1)
                        q += 1
                    for i in range(quad, quad + 4):
                        m, h = pieces[i]
                        at = b * 24 + i * 3
                        e, dl, z = ez[i % 4], dlp[i % 4], dup[i % 4]
                        eng.wait_ge(exp_ready, b * 8 + i + 1)
                        eng.tensor_scalar(w1m, e[:, :], 1.0, -1.0, ALU.add, ALU.add).then_inc(sp_step, 1)
                        eng.wait_ge(ln_ready, b * 8 + i + 1)
                        eng.wait_ge(sp_step, at + 1)
                        eng.tensor_tensor(e[:, :], e[:, :], w1m, ALU.subtract).then_inc(sp_step, 1)
                        eng.wait_ge(sp_step, at + 2)
                        eng.tensor_tensor(e[:, :], e[:, :], dl[:, :], ALU.add).then_inc(sp_step, 1)
                        eng.wait_ge(sp_step, at + 3)
                        eng.wait_ge(z_ready, b * 8 + i + 1 + 8)
                        eng.tensor_tensor(dl[:, :], e[:, :], z[:, :], ALU.add).then_inc(delta_ready, 1)
                        eng.wait_ge(delta_ready, b * 8 + i + 1 + 4)
                        eng.scalar_tensor_tensor(out=z[:, :], in0=dl[:, :], scalar=0.5,
                                                 in1=u2[:, m, h * HALF:(h + 1) * HALF], op0=ALU.mult,
                                                 op1=ALU.mult).then_inc(du_ready, 1)

        @block.sync
        def _(eng):
            with eng.Fori(0, BATCH) as b:
                for i, (m, h) in enumerate(pieces):
                    eng.wait_ge(sr_ready, b * 8 + i + 3)
                    eng.dma_start(row("sr", b, m, h), srp[i % 2][:, :]).then_inc(sr_out[i % 2], 16)
                for i, (m, h) in enumerate(pieces):
                    eng.wait_ge(xs_ready, b * 8 + i + 1)
                    eng.dma_start(row("xs", b, m, h), xsp[i % 2][:, :]).then_inc(xs_out[i % 2], 16)
                    if i >= 1:
                        eng.wait_ge(ud_ready, b * 8 + i)
                        eng.dma_start(row("ud", b, *pieces[i - 1]), udp[(i - 1) % 2][:, :]).then_inc(ud_out[(i - 1) % 2], 16)
                eng.wait_ge(ud_ready, b * 8 + 8)
                eng.dma_start(row("ud", b, *pieces[7]), udp[1][:, :]).then_inc(ud_out[1], 16)
                eng.wait_ge(act_freed, b * XC_X + XC_X)
                for s in range(2):
                    eng.dma_start(d["bc"][ds(b * NST, NST), s, :], bcT[s * NST:(s + 1) * NST, :]).then_inc(bc_out, 16)
                for i, (m, h) in enumerate(pieces):
                    eng.wait_ge(delta_ready, b * 8 + i + 1 + 4)
                    eng.dma_start(row("delta", b, m, h), dlp[i % 4][:, :]).then_inc(delta_out[i % 4], 16)
                    eng.wait_ge(du_ready, b * 8 + i + 5)
                    eng.dma_start(row("du", b, m, h), dup[i % 4][:, :]).then_inc(du_out[i % 4], 16)
            eng.dma_start(d["bc"][BATCH * NST:BATCH * NST + 2, 0, :], bcT[0:2, :]).then_inc(bc_out, 16)
            eng.dma_start(d["bc"][BATCH * NST:BATCH * NST + 2, 1, :], bcT[2:4, :]).then_inc(bc_out, 16)
            for out in (sr_out, xs_out, ud_out, delta_out, du_out):
                for o in out:
                    eng.wait_ge(o, BATCH * 8 * 16 // len(out) + 16)
            eng.wait_ge(bc_out, BATCH * 32 + 64)

        @block.gpsimd
        def _(eng):
            eng.wait_ge(slots_ready, 1)
            eng.wait_ge(t.ids_zeroed, 16)
            n = 0
            for k in range(TOP):
                for i in range(TT):
                    eng.indirect_dma_start(out=d["ids"], out_offset=bass.IndirectOffsetOnAxis(ap=t.place[:, k, i:i + 1], axis=0),
                                           in_=t.tok_id[:, i:i + 1], in_offset=None).then_inc(t.ids_written, 16)
                    n += 16
            eng.wait_ge(t.ids_written, n)
            eng.dma_start(t.ids[:, :], d["ids"].rearrange("(p w) o -> p (w o)", p=P)).then_inc(t.ids_loaded, 16)
            eng.wait_ge(t.ids_loaded, 16)


def experts_and_scan(nc, t, d):
    HR = 4
    LAG = 2
    STEPS = [2, 1, 2, 1, 1, 2, 1, 2, 1, 1, 2, 1, 2, 1]
    SPT = sum(STEPS)
    with ExitStack() as ctx:
        sb = lambda n, s, dt=F32: ctx.enter_context(nc.sbuf_tensor(n, s, dt))
        sem = lambda n: ctx.enter_context(nc.semaphore(n))
        ps = lambda n: ctx.enter_context(nc.psum_tensor(n, [P, HALF], F32))
        w1 = [sb(f"w1_{c}", [P, DC, 2 * P]) for c in range(NWC)]
        w3 = [sb(f"w3_{c}", [P, DC, 2 * P]) for c in range(NWC)]
        w2 = [sb(f"w2_{c}", [P, 2, DM]) for c in range(NWC)]
        delta = sb("delta_b", [P, CC, SEQ])
        du = sb("du_b", [P, CC, SEQ])
        y = sb("y_b", [P, CC, SEQ])
        dA = sb("dA", [P, CC, SEQ])
        hs = sb("h_states", [P, CC, SEQ])
        bc = [sb(f"bc{i}", [P, 2, SEQ]) for i in range(2)]
        xg = sb("xg", [P, SH, DM])
        xT = sb("xT", [P, DC, SLOTS])
        hT = [sb(f"hT{i}", [P, SLOTS]) for i in range(HR)]
        th = [sb(f"th_h{i}", [P, SLOTS]) for i in range(2)]
        gl = [sb(f"gl{i}", [P, SLOTS]) for i in range(2)]
        og = sb("og", [P, SH, DM])
        idc = sb("ids_now", [P, SH], U32)
        ph = [ps(f"ph{i}") for i in range(HR)]
        po = [ps(f"po{i}") for i in range(SH)]
        px = [ps(f"px{i}") for i in range(2)]
        w_in = [sem(f"w_chunk{c}") for c in range(NWC)]
        xg_in = sem("xg_in")
        xg_turned = sem("xg_turned")
        xT_ready = sem("xT_ready")
        up_done = sem("up_done")
        tanh_done = sem("tanh_done")
        gate_step = sem("gate_step")
        hid_done = sem("hid_done")
        down_done = sem("down_done")
        out_done = sem("out_done")
        out_copied = sem("out_copied")
        ys_out = sem("ys_out")
        ids_now = sem("ids_now_ready")
        row_in = sem("row_in")
        sr_in = sem("sr_in")
        bc_in = [sem(f"bc_in{i}") for i in range(2)]
        dA_ready = sem("dA_ready")
        scan_step = sem("scan_step")
        y_final = sem("y_final")
        y_out = sem("y_out")
        act_sync = sem("act_sync")
        pool_sync = sem("pool_sync")
        block = ctx.enter_context(nc.Block())

        def before(f, ring):
            if f >= ring:
                return f - ring + NF
            return max(g for g in range(NF) if g % ring == f % ring)

        UNIT = [("p", 0), ("p", 2), ("s", 0), ("s", 1), ("s", 2), ("s", 3), ("q", 0), ("q", 2), ("r", 0), ("r", 2)]
        assert 2 * len(UNIT) == SPT

        @block.sync
        def _(eng):
            def chunk(e, c):
                eng.dma_start(w1[c][:, :, :], d["w1"][ds(e, 1), :, c * 2 * P:(c + 1) * 2 * P].rearrange(
                    "o (k p) f -> (o p) k f", p=P)).then_inc(w_in[c], 16)
                eng.dma_start(w3[c][:, :, :], d["w3"][ds(e, 1), :, c * 2 * P:(c + 1) * 2 * P].rearrange(
                    "o (k p) f -> (o p) k f", p=P)).then_inc(w_in[c], 16)
                eng.dma_start(w2[c][:, :, :], d["w2"][ds(e, 1), c * 2 * P:(c + 1) * 2 * P, :].rearrange(
                    "o (s p) n -> (o p) s n", p=P)).then_inc(w_in[c], 16)

            def weights(tile, chunks):
                for c in chunks:
                    again = eng.value_load(t.meta[0:1, 1, ds(tile + 1, 1)], min_val=0, max_val=1)
                    with eng.If(again > 0):
                        e = eng.value_load(t.meta[0:1, 0, ds(tile + 1, 1)], min_val=0, max_val=E - 1)
                        eng.wait_ge(down_done, tile * NF + NF + 2 * c + 2)
                        chunk(e, c)
                    with eng.Else():
                        eng.wait_ge(down_done, tile * NF + NF + 2 * c + 2)
                        eng.sem_inc(w_in[c], 48)

            e0 = eng.value_load(t.meta[0:1, 0, 0:1], min_val=0, max_val=E - 1)
            for c in range(NWC):
                chunk(e0, c)
            for i in range(2):
                eng.dma_start(bc[i][:, :, :].rearrange("p s n -> p (s n)"),
                              bcast(d["bc"][i:i + 1, :, :].rearrange("o s n -> o (s n)"), [P, 2 * SEQ])).then_inc(bc_in[i], 16)
            with eng.Fori(0, BATCH) as b:
                with eng.Fori(0, NST // 2) as j:
                    tile = b * GROUP + j
                    m = b * NST + j * 2
                    weights(tile, range(0, 3))
                    for i, part in ((0, range(3, 6)), (1, range(6, 7))):
                        eng.wait_ge(scan_step, (b * (NST // 2) + j) * SPT + i * len(UNIT) + 8 + 1)
                        eng.dma_start(bc[i][:, :, :].rearrange("p s n -> p (s n)"),
                                      bcast(d["bc"][ds(m + 2 + i, 1), :, :].rearrange("o s n -> o (s n)"),
                                            [P, 2 * SEQ])).then_inc(bc_in[i], 16)
                        weights(tile, part)
                weights(b * GROUP + GROUP - 1, range(NWC))
            with eng.Fori(0, PLAIN - 1) as j:
                weights(BATCH * GROUP + j, range(NWC))
            eng.wait_ge(bc_in[0], 16 * (BATCH * NST // 2 + 1))
            eng.wait_ge(bc_in[1], 16 * (BATCH * NST // 2 + 1))

        @block.gpsimd
        def _(eng):
            def gather(tile):
                eng.tensor_copy(idc[:, :], t.ids[:, ds(tile * SH, SH)]).then_inc(ids_now, 1)
                eng.wait_ge(ids_now, tile + 1)
                eng.sem_inc(pool_sync, 1)
                for s in range(SH):
                    eng.indirect_dma_start(out=xg[:, s, :], out_offset=None, in_=d["xn"],
                                           in_offset=bass.IndirectOffsetOnAxis(ap=idc[:, s:s + 1], axis=0)).then_inc(xg_in, 16)

            def next_gather(tile):
                eng.wait_ge(xg_turned, tile + 1)
                eng.sem_inc(pool_sync, 1)
                eng.wait_ge(xg_in, tile * 32 + 32)
                eng.sem_inc(pool_sync, 1)
                gather(tile + 1)

            gather(0)
            with eng.Fori(0, BATCH) as b:
                for buf, name in ((delta, "delta"), (du, "du"), (y, "ud")):
                    eng.dma_start(buf[:, :, :], d[name][ds(b, 1), :, :, :].rearrange("o p c n -> (o p) c n")).then_inc(row_in, 16)
                with eng.Fori(0, GROUP) as j:
                    next_gather(b * GROUP + j)
                eng.wait_ge(scan_step, (b + 1) * (NST // 2) * SPT + 1)
                eng.sem_inc(pool_sync, 1)
                eng.dma_start(dA[:, :, :], d["sr"][ds(b, 1), :, :, :].rearrange("o p c n -> (o p) c n")).then_inc(sr_in, 16)
                eng.wait_ge(y_final, b * 2 + 4)
                eng.sem_inc(pool_sync, 1)
                eng.dma_start(d["yg"][ds(b, 1), :, :, :].rearrange("o p c n -> (o p) c n"), y[:, :, :]).then_inc(y_out, 16)
                eng.wait_ge(y_out, b * 16 + 16)
                eng.sem_inc(pool_sync, 1)
            with eng.Fori(0, PLAIN) as j:
                next_gather(BATCH * GROUP + j)
            eng.wait_ge(y_out, BATCH * 16)
            eng.wait_ge(xg_in, (NT + 1) * 32)

        @block.tensor
        def _(eng):
            eng.sem_inc(down_done, NF)

            def turn(tile):
                eng.wait_ge(xg_in, tile * 32 + 32)
                for c in range(DC):
                    for s in range(SH):
                        last = eng.transpose(px[c // 2][:, (c % 2) * SLOTS + s * P:(c % 2) * SLOTS + (s + 1) * P],
                                             xg[:, s, c * P:(c + 1) * P], t.ident[:, :])
                last.then_inc(xg_turned, 1)

            def up_waits(tile, f):
                c = f // 2
                if f == 0:
                    eng.wait_ge(xT_ready, tile * 2 + 2)
                if f % 2 == 0:
                    eng.wait_ge(w_in[c], tile * 48 + 48)
                eng.wait_ge(hid_done, tile * NF + before(f, HR) + 1)

            def up(tile, f):
                c, o = f // 2, (f % 2) * P
                up_waits(tile, f)
                for n, w in enumerate((w1, w3)):
                    for k in range(DC):
                        last = eng.matmul(ph[f % HR][:, n * SLOTS:(n + 1) * SLOTS], w[c][:, k, o:o + P], xT[:, k, :],
                                          start=(n == 0 and k == 0), stop=(k == DC - 1), skip_group_check=True)
                last.then_inc(up_done, 1)

            def down_waits(tile, f):
                eng.wait_ge(hid_done, tile * NF + NF + f + 1)
                if f == 0:
                    eng.wait_ge(out_copied, tile * SH + SH)

            def down(tile, f):
                down_waits(tile, f)
                for s in range(SH):
                    last = eng.matmul(po[s][:, :], hT[f % HR][:, s * P:(s + 1) * P], w2[f // 2][:, f % 2, :],
                                      start=(f == 0), stop=(f == NF - 1))
                last.then_inc(down_done, 1)

            def tile_work(tile):
                live = eng.value_load(t.meta[0:1, 2, ds(tile, 1)], min_val=0, max_val=1)
                with eng.If(live > 0):
                    for f in range(NF + LAG):
                        if f < NF:
                            up(tile, f)
                        if f == 10:
                            turn(tile + 1)
                        if f >= LAG:
                            down(tile, f - LAG)
                with eng.Else():
                    eng.drain()
                    for f in range(NF + LAG):
                        if f < NF:
                            up_waits(tile, f)
                            eng.sem_inc(up_done, 1)
                        if f == 10:
                            eng.wait_ge(xg_in, tile * 32 + 64)
                            eng.sem_inc(xg_turned, 1)
                        if f >= LAG:
                            down_waits(tile, f - LAG)
                            eng.sem_inc(down_done, 1)

            turn(0)
            with eng.Fori(0, BATCH) as b:
                with eng.Fori(0, GROUP) as j:
                    tile_work(b * GROUP + j)
            with eng.Fori(0, PLAIN) as j:
                tile_work(BATCH * GROUP + j)

        @block.scalar
        def _(eng):
            def turned(tile, after):
                eng.wait_ge(xg_turned, tile + 1)
                if after:
                    eng.wait_ge(up_done, tile * NF)
                for i in range(2):
                    eng.activation(xT[:, 2 * i:2 * i + 2, :].rearrange("p c n -> p (c n)"), px[i][:, :],
                                   ACT.Copy).then_inc(xT_ready, 1)

            def tanh(tile, f):
                eng.wait_ge(up_done, tile * NF + f + 1)
                eng.wait_ge(gate_step, tile * NF + f + 1)
                eng.activation(th[f % 2][:, :], ph[f % HR][:, 0:SLOTS], ACT.Tanh, scale=0.5).then_inc(tanh_done, 1)

            def decay(b, j, i, c):
                n = j * 2 + i
                m = b * NST + n
                if i == 0:
                    eng.wait_ge(scan_step, (b * (NST // 2) + j) * SPT + 1)
                    if c == 0:
                        eng.sem_inc(act_sync, 1)
                        eng.wait_ge(row_in, b * 48 + 48)
                        eng.sem_inc(act_sync, 1)
                        eng.wait_ge(y_final, b * 2 + 2)
                else:
                    eng.wait_ge(scan_step, (b * (NST // 2) + j) * SPT + 3 + c + 1)
                eng.sem_inc(act_sync, 1)
                eng.activation(dA[:, c, :], delta[:, c, :], ACT.Exp, scale=t.A[:, c, ds(n, 1)]).then_inc(dA_ready, 1)

            def outputs(tile):
                eng.wait_ge(down_done, tile * NF + 2 * NF)
                eng.wait_ge(ys_out, tile * 16 + 16)
                for s in range(SH):
                    eng.activation(og[:, s, :], po[s][:, :], ACT.Copy).then_inc(out_copied, 1)
                eng.wait_ge(out_copied, tile * SH + 2 * SH)
                eng.dma_start(d["ys"][ds(tile, 1), :, :].rearrange("o (s p) n -> (o p) s n", p=P), og[:, :, :]).then_inc(ys_out, 16)

            WHEN = {0: [(0, 0), (0, 1)], 1: [(0, 2), (0, 3)], 4: [(1, 0)], 5: [(1, 1)], 6: [(1, 2)], 7: [(1, 3)]}

            def tile_work(tile, b=None, j=None):
                for f in range(NF):
                    tanh(tile, f)
                    if b is not None:
                        for i, c in WHEN.get(f, []):
                            decay(b, j, i, c)
                turned(tile + 1, True)
                outputs(tile)

            turned(0, False)
            with eng.Fori(0, BATCH) as b:
                with eng.Fori(0, NST // 2) as j:
                    tile_work(b * GROUP + j, b, j)
                tile_work(b * GROUP + GROUP - 1)
            with eng.Fori(0, PLAIN) as j:
                tile_work(BATCH * GROUP + j)
            eng.wait_ge(ys_out, NT * 16 + 16)

        @block.vector
        def _(eng):
            eng.sem_inc(hid_done, NF)
            eng.sem_inc(scan_step, 1)
            eng.sem_inc(out_copied, SH)
            eng.sem_inc(ys_out, 16)
            eng.sem_inc(y_final, 2)
            eng.sem_inc(gate_step, 2)

            def hidden(tile, f):
                eng.wait_ge(tanh_done, tile * NF + f + 1)
                eng.scalar_tensor_tensor(out=gl[f % 2][:, :], in0=th[f % 2][:, :], scalar=1.0,
                                         in1=ph[f % HR][:, 0:SLOTS], op0=ALU.add, op1=ALU.mult).then_inc(gate_step, 1)
                eng.wait_ge(down_done, tile * NF + before(f, HR) + 1)
                eng.wait_ge(gate_step, tile * NF + f + 3)
                eng.scalar_tensor_tensor(out=hT[f % HR][:, :], in0=gl[f % 2][:, :], scalar=0.5,
                                         in1=ph[f % HR][:, SLOTS:2 * SLOTS], op0=ALU.mult, op1=ALU.mult).then_inc(hid_done, 1)

            def scan(b, j, k):
                i, u = k // len(UNIT), k % len(UNIT)
                kind, c = UNIT[u]
                at = (b * (NST // 2) + j) * SPT + i * len(UNIT) + 1
                two = lambda buf: buf[:, c:c + 2, :]
                if kind == "p":
                    if c == 0:
                        eng.wait_ge(bc_in[i], (b * (NST // 2) + j + 1) * 16)
                        if i == 0:
                            eng.wait_ge(row_in, b * 48 + 48)
                    eng.wait_ge(scan_step, at - 1 if (i == 1 and c == 0) else at)
                    ins = eng.tensor_tensor(two(hs), two(du), bcast(bc[i][:, 0:1, :], [P, 2, SEQ]), ALU.mult)
                elif kind == "s":
                    eng.wait_ge(scan_step, at + (1 if c < 2 else 2))
                    eng.wait_ge(dA_ready, (b * NST + j * 2 + i) * CC + c + 1)
                    ins = eng.tensor_tensor_scan(hs[:, c, :], dA[:, c, :], hs[:, c, :], 0.0, ALU.mult, ALU.add)
                elif kind == "q":
                    eng.wait_ge(scan_step, at + 4 + c)
                    ins = eng.tensor_tensor(two(hs), two(hs), bcast(bc[i][:, 1:2, :], [P, 2, SEQ]), ALU.mult)
                else:
                    eng.wait_ge(scan_step, at + (7 if c == 0 else 8))
                    ins = eng.tensor_tensor(two(y), two(y), two(hs), ALU.add)
                ins.then_inc(scan_step, 1)

            def tile_work(tile, b=None, j=None, final=False):
                k = 0
                for f in range(NF):
                    hidden(tile, f)
                    if j is not None:
                        for _ in range(STEPS[f]):
                            scan(b, j, k)
                            k += 1
                    if final and f in (11, 12):
                        c = 2 * (f - 11)
                        eng.wait_ge(sr_in, b * 16 + 16)
                        eng.scalar_tensor_tensor(out=y[:, c:c + 2, :].rearrange("p c n -> p (c n)"),
                                                 in0=y[:, c:c + 2, :].rearrange("p c n -> p (c n)"), scalar=0.5,
                                                 in1=dA[:, c:c + 2, :].rearrange("p c n -> p (c n)"),
                                                 op0=ALU.mult, op1=ALU.mult).then_inc(y_final, 1)

            with eng.Fori(0, BATCH) as b:
                with eng.Fori(0, NST // 2) as j:
                    tile_work(b * GROUP + j, b, j)
                tile_work(b * GROUP + GROUP - 1, b, final=True)
            with eng.Fori(0, PLAIN) as j:
                tile_work(BATCH * GROUP + j)


def mamba_out_and_combine(nc, t, d):
    with ExitStack() as ctx:
        sb = lambda n, s, dt=F32: ctx.enter_context(nc.sbuf_tensor(n, s, dt))
        sem = lambda n: ctx.enter_context(nc.semaphore(n))
        NB = 4
        wo = sb("W_out", [P, CC, DM])
        yg = [sb(f"yg{i}", [P, CC, P]) for i in range(NB)]
        xs = [sb(f"xs{i}", [P, CC, P]) for i in range(NB)]
        xr = [sb(f"xr{i}", [P, DM]) for i in range(NB)]
        e1 = [sb(f"e1_{i}", [P, DM]) for i in range(NB)]
        e2 = [sb(f"e2_{i}", [P, DM]) for i in range(NB)]
        acc = [sb(f"acc{i}", [P, DM]) for i in range(NB)]
        sl = [sb(f"slot_now{i}", [P, TOP], U32) for i in range(NB)]
        wg = [sb(f"weight_now{i}", [P, TOP]) for i in range(NB)]
        pz = [ctx.enter_context(nc.psum_tensor(f"pz{i}", [P, DM], F32)) for i in range(NB)]
        wo_in = sem("wo_in")
        mm_in = [sem(f"mm_in{i}") for i in range(NB)]
        e_in = [sem(f"e_in{i}") for i in range(NB)]
        out_st = [sem(f"out_stored{i}") for i in range(NB)]
        proj = sem("proj")
        summed = sem("summed")
        sum_step = sem("sum_step")
        now = sem("slots_now")
        pool_sync = sem("pool_sync4")
        block = ctx.enter_context(nc.Block())
        ROUNDS = TT // NB

        @block.sync
        def _(eng):
            eng.dma_start(wo[:, :, :], d["W_out"].rearrange("(c p) n -> p c n", p=P)).then_inc(wo_in, 16)
            with eng.Fori(0, BATCH) as b:
                for k in range(TPB):
                    i = k % NB
                    tile = b * TPB + k
                    eng.wait_ge(summed, tile + 1)
                    for buf, name in ((yg, "yg"), (xs, "xs")):
                        eng.dma_start(buf[i][:, :, :], d[name][ds(b, 1), :, :, k * P:(k + 1) * P].rearrange(
                            "o p c n -> (o p) c n")).then_inc(mm_in[i], 16)
                    eng.dma_start(xr[i][:, :], d["x"][ds(tile * P, P), :]).then_inc(mm_in[i], 16)

        @block.gpsimd
        def _(eng):
            with eng.Fori(0, ROUNDS) as r:
                for i in range(NB):
                    tile = r * NB + i
                    eng.wait_ge(summed, tile + 1)
                    eng.sem_inc(pool_sync, 1)
                    eng.tensor_copy(sl[i][:, :], t.slot[:, :, ds(tile, 1)].rearrange("p k o -> p (k o)")).then_inc(now, 1)
                    eng.tensor_copy(wg[i][:, :], t.wgt[:, :, ds(tile, 1)].rearrange("p k o -> p (k o)")).then_inc(now, 1)
                    eng.wait_ge(now, tile * 2 + 2)
                    eng.sem_inc(pool_sync, 1)
                    for k, buf in enumerate((e1, e2)):
                        eng.indirect_dma_start(out=buf[i][:, :], out_offset=None, in_=d["ys"].rearrange("t s n -> (t s) n"),
                                               in_offset=bass.IndirectOffsetOnAxis(ap=sl[i][:, k:k + 1], axis=0)).then_inc(e_in[i], 16)

        @block.tensor
        def _(eng):
            eng.sem_inc(summed, NB)
            for i in range(NB):
                eng.sem_inc(out_st[i], 16)
            eng.wait_ge(wo_in, 16)
            with eng.Fori(0, ROUNDS) as r:
                for i in range(NB):
                    eng.wait_ge(mm_in[i], r * 48 + 48)
                    eng.wait_ge(summed, r * NB + i + 1)
                    for c in range(CC):
                        eng.matmul(pz[i][:, :], yg[i][:, c, :], wo[:, c, :], start=(c == 0), stop=False, skip_group_check=True)
                    for c in range(CC):
                        last = eng.matmul(pz[i][:, c * P:(c + 1) * P], xs[i][:, c, :], t.ident[:, :], start=False,
                                          stop=(c == CC - 1), skip_group_check=True)
                    last.then_inc(proj, 1)

        @block.vector
        def _(eng):
            with eng.Fori(0, ROUNDS) as r:
                for i in range(NB):
                    tile = r * NB + i
                    eng.wait_ge(proj, tile + 1)
                    eng.wait_ge(mm_in[i], r * 48 + 48)
                    eng.wait_ge(out_st[i], r * 16 + 16)
                    eng.tensor_tensor(acc[i][:, :], xr[i][:, :], pz[i][:, :], ALU.add).then_inc(sum_step, 1)
                    eng.wait_ge(e_in[i], r * 32 + 32)
                    eng.wait_ge(now, tile * 2 + 2)
                    eng.wait_ge(sum_step, tile * 2 + 1)
                    eng.scalar_tensor_tensor(out=acc[i][:, :], in0=e1[i][:, :], scalar=wg[i][:, 0:1], in1=acc[i][:, :],
                                             op0=ALU.mult, op1=ALU.add).then_inc(sum_step, 1)
                    eng.wait_ge(sum_step, tile * 2 + 2)
                    eng.scalar_tensor_tensor(out=acc[i][:, :], in0=e2[i][:, :], scalar=wg[i][:, 1:2], in1=acc[i][:, :],
                                             op0=ALU.mult, op1=ALU.add).then_inc(summed, 1)

        @block.scalar
        def _(eng):
            with eng.Fori(0, ROUNDS) as r:
                for i in range(NB):
                    tile = r * NB + i
                    eng.wait_ge(summed, tile + 1 + NB)
                    eng.dma_start(d["out"][ds(tile * P, P), :], acc[i][:, :]).then_inc(out_st[i], 16)
            for i in range(NB):
                eng.wait_ge(out_st[i], ROUNDS * 16 + 16)


class Shared:
    pass


def build(nc, d):
    d["xn"] = dram(nc, "xn_d", [TOKENS, DM])
    for name in ("sr", "xs", "ud", "delta", "du", "yg"):
        d[name] = dram(nc, f"{name}_d", [BATCH, P, CC, SEQ])
    d["bc"] = dram(nc, "bc_d", [BATCH * NST + 2, 2, SEQ])
    d["ids"] = dram(nc, "ids_d", [P * IDW, 1], U32)
    d["ys"] = dram(nc, "ys_d", [NT, SLOTS, DM])
    with ExitStack() as ctx:
        sem = lambda n: ctx.enter_context(nc.semaphore(n))
        sb = lambda n, s, dt=F32: ctx.enter_context(nc.sbuf_tensor(n, s, dt))
        t = Shared()
        t.ident = sb("ident", [P, P])
        t.ones = sb("ones", [P, P])
        t.A = sb("A", [P, CC, NST])
        t.ids = sb("ids", [P, IDW], U32)
        t.slot = sb("slot", [P, TOP, TT], U32)
        t.wgt = sb("wgt", [P, TOP, TT])
        t.meta = sb("meta", [P, 3, NT], I32)
        t.gate_in = sem("gate_in")
        t.small_in = sem("small_in")
        t.w_in = sem("w_in")
        t.const_ready = sem("const_ready")
        t.ids_zeroed = sem("ids_zeroed")
        t.ids_written = sem("ids_written")
        t.ids_loaded = sem("ids_loaded")
        t.logits_ready = sem("logits_ready")
        t.a_step = sem("a_step")
        with ExitStack() as front:
            fsb = lambda n, s, dt=F32: front.enter_context(nc.sbuf_tensor(n, s, dt))
            t.xnT = fsb("xnT", [P, DC, TOKENS])
            t.W_in = fsb("W_in", [P, DC, 2 * DIN])
            t.conv_w = fsb("conv_w", [P, KC, CC, DIN])
            t.W_x = fsb("W_x", [P, CC, NX])
            t.W_dt = fsb("W_dt", [P, DIN])
            t.gate = fsb("gate", [P, DC, E])
            t.conv_b = fsb("conv_b", [P, CC])
            t.b_dt = fsb("b_dt", [P, CC])
            t.D = fsb("D", [P, CC])
            t.A_log = fsb("A_log", [P, CC, NST])
            t.xcT = fsb("xcT", [P, CC, SEQ + KC - 1])
            t.tri = fsb("tri", [P, P])
            t.tok_id = fsb("tok_id", [P, TT], U32)
            t.num_i = fsb("num_i", [P, NT], I32)
            t.num = fsb("num", [P, NT])
            t.zero_ids = fsb("zero_ids", [P, IDW], U32)
            t.prob = fsb("prob", [P, TT, E])
            t.red = fsb("red", [P, TT])
            t.red2 = fsb("red2", [P, TT])
            t.top = fsb("top", [P, TT, 8])
            t.topi = fsb("topi", [P, TT, 8], U32)
            t.topf = fsb("topf", [P, TOP, TT])
            t.hot = fsb("hot", [P, TOP, TT, E])
            t.mask = fsb("mask", [P, TT, E])
            t.tot = fsb("tot", [P, E, TT])
            t.cum = fsb("cum", [P, E, TT])
            t.cnt_i = fsb("cnt_i", [P, E], I32)
            t.ntile = fsb("ntile", [P, E])
            t.last_tile = fsb("last_tile", [P, E])
            t.base = fsb("base", [P, E])
            t.place = fsb("place", [P, TOP, TT], U32)
            t.place2 = fsb("place2", [P, TOP, TT], U32)
            t.cmp = fsb("cmp", [P, NT, E - 1])
            t.texp = fsb("texp", [P, NT])
            t.ps_lg = front.enter_context(nc.psum_tensor("ps_lg", [P, HALF], F32))
            norm_and_route_logits(nc, t, d)
            mamba_front(nc, t, d)
        experts_and_scan(nc, t, d)
        mamba_out_and_combine(nc, t, d)


def kernel(**inputs):
    import numpy as np
    import concourse.bacc as bacc
    from concourse.bass_utils import run_bass_kernel_spmd

    lay = {
        "x": inputs["L0_attn_x"].reshape(TOKENS, DM),
        "W_in": inputs["L0_attn_W_in"],
        "conv_w": np.transpose(np.asarray(inputs["L0_attn_conv_w"]), (2, 1, 0)),
        "conv_b": np.asarray(inputs["L0_attn_conv_b"]).reshape(CC, P).T,
        "W_x": inputs["L0_attn_W_x"],
        "W_dt": inputs["L0_attn_W_dt"],
        "b_dt": np.asarray(inputs["L0_attn_b_dt"]).reshape(CC, P).T,
        "A_log": inputs["L0_attn_A_log"],
        "D": np.asarray(inputs["L0_attn_D"]).reshape(CC, P).T,
        "W_out": inputs["L0_attn_W_out"],
        "gate_w": inputs["L0_ffn_gate_w"],
        "w1": inputs["L0_ffn_w1"],
        "w2": inputs["L0_ffn_w2"],
        "w3": inputs["L0_ffn_w3"],
    }
    nc = bacc.Bacc("TRN2", target_bir_lowering=False, num_devices=1)
    arrays, d = {}, {}
    for name, a in lay.items():
        a = np.ascontiguousarray(a)
        arrays[f"in_{name}"] = a
        d[name] = nc.dram_tensor(f"in_{name}", a.shape, mybir.dt.from_np(a.dtype), kind="ExternalInput").ap()
    d["out"] = nc.dram_tensor("out_0", (TOKENS, DM), F32, kind="ExternalOutput").ap()
    build(nc, d)
    r = run_bass_kernel_spmd(nc, [arrays], core_ids=[0])
    return r.results[0]["out_0"].reshape(BATCH, SEQ, DM)
```

```python
from contextlib import ExitStack

import concourse.bass as bass
from concourse import mybir

F32 = mybir.dt.float32
I32 = mybir.dt.int32
U32 = mybir.dt.uint32
ACT = mybir.ActivationFunctionType
ALU = mybir.AluOpType
AX = mybir.AxisListType
ds = bass.ds

P = 128
BATCH, SEQ, DM = 4, 1024, 512
TOKENS = BATCH * SEQ
DC = DM // P
DIN, NST, DTR, KC = 512, 16, 128, 4
CC = DIN // P
NX = DTR + 2 * NST
HALF = 512
NH = SEQ // HALF
E, TOP = 8, 2
MH = 1792
TT = TOKENS // P
TPB = SEQ // P
SLOTS = 256
SH = SLOTS // P
SHIFT = 8
NT = (TOKENS * TOP - E) // SLOTS + E + 1
IDW = NT * SH
NF = MH // P // 2
HM = NF * P
PAIRS = CC // 2
ROWS = BATCH * PAIRS
GROUP = 9
PLAIN = 2 * NT - ROWS * GROUP
NK = ROWS * GROUP + PLAIN
assert PLAIN > 0 and 2 * (GROUP - 1) == NST
EPS = 1e-5
LOG_MAX = 80.0


def dram(nc, name, shape, dt=F32):
    return nc.dram_tensor(name, shape, dt, kind="Internal").ap()


def bcast(ap, shape):
    return ap.broadcast_to(shape)


def norm_and_route_logits(nc, t, d):
    GT = 4
    NG = TT // GT
    with ExitStack() as ctx:
        sb = lambda n, s, dt=F32: ctx.enter_context(nc.sbuf_tensor(n, s, dt))
        sem = lambda n: ctx.enter_context(nc.semaphore(n))
        xin = [sb(f"xin{i}", [P, GT, DM]) for i in range(2)]
        xno = [sb(f"xno{i}", [P, GT, DM]) for i in range(2)]
        st = sb("ln_stats", [P, GT, 6])
        mv = sb("ln_mean_var", [P, GT, 2])
        ve = sb("ln_var_eps", [P, GT])
        sd = sb("ln_std", [P, GT])
        r0 = sb("ln_rstd0", [P, GT])
        r1 = sb("ln_newton", [P, GT])
        rs = sb("ln_rstd", [P, GT])
        ptr = [ctx.enter_context(nc.psum_tensor(f"ptr{i}", [P, HALF], F32)) for i in range(4)]
        x_in = [sem(f"x_in{i}") for i in range(2)]
        var_ready = sem("var_ready")
        std_ready = sem("std_ready")
        ln_step = sem("ln_step")
        ln_sync = sem("ln_sync")
        xn_ready = sem("xn_ready")
        xn_stored = [sem(f"xn_stored{i}") for i in range(2)]
        tr_ready = sem("tr_ready")
        tr_copied = sem("tr_copied")
        consts = sem("consts1")
        ys_filled = sem("ys_filled")
        zero_row = sb("zero_row", [P, 2 * DM])
        x_v = d["x"].rearrange("(g t p) c -> g p t c", p=P, t=GT)
        xn_v = d["xn"].rearrange("(g t p) c -> g p t c", p=P, t=GT)
        block = ctx.enter_context(nc.Block())

        @block.sync
        def _(eng):
            for i in range(2):
                eng.dma_start(xin[i][:, :, :], x_v[i]).then_inc(x_in[i], 16)
            eng.dma_start(t.gate[:, :, :], d["gate_w"].rearrange("(c p) e -> p c e", p=P)).then_inc(t.gate_in, 16)
            eng.dma_start(t.conv_b[:, :], d["conv_b"]).then_inc(t.small_in, 16)
            eng.dma_start(t.b_dt[:, :], d["b_dt"]).then_inc(t.small_in, 16)
            eng.dma_start(t.D[:, :], d["D"]).then_inc(t.small_in, 16)
            eng.dma_start(t.A_log[:, :, :], d["A_log"].rearrange("(c p) n -> p c n", p=P)).then_inc(t.small_in, 16)
            eng.dma_start(t.W_in[:, :, :], d["W_in"].rearrange("(c p) n -> p c n", p=P)).then_inc(t.w_in, 16)
            with eng.Fori(0, NG // 2 - 1) as g:
                for i in range(2):
                    eng.wait_ge(xn_ready, (g * 2 + i + 1) * GT)
                    eng.dma_start(xin[i][:, :, :], x_v[ds(g * 2 + i + 2, 1)].rearrange("o p t c -> (o p) t c")).then_inc(x_in[i], 16)
            eng.dma_start(t.conv_w[:, :, :, :], d["conv_w"].rearrange("k (c p) o -> p k c o", p=P)).then_inc(t.w_in, 16)
            eng.dma_start(t.W_x[:, :, :], d["W_x"].rearrange("(c p) n -> p c n", p=P)).then_inc(t.w_in, 16)
            eng.dma_start(t.W_dt[:, :], d["W_dt"]).then_inc(t.w_in, 16)

        @block.vector
        def _(eng):
            def group(g, i):
                base = g * (2 * (GT + 6)) + i * (GT + 6)
                eng.wait_ge(x_in[i], g * 16 + 16)
                for k in range(GT):
                    eng.bn_stats(st[:, k, :], xin[i][:, k, :]).then_inc(ln_step, 1)
                eng.wait_ge(ln_step, base + GT)
                eng.sem_inc(ln_sync, 1)
                for k in range(GT):
                    last = eng.bn_aggr(mv[:, k, :], st[:, k, :])
                last.then_inc(ln_step, 1)
                eng.wait_ge(ln_step, base + GT + 1)
                eng.tensor_scalar(ve[:, :], mv[:, :, 1], EPS, None, ALU.add).then_inc(var_ready, 1)
                eng.wait_ge(std_ready, g * 2 + i + 1)
                eng.reciprocal(r0[:, :], sd[:, :]).then_inc(ln_step, 1)
                eng.wait_ge(ln_step, base + GT + 2)
                eng.tensor_tensor(r1[:, :], r0[:, :], r0[:, :], ALU.mult).then_inc(ln_step, 1)
                eng.wait_ge(ln_step, base + GT + 3)
                eng.tensor_tensor(r1[:, :], r1[:, :], ve[:, :], ALU.mult).then_inc(ln_step, 1)
                eng.wait_ge(ln_step, base + GT + 4)
                eng.tensor_scalar(r1[:, :], r1[:, :], -0.5, 1.5, ALU.mult, ALU.add).then_inc(ln_step, 1)
                eng.wait_ge(ln_step, base + GT + 5)
                eng.tensor_tensor(rs[:, :], r1[:, :], r0[:, :], ALU.mult).then_inc(ln_step, 1)
                eng.wait_ge(ln_step, base + GT + 6)
                eng.wait_ge(xn_stored[i], g * 16 + 16)
                eng.wait_ge(tr_ready, (g * 2 + i) * 4 + 4)
                for k in range(GT):
                    last = eng.tensor_scalar(xno[i][:, k, :], xin[i][:, k, :], mv[:, k, 0:1], rs[:, k:k + 1],
                                             ALU.subtract, ALU.mult).then_inc(xn_ready, 1)

            with eng.Fori(0, NG // 2) as g:
                for i in range(2):
                    group(g, i)

        @block.gpsimd
        def _(eng):
            eng.memset(t.ident[:, :], 0.0).then_inc(consts, 1)
            eng.memset(t.tri[:, :], 1.0).then_inc(consts, 1)
            eng.memset(t.ones[:, :], 1.0).then_inc(consts, 1)
            eng.wait_ge(consts, 3)
            eng.affine_select(out=t.ident[:, :], in_=t.ident[:, :], compare_op=ALU.not_equal, fill=1.0,
                              base=0, pattern=[[-1, P]], channel_multiplier=1).then_inc(t.const_ready, 1)
            eng.affine_select(out=t.tri[:, :], in_=t.tri[:, :], compare_op=ALU.is_gt, fill=0.0,
                              base=0, pattern=[[1, P]], channel_multiplier=-1).then_inc(t.const_ready, 1)
            eng.iota(t.tok_id[:, :], pattern=[[P, TT]], base=0, channel_multiplier=1).then_inc(t.const_ready, 1)
            eng.iota(t.num_i[:, :], pattern=[[1, NK + 2]], base=0, channel_multiplier=0).then_inc(t.const_ready, 1)
            eng.memset(t.zero_ids[:, :], 0).then_inc(t.const_ready, 1)
            eng.memset(t.xcT[:, :, 0:KC - 1], 0.0).then_inc(t.const_ready, 1)
            eng.memset(zero_row[:, :], 0.0).then_inc(t.const_ready, 1)
            eng.wait_ge(t.const_ready, 7)
            eng.dma_start(d["ids"].rearrange("(p w) o -> p (w o)", p=P), t.zero_ids[:, :]).then_inc(t.ids_zeroed, 16)
            for tile in range(TOKENS * TOP // SLOTS, NT):
                eng.dma_start(d["ys"][tile:tile + 1, :, :, :].rearrange("o (s p) h n -> (o p) s (h n)", p=P),
                              bcast(zero_row[:, :].unsqueeze(1), [P, SH, 2 * DM])).then_inc(ys_filled, 16)
            eng.wait_ge(ys_filled, (NT - TOKENS * TOP // SLOTS) * 16)

        @block.scalar
        def _(eng):
            def group(g, i):
                eng.wait_ge(var_ready, g * 2 + i + 1)
                eng.activation(sd[:, :], ve[:, :], ACT.Sqrt).then_inc(std_ready, 1)
                eng.wait_ge(xn_ready, (g * 2 + i + 1) * GT)
                eng.dma_start(xn_v[ds(g * 2 + i, 1)].rearrange("o p t c -> (o p) t c"), xno[i][:, :, :]).then_inc(xn_stored[i], 16)
                for c in range(DC):
                    eng.wait_ge(tr_ready, (g * 2 + i) * 4 + c + 1 + 8)
                    eng.activation(t.xnT[:, c, ds((g * 2 + i) * HALF, HALF)], ptr[c][:, :], ACT.Copy).then_inc(tr_copied, 1)
            with eng.Fori(0, NG // 2) as g:
                for i in range(2):
                    group(g, i)
            for i in range(2):
                eng.wait_ge(xn_stored[i], NG * 8 + 16)

        @block.tensor
        def _(eng):
            for i in range(2):
                eng.sem_inc(xn_stored[i], 16)
            eng.sem_inc(tr_ready, 8)
            eng.sem_inc(tr_copied, 4)
            eng.wait_ge(t.const_ready, 6)
            eng.wait_ge(t.gate_in, 16)

            def group(g, i):
                eng.wait_ge(xn_ready, (g * 2 + i + 1) * GT)
                for c in range(DC):
                    eng.wait_ge(tr_copied, (g * 2 + i) * 4 + c + 1)
                    for k in range(GT):
                        last = eng.transpose(ptr[c][:, k * P:(k + 1) * P], xno[i][:, k, c * P:(c + 1) * P], t.ident[:, :])
                    last.then_inc(tr_ready, 1)

            with eng.Fori(0, NG // 2) as g:
                for i in range(2):
                    group(g, i)
            eng.wait_ge(tr_copied, NG * 4 + 4)
            for i in range(TT):
                for c in range(DC):
                    last = eng.matmul(t.ps_lg[:, i * E:(i + 1) * E], t.xnT[:, c, i * P:(i + 1) * P], t.gate[:, c, :],
                                      start=(c == 0), stop=(c == DC - 1), skip_group_check=True)
            last.then_inc(t.logits_ready, 1)


def mamba_front(nc, t, d):
    JOBS = 36
    RING = 6
    XC_X = 12
    with ExitStack() as ctx:
        sb = lambda n, s, dt=F32: ctx.enter_context(nc.sbuf_tensor(n, s, dt))
        sem = lambda n: ctx.enter_context(nc.semaphore(n))
        u2 = sb("u2", [P, CC, SEQ])
        din = sb("din", [P, SEQ])
        bcT = sb("bcT", [2 * NST, SEQ])
        th = [sb(f"th_r{i}", [P, HALF]) for i in range(2)]
        th2 = [sb(f"th_x{i}", [P, HALF]) for i in range(2)]
        srp = [sb(f"sr_piece{i}", [P, HALF]) for i in range(2)]
        xsp = [sb(f"xs_piece{i}", [P, HALF]) for i in range(2)]
        udp = [sb(f"ud_piece{i}", [P, HALF]) for i in range(2)]
        dlp = [sb(f"delta_piece{i}", [P, HALF]) for i in range(4)]
        dup = [sb(f"du_piece{i}", [P, HALF]) for i in range(4)]
        ez = th + th2
        w1m = t.hot[:, :, :, :].rearrange("p k i e -> p (k i e)")
        ring = [ctx.enter_context(nc.psum_tensor(f"front{i}", [P, HALF], F32)) for i in range(RING)]
        ps_rt = ctx.enter_context(nc.psum_tensor("ps_rt", [P, HALF], F32))
        bank_full = sem("bank_full")
        act_freed = sem("act_freed")
        th_r = sem("th_r")
        sr_ready = sem("sr_ready")
        sr_out = [sem(f"sr_out{i}") for i in range(2)]
        xs_ready = sem("xs_ready")
        xs_out = [sem(f"xs_out{i}") for i in range(2)]
        th_x = sem("th_x")
        u_ready = sem("u_ready")
        ud_ready = sem("ud_ready")
        ud_out = [sem(f"ud_out{i}") for i in range(2)]
        bc_out = sem("bc_out")
        abs_ready = sem("abs_ready")
        exp_ready = sem("exp_ready")
        z_ready = sem("z_ready")
        ln_ready = sem("ln_ready")
        sp_step = sem("softplus_step")
        delta_ready = sem("delta_ready")
        delta_out = [sem(f"delta_out{i}") for i in range(4)]
        du_ready = sem("du_ready")
        du_out = [sem(f"du_out{i}") for i in range(4)]
        r_step = sem("route_step")
        r_exp = sem("route_exp")
        r_max = sem("route_max")
        r_mask = sem("route_mask")
        r_count = sem("route_count")
        slots_ready = sem("slots_ready")
        block = ctx.enter_context(nc.Block())

        pieces = [(c, h) for c in range(CC) for h in range(NH)]

        def row(name, b, c, h):
            return d[name][ds(b * PAIRS + c // 2, 1), :, c % 2, h * HALF:(h + 1) * HALF].rearrange("o p n -> (o p) n")

        @block.tensor
        def _(eng):
            eng.wait_ge(r_mask, 1)
            eng.matmul(ps_rt[:, 0:TT * E], t.tri[:, :], t.mask[:, :, :].rearrange("p i e -> p (i e)"), start=True, stop=True)
            eng.matmul(ps_rt[:, TT * E:2 * TT * E], t.ones[:, :], t.mask[:, :, :].rearrange("p i e -> p (i e)"),
                       start=False, stop=True, skip_group_check=True).then_inc(r_count, 1)
            eng.wait_ge(t.w_in, 64)
            with eng.Fori(0, BATCH) as b:
                q = 0
                owner = ([(act_freed, XC_X, n + 1) for n in range(8)]
                         + [(sr_ready, 8, n + 1 + 2) for n in range(8)]
                         + [(xs_ready, 8, n + 1) for n in range(8)]
                         + [(act_freed, XC_X, n + 1) for n in range(8, 12)]
                         + [(z_ready, 8, n + 1 + 8) for n in range(8)])

                def bank():
                    s, per, n = owner[(q - RING) % JOBS]
                    eng.wait_ge(s, b * per + n - (per if q < RING else 0))
                    return ring[q % RING]

                for m in range(2 * CC):
                    for h in range(NH):
                        o = bank()
                        for c in range(DC):
                            last = eng.matmul(o[:, :], t.W_in[:, c, m * P:(m + 1) * P],
                                              t.xnT[:, c, ds(b * SEQ + h * HALF, HALF)], start=(c == 0), stop=(c == DC - 1))
                        last.then_inc(bank_full, 1)
                        q += 1
                for m, h in pieces:
                    o = bank()
                    if m == 0 and h == 0:
                        eng.wait_ge(act_freed, b * XC_X + 8)
                    for k in range(KC):
                        for c in range(CC):
                            last = eng.matmul(o[:, :], t.conv_w[:, k, c, m * P:(m + 1) * P],
                                              t.xcT[:, c, h * HALF + k:h * HALF + k + HALF],
                                              start=(k == 0 and c == 0), stop=(k == KC - 1 and c == CC - 1))
                    last.then_inc(bank_full, 1)
                    q += 1
                for part in range(2):
                    for h in range(NH):
                        o = bank()
                        eng.wait_ge(u_ready, b * 8 + 8 + 2)
                        lo, hi = (0, DTR) if part == 0 else (DTR, NX)
                        for c in range(CC):
                            last = eng.matmul(o[0:hi - lo, :], t.W_x[:, c, lo:hi], u2[:, c, h * HALF:(h + 1) * HALF],
                                              start=(c == 0), stop=(c == CC - 1))
                        last.then_inc(bank_full, 1)
                        q += 1
                for m, h in pieces:
                    o = bank()
                    eng.wait_ge(act_freed, b * XC_X + 10)
                    eng.matmul(o[:, :], t.W_dt[:, m * P:(m + 1) * P], din[:, h * HALF:(h + 1) * HALF],
                               start=True, stop=True).then_inc(bank_full, 1)
                    q += 1

        @block.scalar
        def _(eng):
            eng.wait_ge(t.a_step, 1)
            eng.activation(t.A[:, :].rearrange("p (c n) -> p c n", n=NST), t.A_log[:, :, :], ACT.Exp).then_inc(t.a_step, 1)
            eng.wait_ge(t.a_step, 2)
            eng.activation(t.A[:, :].rearrange("p (c n) -> p c n", n=NST), t.A[:, :].rearrange("p (c n) -> p c n", n=NST), ACT.Copy, scale=-1.0).then_inc(t.a_step, 1)
            eng.wait_ge(r_max, 1)
            eng.activation(t.prob[:, :, :], t.prob[:, :, :], ACT.Exp).then_inc(r_exp, 1)
            with eng.Fori(0, BATCH) as b:
                q = 0
                for m, h in pieces:
                    eng.wait_ge(bank_full, b * JOBS + q + 1)
                    eng.activation(t.xcT[:, m, KC - 1 + h * HALF:KC - 1 + (h + 1) * HALF], ring[q % RING][:, :],
                                   ACT.Copy).then_inc(act_freed, 1)
                    q += 1
                eng.wait_ge(delta_ready, b * 8 + 4)
                for i in range(8):
                    eng.wait_ge(bank_full, b * JOBS + q + 1)
                    eng.wait_ge(sr_ready, b * 8 + i + 1)
                    eng.activation(th[i % 2][:, :], ring[q % RING][:, :], ACT.Tanh, scale=0.5).then_inc(th_r, 1)
                    q += 1
                for i in range(8):
                    eng.wait_ge(xs_ready, b * 8 + i + 1)
                    eng.wait_ge(u_ready, b * 8 + i + 1)
                    eng.activation(th2[i % 2][:, :], xsp[i % 2][:, :], ACT.Tanh, scale=0.5).then_inc(th_x, 1)
                    q += 1
                for h in range(NH):
                    eng.wait_ge(bank_full, b * JOBS + q + 1)
                    eng.activation(din[:, h * HALF:(h + 1) * HALF], ring[q % RING][:, :], ACT.Copy,
                                   scale=0.5).then_inc(act_freed, 1)
                    q += 1
                for h in range(NH):
                    eng.wait_ge(bank_full, b * JOBS + q + 1)
                    eng.wait_ge(bc_out, b * 64 + 64)
                    eng.activation(bcT[:, h * HALF:(h + 1) * HALF], ring[q % RING][0:2 * NST, :], ACT.Copy,
                                   scale=0.5).then_inc(act_freed, 1)
                    q += 1
                for quad in range(0, 8, 4):
                    for i in range(quad, quad + 4):
                        m = pieces[i][0]
                        eng.wait_ge(bank_full, b * JOBS + q + 1)
                        eng.wait_ge(delta_ready, b * 8 + i + 1)
                        eng.activation(ez[i % 4][:, :], ring[q % RING][:, :], ACT.Abs,
                                       bias=t.b_dt[:, m:m + 1]).then_inc(abs_ready, 1)
                        q += 1
                    for i in range(quad, quad + 4):
                        eng.wait_ge(abs_ready, b * 8 + i + 1)
                        eng.activation(ez[i % 4][:, :], ez[i % 4][:, :], ACT.Exp, scale=-1.0).then_inc(exp_ready, 1)
                    for i in range(quad, quad + 4):
                        eng.wait_ge(exp_ready, b * 8 + i + 1)
                        eng.wait_ge(delta_out[i % 4], (b * 2 + i // 4 + 1) * 16)
                        eng.wait_ge(du_ready, b * 8 + i + 1)
                        eng.activation(dlp[i % 4][:, :], ez[i % 4][:, :], ACT.Ln, bias=1.0).then_inc(ln_ready, 1)

        @block.vector
        def _(eng):
            for out in (sr_out, xs_out, ud_out, delta_out, du_out):
                for o in out:
                    eng.sem_inc(o, 16)
            eng.sem_inc(bc_out, 64)
            eng.sem_inc(sr_ready, 2)
            eng.sem_inc(du_ready, 4)
            eng.sem_inc(u_ready, 2)
            eng.sem_inc(z_ready, 8)
            eng.sem_inc(delta_ready, 4)
            eng.wait_ge(t.small_in, 64)
            eng.tensor_scalar(t.A_log[:, :, :], t.A_log[:, :, :], LOG_MAX, None, ALU.min).then_inc(t.a_step, 1)
            step = [0]

            def link(ins):
                step[0] += 1
                ins.then_inc(r_step, 1)
                eng.wait_ge(r_step, step[0])

            link(eng.tensor_copy(t.prob[:, :, :].rearrange("p i e -> p (i e)"), t.ps_lg[:, 0:TT * E]))
            link(eng.tensor_reduce(t.red[:, :], t.prob[:, :, :], AX.X, ALU.max))
            eng.tensor_tensor(t.prob[:, :, :], t.prob[:, :, :], bcast(t.red[:, :].unsqueeze(2), [P, TT, E]),
                              ALU.subtract).then_inc(r_max, 1)
            eng.wait_ge(r_exp, 1)
            link(eng.tensor_reduce(t.red[:, :], t.prob[:, :, :], AX.X, ALU.add))
            link(eng.reciprocal(t.red2[:, :], t.red[:, :]))
            link(eng.tensor_tensor(t.prob[:, :, :], t.prob[:, :, :], bcast(t.red2[:, :].unsqueeze(2), [P, TT, E]), ALU.mult))
            for i in range(TT):
                eng.max(t.top[:, i, :], t.prob[:, i, :]).then_inc(r_step, 1)
            step[0] += TT
            eng.wait_ge(r_step, step[0])
            for i in range(TT):
                eng.max_index(t.topi[:, i, :], t.top[:, i, :], t.prob[:, i, :]).then_inc(r_step, 1)
            step[0] += TT
            eng.wait_ge(r_step, step[0])
            link(eng.tensor_tensor(t.red[:, :], t.top[:, :, 0], t.top[:, :, 1], ALU.add))
            link(eng.reciprocal(t.red2[:, :], t.red[:, :]))
            for k in range(TOP):
                link(eng.tensor_tensor(t.wgt[:, k, :], t.top[:, :, k], t.red2[:, :], ALU.mult))
                link(eng.tensor_copy(t.topf[:, k, :], t.topi[:, :, k]))
            eng.wait_ge(t.const_ready, 6)
            link(eng.tensor_copy(t.num[:, :], t.num_i[:, :]))
            for k in range(TOP):
                link(eng.tensor_tensor(t.hot[:, k, :, :], bcast(t.num[:, 0:E].unsqueeze(1), [P, TT, E]),
                                       bcast(t.topf[:, k, :].unsqueeze(2), [P, TT, E]), ALU.is_equal))
            eng.tensor_tensor(t.mask[:, :, :], t.hot[:, 0, :, :], t.hot[:, 1, :, :], ALU.add).then_inc(r_mask, 1)
            eng.wait_ge(r_count, 1)
            rank = ps_rt[:, 0:TT * E].rearrange("p (i e) -> p i e", e=E)
            total = ps_rt[:, TT * E:2 * TT * E].rearrange("p (i e) -> p e i", e=E)
            link(eng.tensor_copy(t.tot[:, :, :], total))
            for e in range(E):
                link(eng.tensor_tensor_scan(t.cum[:, e, :], t.ones[:, 0:TT], t.tot[:, e, :], 0.0, ALU.mult, ALU.add))
            link(eng.tensor_scalar(t.cnt_i[:, :], t.cum[:, :, TT - 1], float(SLOTS - 1), None, ALU.add))
            link(eng.tensor_scalar(t.cnt_i[:, :], t.cnt_i[:, :], SHIFT, None, ALU.arith_shift_right))
            link(eng.tensor_copy(t.ntile[:, :], t.cnt_i[:, :]))
            link(eng.tensor_tensor_scan(t.last_tile[:, :], t.ones[:, 0:E], t.ntile[:, :], 0.0, ALU.mult, ALU.add))
            link(eng.tensor_tensor(t.base[:, :], t.last_tile[:, :], t.ntile[:, :], ALU.subtract))
            link(eng.tensor_scalar(t.base[:, :], t.base[:, :], float(SLOTS), None, ALU.mult))
            link(eng.tensor_tensor(t.cum[:, :, :], t.cum[:, :, :], t.tot[:, :, :], ALU.subtract))
            link(eng.tensor_tensor(t.cum[:, :, :], t.cum[:, :, :], bcast(t.base[:, :].unsqueeze(2), [P, E, TT]), ALU.add))
            link(eng.tensor_tensor(t.prob[:, :, :], t.cum[:, :, :].rearrange("p e i -> p i e"), rank, ALU.add))
            for k in range(TOP):
                link(eng.tensor_tensor(t.hot[:, k, :, :], t.hot[:, k, :, :], t.prob[:, :, :], ALU.mult))
                link(eng.tensor_reduce(t.topf[:, k, :], t.hot[:, k, :, :], AX.X, ALU.add))
            link(eng.tensor_copy(t.slot[:, :, :], t.topf[:, :, :]))
            link(eng.tensor_scalar(t.place[:, :, :], t.slot[:, :, :], P - 1, None, ALU.bitwise_and))
            link(eng.tensor_scalar(t.place2[:, :, :], t.slot[:, :, :], 7, None, ALU.logical_shift_right))
            eng.scalar_tensor_tensor(out=t.place[:, :, :], in0=t.place[:, :, :], scalar=float(IDW),
                                     in1=t.place2[:, :, :], op0=ALU.mult, op1=ALU.add).then_inc(slots_ready, 1)
            step_no = t.num[:, :]
            last2, cmp_buf = t.base[:, :], u2[:, 0, 0:(NK + 2) * E].rearrange("p (k e) -> p k e", e=E)
            expert, first, count, within, half, live, tmp = (u2[:, 1, i * 128:i * 128 + NK + 2] for i in range(7))
            by_step = lambda v, n: bcast(v.unsqueeze(2), [P, NK + 2, n])
            by_expert = lambda v, n: bcast(v[:, 0:n].unsqueeze(1), [P, NK + 2, n])
            past = cmp_buf[:, :, 0:E - 1]
            link(eng.tensor_scalar(last2, t.last_tile[:, :], 2.0, None, ALU.mult))
            link(eng.tensor_tensor(past, by_step(step_no, E - 1), by_expert(last2, E - 1), ALU.is_ge))
            link(eng.tensor_reduce(expert, past, AX.X, ALU.add))
            link(eng.tensor_tensor(past, past, by_expert(t.ntile[:, :], E - 1), ALU.mult))
            link(eng.tensor_reduce(first, past, AX.X, ALU.add))
            link(eng.tensor_tensor(cmp_buf, by_expert(t.num[:, :], E), by_step(expert, E), ALU.is_equal))
            link(eng.tensor_tensor(cmp_buf, cmp_buf, by_expert(t.ntile[:, :], E), ALU.mult))
            link(eng.tensor_reduce(count, cmp_buf, AX.X, ALU.add))
            link(eng.scalar_tensor_tensor(out=within, in0=first, scalar=-2.0, in1=step_no, op0=ALU.mult, op1=ALU.add))
            link(eng.tensor_tensor(half, within, count, ALU.is_ge))
            link(eng.tensor_tensor(live, step_no, bcast(last2[:, E - 1:E], [P, NK + 2]), ALU.is_lt))
            link(eng.tensor_tensor(tmp, within, count, ALU.is_equal))
            link(eng.scalar_tensor_tensor(out=tmp, in0=within, scalar=0.0, in1=tmp, op0=ALU.is_equal, op1=ALU.add))
            link(eng.tensor_tensor(t.meta[:, 1, :], tmp, live, ALU.mult))
            link(eng.tensor_tensor(tmp, half, count, ALU.mult))
            link(eng.tensor_tensor(within, within, tmp, ALU.subtract))
            link(eng.scalar_tensor_tensor(out=within, in0=within, scalar=float(1 - NT), in1=first, op0=ALU.add, op1=ALU.add))
            link(eng.tensor_tensor(within, within, live, ALU.mult))
            link(eng.tensor_scalar(t.meta[:, 4, :], within, float(NT - 1), None, ALU.add))
            link(eng.tensor_copy(t.meta[:, 0, :], expert))
            link(eng.tensor_copy(t.meta[:, 2, :], live))
            link(eng.tensor_copy(t.meta[:, 3, :], half))

            eng.wait_ge(t.small_in, 64)
            with eng.Fori(0, BATCH) as b:
                q = 8
                for i in range(8):
                    eng.wait_ge(th_r, b * 8 + i + 1)
                    eng.wait_ge(sr_out[i % 2], (b * 4 + i // 2 + 1) * 16)
                    eng.scalar_tensor_tensor(out=srp[i % 2][:, :], in0=th[i % 2][:, :], scalar=1.0,
                                             in1=ring[q % RING][:, :], op0=ALU.add, op1=ALU.mult).then_inc(sr_ready, 1)
                    q += 1

                def silu(i):
                    m, h = pieces[i]
                    eng.wait_ge(th_x, b * 8 + i + 1)
                    eng.scalar_tensor_tensor(out=u2[:, m, h * HALF:(h + 1) * HALF], in0=th2[i % 2][:, :], scalar=1.0,
                                             in1=xsp[i % 2][:, :], op0=ALU.add, op1=ALU.mult).then_inc(u_ready, 1)
                    eng.wait_ge(u_ready, b * 8 + i + 1 + 2)
                    eng.wait_ge(ud_out[i % 2], (b * 4 + i // 2 + 1) * 16)
                    eng.tensor_scalar(udp[i % 2][:, :], u2[:, m, h * HALF:(h + 1) * HALF], t.D[:, m:m + 1], 0.5,
                                      ALU.mult, ALU.mult).then_inc(ud_ready, 1)

                for i, (m, h) in enumerate(pieces):
                    eng.wait_ge(bank_full, b * JOBS + q + 1)
                    eng.wait_ge(xs_out[i % 2], (b * 4 + i // 2 + 1) * 16)
                    eng.wait_ge(u_ready, b * 8 + i + 1)
                    eng.tensor_scalar(xsp[i % 2][:, :], ring[q % RING][:, :], t.conv_b[:, m:m + 1], None,
                                      ALU.add).then_inc(xs_ready, 1)
                    if i >= 1:
                        silu(i - 1)
                    q += 1
                silu(7)
                q = JOBS - 8
                for quad in range(0, 8, 4):
                    for i in range(quad, quad + 4):
                        m = pieces[i][0]
                        eng.wait_ge(abs_ready, b * 8 + i + 1)
                        eng.wait_ge(du_out[i % 4], (b * 2 + i // 4 + 1) * 16)
                        eng.tensor_scalar(dup[i % 4][:, :], ring[q % RING][:, :], t.b_dt[:, m:m + 1], 0.0,
                                          ALU.add, ALU.max).then_inc(z_ready, 1)
                        q += 1
                    for i in range(quad, quad + 4):
                        m, h = pieces[i]
                        at = b * 24 + i * 3
                        e, dl, z = ez[i % 4], dlp[i % 4], dup[i % 4]
                        eng.wait_ge(exp_ready, b * 8 + i + 1)
                        eng.tensor_scalar(w1m, e[:, :], 1.0, -1.0, ALU.add, ALU.add).then_inc(sp_step, 1)
                        eng.wait_ge(ln_ready, b * 8 + i + 1)
                        eng.wait_ge(sp_step, at + 1)
                        eng.tensor_tensor(e[:, :], e[:, :], w1m, ALU.subtract).then_inc(sp_step, 1)
                        eng.wait_ge(sp_step, at + 2)
                        eng.tensor_tensor(e[:, :], e[:, :], dl[:, :], ALU.add).then_inc(sp_step, 1)
                        eng.wait_ge(sp_step, at + 3)
                        eng.wait_ge(z_ready, b * 8 + i + 1 + 8)
                        eng.tensor_tensor(dl[:, :], e[:, :], z[:, :], ALU.add).then_inc(delta_ready, 1)
                        eng.wait_ge(delta_ready, b * 8 + i + 1 + 4)
                        eng.scalar_tensor_tensor(out=z[:, :], in0=dl[:, :], scalar=0.5,
                                                 in1=u2[:, m, h * HALF:(h + 1) * HALF], op0=ALU.mult,
                                                 op1=ALU.mult).then_inc(du_ready, 1)

        @block.sync
        def _(eng):
            with eng.Fori(0, BATCH) as b:
                for i, (m, h) in enumerate(pieces):
                    eng.wait_ge(sr_ready, b * 8 + i + 3)
                    eng.dma_start(row("sr", b, m, h), srp[i % 2][:, :]).then_inc(sr_out[i % 2], 16)
                for i, (m, h) in enumerate(pieces):
                    eng.wait_ge(xs_ready, b * 8 + i + 1)
                    eng.dma_start(row("xs", b, m, h), xsp[i % 2][:, :]).then_inc(xs_out[i % 2], 16)
                    if i >= 1:
                        eng.wait_ge(ud_ready, b * 8 + i)
                        eng.dma_start(row("ud", b, *pieces[i - 1]), udp[(i - 1) % 2][:, :]).then_inc(ud_out[(i - 1) % 2], 16)
                eng.wait_ge(ud_ready, b * 8 + 8)
                eng.dma_start(row("ud", b, *pieces[7]), udp[1][:, :]).then_inc(ud_out[1], 16)
                eng.wait_ge(act_freed, b * XC_X + XC_X)
                for r in range(PAIRS):
                    for s in range(2):
                        eng.dma_start(d["bc"][ds((b * PAIRS + r) * NST, NST), s, :],
                                      bcT[s * NST:(s + 1) * NST, :]).then_inc(bc_out, 16)
                for i, (m, h) in enumerate(pieces):
                    eng.wait_ge(delta_ready, b * 8 + i + 1 + 4)
                    eng.dma_start(row("delta", b, m, h), dlp[i % 4][:, :]).then_inc(delta_out[i % 4], 16)
                    eng.wait_ge(du_ready, b * 8 + i + 5)
                    eng.dma_start(row("du", b, m, h), dup[i % 4][:, :]).then_inc(du_out[i % 4], 16)
            eng.dma_start(d["bc"][ROWS * NST:ROWS * NST + 2, 0, :], bcT[0:2, :]).then_inc(bc_out, 16)
            eng.dma_start(d["bc"][ROWS * NST:ROWS * NST + 2, 1, :], bcT[2:4, :]).then_inc(bc_out, 16)
            for out in (sr_out, xs_out, ud_out, delta_out, du_out):
                for o in out:
                    eng.wait_ge(o, BATCH * 8 * 16 // len(out) + 16)
            eng.wait_ge(bc_out, BATCH * 64 + 96)

        @block.gpsimd
        def _(eng):
            eng.wait_ge(slots_ready, 1)
            eng.wait_ge(t.ids_zeroed, 16)
            n = 0
            for k in range(TOP):
                for i in range(TT):
                    eng.indirect_dma_start(out=d["ids"], out_offset=bass.IndirectOffsetOnAxis(ap=t.place[:, k, i:i + 1], axis=0),
                                           in_=t.tok_id[:, i:i + 1], in_offset=None).then_inc(t.ids_written, 16)
                    n += 16
            eng.wait_ge(t.ids_written, n)
            eng.dma_start(t.ids[:, :], d["ids"].rearrange("(p w) o -> p (w o)", p=P)).then_inc(t.ids_loaded, 16)
            eng.wait_ge(t.ids_loaded, 16)


def experts_and_scan(nc, t, d):
    LAG = 3
    ORDER = [("up", 3), ("down", 0), ("up", 4), ("down", 1), ("turn", 0), ("up", 5), ("down", 2), ("up", 6), ("down", 3),
             ("down", 4), ("down", 5), ("next up", 0), ("next up", 1), ("down", 6), ("next up", 2)]
    assert sorted(f for what, f in ORDER if what == "down") == list(range(NF)) and LAG == 3
    HR = 4
    RING3 = [0, 1, 2, 0, 1, 2, 1]
    RING4 = [f % HR for f in range(NF)]
    CHUNK = 3 * DM
    AHEAD = 3
    F32R = mybir.dt.float32r
    SCAN = [("p", 0, 0), ("s", 0, 0), ("s", 0, 1), ("p", 1, 0), ("q", 0, 0), ("s", 1, 0), ("r", 0, 0), ("s", 1, 1),
            ("q", 1, 0), ("r", 1, 0)]
    NS = len(SCAN)
    STEPS = [1, 2, 1, 2, 2, 1, 1]
    assert sum(STEPS) == NS and len(STEPS) == NF
    done = {key: n + 1 for n, key in enumerate(SCAN)}
    with ExitStack() as ctx:
        sb = lambda n, s, dt=F32: ctx.enter_context(nc.sbuf_tensor(n, s, dt))
        sem = lambda n: ctx.enter_context(nc.semaphore(n))
        ps = lambda n: ctx.enter_context(nc.psum_tensor(n, [P, HALF], F32))
        raw = [sb(f"w_raw{i}", [P, CHUNK]) for i in range(3)]
        whi = [sb(f"w_hi{f}", [P, CHUNK], F32R) for f in range(NF)]
        wlo = [sb(f"w_lo{f}", [P, CHUNK], F32R) for f in range(NF)]
        delta = sb("delta_b", [P, 2, SEQ])
        du = sb("du_b", [P, 2, SEQ])
        y = sb("y_b", [P, 2, SEQ])
        dA = [sb(f"dA{i}", [P, 2, SEQ]) for i in range(2)]
        hs = [sb(f"h_states{i}", [P, 2, SEQ]) for i in range(2)]
        bc = [sb(f"bc{i}", [P, 2, SEQ]) for i in range(2)]
        xg = sb("xg", [P, SH, DM])
        xhi = sb("x_hi", [P, DC, SLOTS], F32R)
        xlo = sb("x_lo", [P, DC, SLOTS], F32R)
        hid = [sb(f"hidden{i}", [P, SLOTS]) for i in range(3)]
        hhi = [sb(f"h_hi{i}", [P, SLOTS], F32R) for i in range(HR)]
        hlo = [sb(f"h_lo{i}", [P, SLOTS], F32R) for i in range(HR)]
        og = sb("og", [P, SH, DM])
        idc = sb("ids_now", [P, SH], U32)
        warm = sb("table_warm", [P, 1])
        ph = [ps(f"ph{i}") for i in range(HR)]
        po = [ps(f"po{i}") for i in range(SH)]
        px = [ps(f"px{i}") for i in range(2)]
        raw_in = [sem(f"raw_in{f}") for f in range(NF)]
        whi_done = sem("whi_done")
        w_ready = sem("w_ready")
        xg_in = sem("xg_in")
        xg_turned = sem("xg_turned")
        xhi_ready = sem("xhi_ready")
        xT_ready = sem("xT_ready")
        up_done = sem("up_done")
        tanh_done = sem("tanh_done")
        gate_step = sem("gate_step")
        val_done = sem("val_done")
        hhi_done = sem("hhi_done")
        hid_done = sem("hid_done")
        down_done = sem("down_done")
        out_copied = sem("out_copied")
        og_free = sem("og_free")
        ys_out = sem("ys_out")
        ids_now = sem("ids_now_ready")
        row_in = sem("row_in")
        y_in = sem("y_in")
        sr_in = sem("sr_in")
        bc_in = [sem(f"bc_in{i}") for i in range(2)]
        dA_ready = sem("dA_ready")
        scan_step = sem("scan_step")
        y_final = sem("y_final")
        y_out = sem("y_out")
        act_sync = sem("act_sync")
        pool_sync = sem("pool_sync")
        block = ctx.enter_context(nc.Block())

        def before(f, ring):
            same = [g for g in range(f) if ring[g] == ring[f]]
            if same:
                return same[-1] + NF
            return max(g for g in range(NF) if ring[g] == ring[f])

        def meta(eng, what, k, most):
            return eng.value_load(t.meta[0:1, what, ds(k, 1)], min_val=0, max_val=most)

        def all_steps(eng, body):
            with eng.Fori(0, BATCH) as b:
                with eng.Fori(0, PAIRS) as r:
                    row = b * PAIRS + r
                    with eng.Fori(0, GROUP - 1) as j:
                        body(row * GROUP + j, (row, r, j), False, False)
                    body(row * GROUP + GROUP - 1, None, row, False)
            with eng.Fori(0, PLAIN) as j:
                live = meta(eng, 2, ROWS * GROUP + j, 1)
                with eng.If(live > 0):
                    body(ROWS * GROUP + j, None, False, True)

        @block.sync
        def _(eng):
            def chunk(e, h, f):
                dst = raw[RING3[f]]
                at = h * HM + f * P
                for n, name in enumerate(("w1", "w3")):
                    eng.dma_start(dst[:, n * DM:(n + 1) * DM].rearrange("p (k m) -> p k m", m=P),
                                  d[name][ds(e, 1), :, ds(at, P)].rearrange("o (k p) m -> (o p) k m", p=P)).then_inc(raw_in[f], 16)
                eng.dma_start(dst[:, 2 * DM:3 * DM], d["w2"][ds(e, 1), ds(at, P), :].rearrange("o p n -> (o p) n")).then_inc(raw_in[f], 16)

            def weights(k, chunks):
                again = meta(eng, 1, k, 2)
                for f in chunks:
                    prev = before(f, RING3)
                    free = (k * NF + prev - NF if prev >= NF else (k - 1) * NF + prev) + 1 + 1
                    with eng.If(again > 0):
                        e = meta(eng, 0, k, E - 1)
                        h = meta(eng, 3, k, 1)
                        eng.wait_ge(w_ready, free)
                        chunk(e, h, f)
                    with eng.Else():
                        eng.wait_ge(w_ready, free)
                        eng.sem_inc(raw_in[f], 48)

            def bc_load(m, i):
                eng.dma_start(bc[i][:, :, :].rearrange("p s n -> p (s n)"),
                              bcast(d["bc"][ds(m, 1), :, :].rearrange("o s n -> o (s n)"), [P, 2 * SEQ])).then_inc(bc_in[i], 16)

            def body(k, scan, final, plain):
                weights(k, [NF - 1])
                if scan is None:
                    weights(k + 1, range(NF - 1))
                    return
                row, r, j = scan
                at = (row * (GROUP - 1) + j) * NS + NS
                for chunks, i in (((0, 1, 2), 0), ((3, 4), 1), ((5,), None)):
                    if i is not None:
                        weights(k + 1, chunks)
                        eng.wait_ge(scan_step, at + done["q", i, 0])
                        bc_load(row * NST + j * 2 + 2 + i, i)
                    else:
                        weights(k + 1, chunks)

            e0 = meta(eng, 0, 0, E - 1)
            for f in range(NF - 1):
                if f >= 3:
                    eng.wait_ge(w_ready, before(f, RING3) - NF + 1 + 1)
                chunk(e0, 0, f)
                if f < 2:
                    bc_load(f, f)
            all_steps(eng, body)
            for i in range(2):
                eng.wait_ge(bc_in[i], 16 * (ROWS * NST // 2 + 1))

        @block.gpsimd
        def _(eng):
            def gather(k):
                tile = meta(eng, 4, k, NT - 1)
                eng.tensor_copy(idc[:, :], t.ids[:, ds(tile * SH, SH)]).then_inc(ids_now, 1)
                eng.wait_ge(ids_now, k + 1)
                eng.sem_inc(pool_sync, 1)
                for s in range(SH):
                    eng.indirect_dma_start(out=xg[:, s, :], out_offset=None, in_=d["xn"],
                                           in_offset=bass.IndirectOffsetOnAxis(ap=idc[:, s:s + 1], axis=0)).then_inc(xg_in, 16)

            def outputs(k):
                tile = meta(eng, 4, k, NT - 1)
                half = meta(eng, 3, k, 1)
                eng.wait_ge(out_copied, k * SH + 2 * SH)
                eng.sem_inc(pool_sync, 1)
                eng.dma_start(d["ys"][ds(tile, 1), :, ds(half, 1), :].rearrange("o (s p) h n -> (o p) s (h n)", p=P),
                              og[:, :, :]).then_inc(ys_out, 16)
                eng.wait_ge(ys_out, k * 16 + 16)
                eng.sem_inc(og_free, 1)

            def load(buf, name, row):
                return eng.dma_start(buf[:, :, :], d[name][ds(row, 1), :, :, :].rearrange("o p c n -> (o p) c n"))

            def body(k, scan, final, plain):
                if final is not False:
                    eng.wait_ge(scan_step, (final + 1) * (GROUP - 1) * NS + NS)
                    eng.sem_inc(pool_sync, 1)
                    load(dA[0], "sr", final).then_inc(sr_in, 16)
                    with eng.If(final < ROWS - 1):
                        load(delta, "delta", final + 1).then_inc(row_in, 16)
                        load(du, "du", final + 1).then_inc(row_in, 16)
                eng.wait_ge(xg_turned, k + 2)
                eng.sem_inc(pool_sync, 1)
                gather(k + 2)
                if final is not False:
                    eng.wait_ge(y_final, final + 2)
                    eng.sem_inc(pool_sync, 1)
                    eng.dma_start(d["yg"][ds(final, 1), :, :, :].rearrange("o p c n -> (o p) c n"), y[:, :, :]).then_inc(y_out, 16)
                    eng.wait_ge(y_out, final * 16 + 16)
                    eng.sem_inc(pool_sync, 1)
                    with eng.If(final < ROWS - 1):
                        load(y, "ud", final + 1).then_inc(y_in, 16)
                outputs(k)
                if plain:
                    eng.wait_ge(xg_in, k * 32 + 96)
                    eng.sem_inc(pool_sync, 1)

            gather(0)
            load(delta, "delta", 0).then_inc(row_in, 16)
            load(du, "du", 0).then_inc(row_in, 16)
            load(y, "ud", 0).then_inc(y_in, 16)
            eng.wait_ge(xg_turned, 1)
            eng.sem_inc(pool_sync, 1)
            gather(1)
            all_steps(eng, body)
            eng.wait_ge(xg_in, (ROWS * GROUP + 2) * 32)

        @block.tensor
        def _(eng):
            eng.sem_inc(down_done, NF)

            def turn(k):
                eng.wait_ge(xg_in, k * 32 + 32)
                for c in range(DC):
                    for s in range(SH):
                        last = eng.transpose(px[c // 2][:, (c % 2) * SLOTS + s * P:(c % 2) * SLOTS + (s + 1) * P],
                                             xg[:, s, c * P:(c + 1) * P], t.ident[:, :])
                last.then_inc(xg_turned, 1)

            def up_waits(k, f):
                if f == 0:
                    eng.wait_ge(xT_ready, k * 2 + 2)
                eng.wait_ge(w_ready, k * NF + f + 1 + 1)
                eng.wait_ge(val_done, k * NF + before(f, RING4) + 1)

            def up(k, f):
                up_waits(k, f)
                for n in range(2):
                    for c in range(DC):
                        at = n * DM + c * P
                        for p, (w, x) in enumerate(((whi, xhi), (whi, xlo), (wlo, xhi))):
                            last = eng.matmul(ph[RING4[f]][:, n * SLOTS:(n + 1) * SLOTS], w[f][:, at:at + P], x[:, c, :],
                                              start=(n == 0 and c == 0 and p == 0), stop=(c == DC - 1 and p == 2),
                                              skip_group_check=True)
                last.then_inc(up_done, 1)

            def down_waits(k, f):
                eng.wait_ge(hid_done, k * NF + NF + f + 1)
                if f == 0:
                    eng.wait_ge(out_copied, k * SH + SH)

            def down(k, f):
                down_waits(k, f)
                for s in range(SH):
                    for p, (h, w) in enumerate(((hhi, whi), (hhi, wlo), (hlo, whi))):
                        last = eng.matmul(po[s][:, :], h[RING4[f]][:, s * P:(s + 1) * P], w[f][:, 2 * DM:3 * DM],
                                          start=(f == 0 and p == 0), stop=(f == NF - 1 and p == 2))
                last.then_inc(down_done, 1)

            def work(k):
                for what, f in ORDER:
                    if what == "up":
                        up(k, f)
                    elif what == "next up":
                        up(k + 1, f)
                    elif what == "down":
                        down(k, f)
                    else:
                        turn(k + 1)

            def body(k, scan, final, plain):
                if plain:
                    work(k)
                    return
                live = meta(eng, 2, k, 1)
                with eng.If(live > 0):
                    work(k)
                with eng.Else():
                    eng.drain()
                    for what, f in ORDER:
                        if what == "turn":
                            eng.wait_ge(xg_in, k * 32 + 64)
                            eng.sem_inc(xg_turned, 1)
                        elif what == "down":
                            down_waits(k, f)
                            eng.sem_inc(down_done, 1)
                        else:
                            up_waits(k if what == "up" else k + 1, f)
                            eng.sem_inc(up_done, 1)

            turn(0)
            for f in range(LAG):
                up(0, f)
            all_steps(eng, body)

        @block.scalar
        def _(eng):
            def split(k, f):
                eng.wait_ge(raw_in[f], k * 48 + 48)
                eng.wait_ge(down_done, k * NF + f + 1)
                eng.activation(whi[f][:, :], raw[RING3[f]][:, :], ACT.Copy).then_inc(whi_done, 1)

            def kept(k, f, count):
                eng.wait_ge(whi_done, k * NF + f + 1)
                eng.sem_inc(whi_done, count)

            def turned(k):
                eng.wait_ge(xg_turned, k + 1)
                eng.wait_ge(up_done, k * NF + 1)
                for i in range(2):
                    eng.activation(xhi[:, 2 * i:2 * i + 2, :].rearrange("p c n -> p (c n)"), px[i][:, :],
                                   ACT.Copy).then_inc(xhi_ready, 1)

            def tanh(k, f):
                eng.wait_ge(up_done, k * NF + f + 1 + 1)
                eng.wait_ge(hid_done, k * NF + before(f, RING3) + 1)
                eng.activation(hid[RING3[f]][:, :], ph[RING4[f]][:, 0:SLOTS], ACT.Tanh, scale=0.5).then_inc(tanh_done, 1)

            def hidden_hi(k, f):
                eng.wait_ge(val_done, k * NF + NF + f + 1)
                eng.wait_ge(down_done, k * NF + before(f, RING4) + 1)
                eng.activation(hhi[RING4[f]][:, :], hid[RING3[f]][:, :], ACT.Copy).then_inc(hhi_done, 1)

            def decay(scan, i, c):
                row, r, j = scan
                at = (row * (GROUP - 1) + j) * NS
                eng.wait_ge(scan_step, at + done["s", i, c])
                if i == 0 and c == 0:
                    eng.sem_inc(act_sync, 1)
                    eng.wait_ge(row_in, row * 32 + 32)
                    eng.sem_inc(act_sync, 1)
                    eng.wait_ge(y_final, row + 1)
                eng.sem_inc(act_sync, 1)
                eng.activation(dA[i][:, c, :], delta[:, c, :], ACT.Exp,
                               scale=t.A[:, ds((r * 2 + c) * NST + j * 2 + i, 1)]).then_inc(dA_ready, 1)

            def outputs(k):
                eng.wait_ge(down_done, k * NF + 2 * NF)
                eng.wait_ge(og_free, k + 1)
                for s in range(SH):
                    eng.activation(og[:, s, :], po[s][:, :], ACT.Copy).then_inc(out_copied, 1)

            WHEN = {1: ((0, 0),), 2: ((0, 1),), 3: ((1, 0),), 4: ((1, 1),)}

            def body(k, scan, final, plain):
                def chunks(fs, fresh):
                    for f in fs:
                        if f == NF - 1:
                            turned(k + 1)
                        if f < NF:
                            tanh(k, f)
                        else:
                            tanh(k + 1, 0)
                        if fresh:
                            if f + AHEAD < NF:
                                split(k, f + AHEAD)
                            else:
                                split(k + 1, f + AHEAD - NF)
                        if scan is not None and f in WHEN:
                            for i, c in WHEN[f]:
                                decay(scan, i, c)
                        if f < NF:
                            hidden_hi(k, f)

                again = meta(eng, 1, k, 2)
                hidden_hi(k, 0)
                with eng.If(again > 0):
                    chunks(range(1, NF - AHEAD), True)
                with eng.Else():
                    kept(k, AHEAD + 1, NF - AHEAD - 1)
                    chunks(range(1, NF - AHEAD), False)
                then = meta(eng, 1, k + 1, 2)
                with eng.If(then > 0):
                    chunks(range(NF - AHEAD, NF + 1), True)
                with eng.Else():
                    kept(k + 1, 0, AHEAD + 1)
                    chunks(range(NF - AHEAD, NF + 1), False)
                outputs(k)

            eng.activation(warm[:, :], t.A[:, 0:1], ACT.Exp)
            for f in range(AHEAD):
                split(0, f)
            turned(0)
            tanh(0, 0)
            split(0, AHEAD)
            all_steps(eng, body)

        @block.vector
        def _(eng):
            eng.sem_inc(val_done, NF)
            eng.sem_inc(hid_done, NF)
            eng.sem_inc(scan_step, NS)
            eng.sem_inc(out_copied, SH)
            eng.sem_inc(og_free, 1)
            eng.sem_inc(y_final, 1)
            eng.sem_inc(up_done, 1)
            eng.sem_inc(whi_done, 1)
            eng.sem_inc(w_ready, 1)

            def split(k, f):
                eng.wait_ge(whi_done, k * NF + f + 1 + 1)
                eng.tensor_tensor(wlo[f][:, :], raw[RING3[f]][:, :], whi[f][:, :].bitcast(F32), ALU.subtract).then_inc(w_ready, 1)

            def kept(k, f, count):
                eng.wait_ge(w_ready, k * NF + f + 1)
                eng.sem_inc(w_ready, count)

            def turned(k):
                for i in range(2):
                    eng.wait_ge(xhi_ready, k * 2 + i + 1)
                    eng.tensor_tensor(xlo[:, 2 * i:2 * i + 2, :].rearrange("p c n -> p (c n)"), px[i][:, :],
                                      xhi[:, 2 * i:2 * i + 2, :].rearrange("p c n -> p (c n)").bitcast(F32),
                                      ALU.subtract).then_inc(xT_ready, 1)

            def gate(k, f):
                eng.wait_ge(tanh_done, k * NF + f + 1)
                eng.scalar_tensor_tensor(out=hid[RING3[f]][:, :], in0=hid[RING3[f]][:, :], scalar=1.0,
                                         in1=ph[RING4[f]][:, 0:SLOTS], op0=ALU.add, op1=ALU.mult).then_inc(gate_step, 1)

            def value(k, f):
                eng.wait_ge(gate_step, k * NF + f + 1)
                eng.scalar_tensor_tensor(out=hid[RING3[f]][:, :], in0=hid[RING3[f]][:, :], scalar=0.5,
                                         in1=ph[RING4[f]][:, SLOTS:2 * SLOTS], op0=ALU.mult, op1=ALU.mult).then_inc(val_done, 1)

            def hidden_lo(k, f):
                eng.wait_ge(hhi_done, k * NF + f + 1)
                eng.tensor_tensor(hlo[RING4[f]][:, :], hid[RING3[f]][:, :], hhi[RING4[f]][:, :].bitcast(F32),
                                  ALU.subtract).then_inc(hid_done, 1)

            def scan_one(scan, n):
                row, r, j = scan
                kind, i, c = SCAN[n]
                m = row * (GROUP - 1) + j
                at = m * NS + NS
                need = lambda *key: eng.wait_ge(scan_step, at + done[key])
                if kind == "p":
                    if i == 0:
                        eng.wait_ge(row_in, row * 32 + 32)
                    eng.wait_ge(bc_in[i], m * 16 + 16)
                    eng.wait_ge(scan_step, at - NS + done["r", i, 0])
                    ins = eng.tensor_tensor(hs[i][:, :, :], du[:, :, :], bcast(bc[i][:, 0:1, :], [P, 2, SEQ]), ALU.mult)
                elif kind == "s":
                    need("p", i, 0)
                    eng.wait_ge(dA_ready, m * 4 + i * 2 + c + 1)
                    ins = eng.tensor_tensor_scan(hs[i][:, c, :], dA[i][:, c, :], hs[i][:, c, :], 0.0, ALU.mult, ALU.add)
                elif kind == "q":
                    need("s", i, 1)
                    ins = eng.tensor_tensor(hs[i][:, :, :], hs[i][:, :, :], bcast(bc[i][:, 1:2, :], [P, 2, SEQ]), ALU.mult)
                else:
                    if i == 0:
                        eng.wait_ge(y_in, row * 16 + 16)
                    need("q", i, 0)
                    ins = eng.tensor_tensor(y[:, :, :], y[:, :, :], hs[i][:, :, :], ALU.add)
                ins.then_inc(scan_step, 1)

            def body(k, scan, final, plain):
                def chunks(fs, fresh):
                    for f in fs:
                        if f == NF - 1:
                            hidden_lo(k, f - 1)
                            turned(k + 1)
                        gate(k, f)
                        if 0 < f < NF - 1:
                            hidden_lo(k, f - 1)
                        value(k, f)
                        if f == NF - 1:
                            hidden_lo(k, f)
                        if fresh:
                            if f + AHEAD < NF:
                                split(k, f + AHEAD)
                            else:
                                split(k + 1, f + AHEAD - NF)
                        if scan is not None:
                            for n in range(sum(STEPS[:f]), sum(STEPS[:f + 1])):
                                scan_one(scan, n)
                        if final is not False and f == NF - 3:
                            eng.wait_ge(sr_in, final * 16 + 16)
                            flat = lambda v: v[:, :, :].rearrange("p c n -> p (c n)")
                            eng.scalar_tensor_tensor(out=flat(y), in0=flat(y), scalar=0.5, in1=flat(dA[0]),
                                                     op0=ALU.mult, op1=ALU.mult).then_inc(y_final, 1)

                again = meta(eng, 1, k, 2)
                with eng.If(again > 0):
                    chunks(range(NF - AHEAD), True)
                with eng.Else():
                    kept(k, AHEAD, NF - AHEAD)
                    chunks(range(NF - AHEAD), False)
                then = meta(eng, 1, k + 1, 2)
                with eng.If(then > 0):
                    chunks(range(NF - AHEAD, NF), True)
                with eng.Else():
                    kept(k + 1, 0, AHEAD)
                    chunks(range(NF - AHEAD, NF), False)

            for f in range(AHEAD):
                split(0, f)
            turned(0)
            all_steps(eng, body)

def mamba_out_and_combine(nc, t, d):
    with ExitStack() as ctx:
        sb = lambda n, s, dt=F32: ctx.enter_context(nc.sbuf_tensor(n, s, dt))
        sem = lambda n: ctx.enter_context(nc.semaphore(n))
        NB = 4
        wo = sb("W_out", [P, CC, DM])
        yg = [sb(f"yg{i}", [P, CC, P]) for i in range(NB)]
        xs = [sb(f"xs{i}", [P, CC, P]) for i in range(NB)]
        xr = [sb(f"xr{i}", [P, DM]) for i in range(NB)]
        e1 = [sb(f"e1_{i}", [P, 2 * DM]) for i in range(NB)]
        e2 = [sb(f"e2_{i}", [P, 2 * DM]) for i in range(NB)]
        acc = [sb(f"acc{i}", [P, DM]) for i in range(NB)]
        sl = [sb(f"slot_now{i}", [P, TOP], U32) for i in range(NB)]
        wg = [sb(f"weight_now{i}", [P, TOP]) for i in range(NB)]
        pz = [ctx.enter_context(nc.psum_tensor(f"pz{i}", [P, DM], F32)) for i in range(NB)]
        wo_in = sem("wo_in")
        mm_in = [sem(f"mm_in{i}") for i in range(NB)]
        e_in = [sem(f"e_in{i}") for i in range(NB)]
        out_st = [sem(f"out_stored{i}") for i in range(NB)]
        proj = sem("proj")
        summed = sem("summed")
        sum_step = sem("sum_step")
        now = sem("slots_now")
        pool_sync = sem("pool_sync4")
        block = ctx.enter_context(nc.Block())
        ROUNDS = TT // NB

        @block.sync
        def _(eng):
            eng.dma_start(wo[:, :, :], d["W_out"].rearrange("(c p) n -> p c n", p=P)).then_inc(wo_in, 16)
            with eng.Fori(0, BATCH) as b:
                for k in range(TPB):
                    i = k % NB
                    tile = b * TPB + k
                    eng.wait_ge(summed, tile + 1)
                    for buf, name in ((yg, "yg"), (xs, "xs")):
                        for r in range(PAIRS):
                            eng.dma_start(buf[i][:, 2 * r:2 * r + 2, :], d[name][ds(b * PAIRS + r, 1), :, :, k * P:(k + 1) * P].rearrange(
                                "o p c n -> (o p) c n")).then_inc(mm_in[i], 16)
                    eng.dma_start(xr[i][:, :], d["x"][ds(tile * P, P), :]).then_inc(mm_in[i], 16)

        @block.gpsimd
        def _(eng):
            with eng.Fori(0, ROUNDS) as r:
                for i in range(NB):
                    tile = r * NB + i
                    eng.wait_ge(summed, tile + 1)
                    eng.sem_inc(pool_sync, 1)
                    eng.tensor_copy(sl[i][:, :], t.slot[:, :, ds(tile, 1)].rearrange("p k o -> p (k o)")).then_inc(now, 1)
                    eng.tensor_copy(wg[i][:, :], t.wgt[:, :, ds(tile, 1)].rearrange("p k o -> p (k o)")).then_inc(now, 1)
                    eng.wait_ge(now, tile * 2 + 2)
                    eng.sem_inc(pool_sync, 1)
                    for k, buf in enumerate((e1, e2)):
                        eng.indirect_dma_start(out=buf[i][:, :], out_offset=None, in_=d["ys"].rearrange("t s h n -> (t s) (h n)"),
                                               in_offset=bass.IndirectOffsetOnAxis(ap=sl[i][:, k:k + 1], axis=0)).then_inc(e_in[i], 16)

        @block.tensor
        def _(eng):
            eng.sem_inc(summed, NB)
            for i in range(NB):
                eng.sem_inc(out_st[i], 16)
            eng.wait_ge(wo_in, 16)
            with eng.Fori(0, ROUNDS) as r:
                for i in range(NB):
                    eng.wait_ge(mm_in[i], r * 80 + 80)
                    eng.wait_ge(summed, r * NB + i + 1)
                    for c in range(CC):
                        eng.matmul(pz[i][:, :], yg[i][:, c, :], wo[:, c, :], start=(c == 0), stop=False, skip_group_check=True)
                    for c in range(CC):
                        last = eng.matmul(pz[i][:, c * P:(c + 1) * P], xs[i][:, c, :], t.ident[:, :], start=False,
                                          stop=(c == CC - 1), skip_group_check=True)
                    last.then_inc(proj, 1)

        @block.vector
        def _(eng):
            with eng.Fori(0, ROUNDS) as r:
                for i in range(NB):
                    tile = r * NB + i
                    eng.wait_ge(proj, tile + 1)
                    eng.wait_ge(mm_in[i], r * 80 + 80)
                    eng.wait_ge(out_st[i], r * 16 + 16)
                    eng.tensor_tensor(acc[i][:, :], xr[i][:, :], pz[i][:, :], ALU.add).then_inc(sum_step, 1)
                    eng.wait_ge(e_in[i], r * 32 + 32)
                    eng.wait_ge(now, tile * 2 + 2)
                    for n in range(4):
                        eng.wait_ge(sum_step, tile * 4 + n + 1)
                        ins = eng.scalar_tensor_tensor(out=acc[i][:, :], in0=(e1, e2)[n // 2][i][:, (n % 2) * DM:(n % 2 + 1) * DM],
                                                       scalar=wg[i][:, n // 2:n // 2 + 1], in1=acc[i][:, :],
                                                       op0=ALU.mult, op1=ALU.add)
                        ins.then_inc(sum_step if n < 3 else summed, 1)

        @block.scalar
        def _(eng):
            with eng.Fori(0, ROUNDS) as r:
                for i in range(NB):
                    tile = r * NB + i
                    eng.wait_ge(summed, tile + 1 + NB)
                    eng.dma_start(d["out"][ds(tile * P, P), :], acc[i][:, :]).then_inc(out_st[i], 16)
            for i in range(NB):
                eng.wait_ge(out_st[i], ROUNDS * 16 + 16)


class Shared:
    pass


def build(nc, d):
    d["xn"] = dram(nc, "xn_d", [TOKENS, DM])
    for name in ("sr", "xs", "ud", "delta", "du", "yg"):
        d[name] = dram(nc, f"{name}_d", [ROWS + 1, P, 2, SEQ])
    d["bc"] = dram(nc, "bc_d", [ROWS * NST + 2, 2, SEQ])
    d["ids"] = dram(nc, "ids_d", [P * IDW, 1], U32)
    d["ys"] = dram(nc, "ys_d", [NT, SLOTS, 2, DM])
    with ExitStack() as ctx:
        sem = lambda n: ctx.enter_context(nc.semaphore(n))
        sb = lambda n, s, dt=F32: ctx.enter_context(nc.sbuf_tensor(n, s, dt))
        t = Shared()
        t.ident = sb("ident", [P, P])
        t.ones = sb("ones", [P, P])
        t.A = sb("A", [P, CC * NST])
        t.ids = sb("ids", [P, IDW], U32)
        t.slot = sb("slot", [P, TOP, TT], U32)
        t.wgt = sb("wgt", [P, TOP, TT])
        t.meta = sb("meta", [P, 5, NK + 2], I32)
        t.gate_in = sem("gate_in")
        t.small_in = sem("small_in")
        t.w_in = sem("w_in")
        t.const_ready = sem("const_ready")
        t.ids_zeroed = sem("ids_zeroed")
        t.ids_written = sem("ids_written")
        t.ids_loaded = sem("ids_loaded")
        t.logits_ready = sem("logits_ready")
        t.a_step = sem("a_step")
        with ExitStack() as front:
            fsb = lambda n, s, dt=F32: front.enter_context(nc.sbuf_tensor(n, s, dt))
            t.xnT = fsb("xnT", [P, DC, TOKENS])
            t.W_in = fsb("W_in", [P, DC, 2 * DIN])
            t.conv_w = fsb("conv_w", [P, KC, CC, DIN])
            t.W_x = fsb("W_x", [P, CC, NX])
            t.W_dt = fsb("W_dt", [P, DIN])
            t.gate = fsb("gate", [P, DC, E])
            t.conv_b = fsb("conv_b", [P, CC])
            t.b_dt = fsb("b_dt", [P, CC])
            t.D = fsb("D", [P, CC])
            t.A_log = fsb("A_log", [P, CC, NST])
            t.xcT = fsb("xcT", [P, CC, SEQ + KC - 1])
            t.tri = fsb("tri", [P, P])
            t.tok_id = fsb("tok_id", [P, TT], U32)
            t.num_i = fsb("num_i", [P, NK + 2], I32)
            t.num = fsb("num", [P, NK + 2])
            t.zero_ids = fsb("zero_ids", [P, IDW], U32)
            t.prob = fsb("prob", [P, TT, E])
            t.red = fsb("red", [P, TT])
            t.red2 = fsb("red2", [P, TT])
            t.top = fsb("top", [P, TT, 8])
            t.topi = fsb("topi", [P, TT, 8], U32)
            t.topf = fsb("topf", [P, TOP, TT])
            t.hot = fsb("hot", [P, TOP, TT, E])
            t.mask = fsb("mask", [P, TT, E])
            t.tot = fsb("tot", [P, E, TT])
            t.cum = fsb("cum", [P, E, TT])
            t.cnt_i = fsb("cnt_i", [P, E], I32)
            t.ntile = fsb("ntile", [P, E])
            t.last_tile = fsb("last_tile", [P, E])
            t.base = fsb("base", [P, E])
            t.place = fsb("place", [P, TOP, TT], U32)
            t.place2 = fsb("place2", [P, TOP, TT], U32)
            t.ps_lg = front.enter_context(nc.psum_tensor("ps_lg", [P, HALF], F32))
            norm_and_route_logits(nc, t, d)
            mamba_front(nc, t, d)
        experts_and_scan(nc, t, d)
        mamba_out_and_combine(nc, t, d)


def kernel(**inputs):
    import numpy as np
    import concourse.bacc as bacc
    from concourse.bass_utils import run_bass_kernel_spmd

    lay = {
        "x": inputs["L0_attn_x"].reshape(TOKENS, DM),
        "W_in": inputs["L0_attn_W_in"],
        "conv_w": np.transpose(np.asarray(inputs["L0_attn_conv_w"]), (2, 1, 0)),
        "conv_b": np.asarray(inputs["L0_attn_conv_b"]).reshape(CC, P).T,
        "W_x": inputs["L0_attn_W_x"],
        "W_dt": inputs["L0_attn_W_dt"],
        "b_dt": np.asarray(inputs["L0_attn_b_dt"]).reshape(CC, P).T,
        "A_log": inputs["L0_attn_A_log"],
        "D": np.asarray(inputs["L0_attn_D"]).reshape(CC, P).T,
        "W_out": inputs["L0_attn_W_out"],
        "gate_w": inputs["L0_ffn_gate_w"],
        "w1": inputs["L0_ffn_w1"],
        "w2": inputs["L0_ffn_w2"],
        "w3": inputs["L0_ffn_w3"],
    }
    nc = bacc.Bacc("TRN2", target_bir_lowering=False, num_devices=1)
    arrays, d = {}, {}
    for name, a in lay.items():
        a = np.ascontiguousarray(a)
        arrays[f"in_{name}"] = a
        d[name] = nc.dram_tensor(f"in_{name}", a.shape, mybir.dt.from_np(a.dtype), kind="ExternalInput").ap()
    d["out"] = nc.dram_tensor("out_0", (TOKENS, DM), F32, kind="ExternalOutput").ap()
    build(nc, d)
    r = run_bass_kernel_spmd(nc, [arrays], core_ids=[0])
    return r.results[0]["out_0"].reshape(BATCH, SEQ, DM)
```

```python
from contextlib import ExitStack

import concourse.bass as bass
from concourse import mybir

F32 = mybir.dt.float32
I32 = mybir.dt.int32
U32 = mybir.dt.uint32
F32R = mybir.dt.float32r
ACT = mybir.ActivationFunctionType
ALU = mybir.AluOpType
AX = mybir.AxisListType
ds = bass.ds

P = 128
BATCH, SEQ, DM = 4, 1024, 512
TOKENS = BATCH * SEQ
DC = DM // P
DIN, NST, DTR, KC = 512, 16, 128, 4
CC = DIN // P
NX = DTR + 2 * NST
HALF = 512
NH = SEQ // HALF
E, TOP = 8, 2
MH = 1792
TT = TOKENS // P
TPB = SEQ // P
SLOTS = 256
SH = SLOTS // P
SHIFT = 8
NT = (TOKENS * TOP - E) // SLOTS + E + 1
IDW = NT * SH
NF = MH // P // 2
HM = NF * P
PAIRS = CC // 2
ROWS = BATCH * PAIRS
GROUP = 9
PLAIN = 2 * NT - ROWS * GROUP
NK = ROWS * GROUP + PLAIN
assert PLAIN > 0 and 2 * (GROUP - 1) == NST
EPS = 1e-5
LOG_MAX = 80.0


def dram(nc, name, shape, dt=F32):
    return nc.dram_tensor(name, shape, dt, kind="Internal").ap()


def bcast(ap, shape):
    return ap.broadcast_to(shape)


def norm_and_route_logits(nc, t, d):
    GT = 4
    NG = TT // GT
    with ExitStack() as ctx:
        sb = lambda n, s, dt=F32: ctx.enter_context(nc.sbuf_tensor(n, s, dt))
        sem = lambda n: ctx.enter_context(nc.semaphore(n))
        xnT = sb("xnT", [P, DC, TOKENS])
        xin = [sb(f"xin{i}", [P, GT, DM]) for i in range(2)]
        xno = [sb(f"xno{i}", [P, GT, DM]) for i in range(2)]
        st = sb("ln_stats", [P, GT, 6])
        mv = sb("ln_mean_var", [P, GT, 2])
        ve = sb("ln_var_eps", [P, GT])
        sd = sb("ln_std", [P, GT])
        r0 = sb("ln_rstd0", [P, GT])
        r1 = sb("ln_newton", [P, GT])
        rs = sb("ln_rstd", [P, GT])
        lgT = sb("logits_T", [E, TOKENS])
        plg = [ctx.enter_context(nc.psum_tensor(f"plg{i}", [P, HALF], F32)) for i in range(2)]
        ptr = [ctx.enter_context(nc.psum_tensor(f"ptr{i}", [P, HALF], F32)) for i in range(4)]
        x_in = [sem(f"x_in{i}") for i in range(2)]
        var_ready = sem("var_ready")
        std_ready = sem("std_ready")
        ln_step = sem("ln_step")
        ln_sync = sem("ln_sync")
        xn_ready = sem("xn_ready")
        xn_stored = [sem(f"xn_stored{i}") for i in range(2)]
        xnT_stored = [sem(f"xnT_stored{i}") for i in range(2)]
        tr_ready = sem("tr_ready")
        lgT_ready = sem("lgT_ready")
        lgT_copied = sem("lgT_copied")
        tr_copied = sem("tr_copied")
        consts = sem("consts1")
        ys_filled = sem("ys_filled")
        zero_row = sb("zero_row", [P, DM])
        x_v = d["x"].rearrange("(g t p) c -> g p t c", p=P, t=GT)
        xn_v = d["xn"].rearrange("(g t p) c -> g p t c", p=P, t=GT)
        block = ctx.enter_context(nc.Block())

        def one_behind(eng, group, logits):
            group(0, 0)
            with eng.Fori(0, NG // 2 - 1) as g:
                group(g, 1)
                logits(g, 0)
                group(g + 1, 0)
                logits(g, 1)
            group(NG // 2 - 1, 1)
            logits(NG // 2 - 1, 0)
            logits(NG // 2 - 1, 1)

        @block.sync
        def _(eng):
            for i in range(2):
                eng.dma_start(xin[i][:, :, :], x_v[i]).then_inc(x_in[i], 16)
            eng.dma_start(t.gate[:, :, :], d["gate_w"].rearrange("(c p) e -> p c e", p=P)).then_inc(t.gate_in, 16)
            eng.dma_start(t.conv_b[:, :], d["conv_b"]).then_inc(t.small_in, 16)
            eng.dma_start(t.b_dt[:, :], d["b_dt"]).then_inc(t.small_in, 16)
            eng.dma_start(t.D[:, :], d["D"]).then_inc(t.small_in, 16)
            eng.dma_start(t.A_log[:, :, :], d["A_log"].rearrange("(c p) n -> p c n", p=P)).then_inc(t.small_in, 16)
            eng.dma_start(t.W_in[:, :, :], d["W_in"].rearrange("(c p) n -> p c n", p=P)).then_inc(t.w_in, 16)
            with eng.Fori(0, NG // 2 - 1) as g:
                for i in range(2):
                    eng.wait_ge(xn_ready, (g * 2 + i + 1) * GT)
                    eng.dma_start(xin[i][:, :, :], x_v[ds(g * 2 + i + 2, 1)].rearrange("o p t c -> (o p) t c")).then_inc(x_in[i], 16)
            eng.dma_start(t.W_x[:, :, :], d["W_x"].rearrange("(c p) n -> p c n", p=P)).then_inc(t.w_in, 16)
            eng.dma_start(t.W_dt[:, :], d["W_dt"]).then_inc(t.w_in, 16)
            for i in range(2):
                eng.wait_ge(xnT_stored[i], 32)
            eng.dma_start(t.xn_b[:, :, :], d["xnT"][0:1, :, :, :].rearrange("o p c n -> (o p) c n")).then_inc(t.xn_in, 16)

        @block.vector
        def _(eng):
            def group(g, i):
                base = g * (2 * (GT + 6)) + i * (GT + 6)
                eng.wait_ge(x_in[i], g * 16 + 16)
                for k in range(GT):
                    eng.bn_stats(st[:, k, :], xin[i][:, k, :]).then_inc(ln_step, 1)
                eng.wait_ge(ln_step, base + GT)
                eng.sem_inc(ln_sync, 1)
                for k in range(GT):
                    last = eng.bn_aggr(mv[:, k, :], st[:, k, :])
                last.then_inc(ln_step, 1)
                eng.wait_ge(ln_step, base + GT + 1)
                eng.tensor_scalar(ve[:, :], mv[:, :, 1], EPS, None, ALU.add).then_inc(var_ready, 1)
                eng.wait_ge(std_ready, g * 2 + i + 1)
                eng.reciprocal(r0[:, :], sd[:, :]).then_inc(ln_step, 1)
                eng.wait_ge(ln_step, base + GT + 2)
                eng.tensor_tensor(r1[:, :], r0[:, :], r0[:, :], ALU.mult).then_inc(ln_step, 1)
                eng.wait_ge(ln_step, base + GT + 3)
                eng.tensor_tensor(r1[:, :], r1[:, :], ve[:, :], ALU.mult).then_inc(ln_step, 1)
                eng.wait_ge(ln_step, base + GT + 4)
                eng.tensor_scalar(r1[:, :], r1[:, :], -0.5, 1.5, ALU.mult, ALU.add).then_inc(ln_step, 1)
                eng.wait_ge(ln_step, base + GT + 5)
                eng.tensor_tensor(rs[:, :], r1[:, :], r0[:, :], ALU.mult).then_inc(ln_step, 1)
                eng.wait_ge(ln_step, base + GT + 6)
                eng.wait_ge(xn_stored[i], g * 16 + 16)
                eng.wait_ge(tr_ready, (g * 2 + i) * 4 + 4)
                for k in range(GT):
                    last = eng.tensor_scalar(xno[i][:, k, :], xin[i][:, k, :], mv[:, k, 0:1], rs[:, k:k + 1],
                                             ALU.subtract, ALU.mult).then_inc(xn_ready, 1)

            with eng.Fori(0, NG // 2) as g:
                for i in range(2):
                    group(g, i)

        @block.gpsimd
        def _(eng):
            eng.memset(t.ident[:, :], 0.0).then_inc(consts, 1)
            eng.memset(t.tri[:, :], 1.0).then_inc(consts, 1)
            eng.memset(t.ones[:, :], 1.0).then_inc(consts, 1)
            eng.wait_ge(consts, 3)
            eng.affine_select(out=t.ident[:, :], in_=t.ident[:, :], compare_op=ALU.not_equal, fill=1.0,
                              base=0, pattern=[[-1, P]], channel_multiplier=1).then_inc(t.const_ready, 1)
            eng.affine_select(out=t.tri[:, :], in_=t.tri[:, :], compare_op=ALU.is_gt, fill=0.0,
                              base=0, pattern=[[1, P]], channel_multiplier=-1).then_inc(t.const_ready, 1)
            eng.iota(t.tok_id[:, :], pattern=[[P, TT]], base=0, channel_multiplier=1).then_inc(t.const_ready, 1)
            eng.iota(t.num_i[:, :], pattern=[[1, NK + 2]], base=0, channel_multiplier=0).then_inc(t.const_ready, 1)
            eng.memset(t.zero_ids[:, :], 0).then_inc(t.const_ready, 1)
            eng.memset(zero_row[:, :], 0.0).then_inc(t.const_ready, 1)
            eng.wait_ge(t.const_ready, 6)
            eng.dma_start(d["ids"].rearrange("(p w) o -> p (w o)", p=P), t.zero_ids[:, :]).then_inc(t.ids_zeroed, 16)
            for tile in range(TOKENS * TOP // SLOTS, NT):
                eng.wait_ge(xn_ready, (tile - TOKENS * TOP // SLOTS + 1) * GT)
                eng.dma_start(d["ys"][tile:tile + 1, :, :].rearrange("o (s p) n -> (o p) s n", p=P),
                              bcast(zero_row[:, :].unsqueeze(1), [P, SH, DM])).then_inc(ys_filled, 16)
            eng.wait_ge(ys_filled, (NT - TOKENS * TOP // SLOTS) * 16)

        @block.scalar
        def _(eng):
            def group(g, i):
                eng.wait_ge(var_ready, g * 2 + i + 1)
                eng.activation(sd[:, :], ve[:, :], ACT.Sqrt).then_inc(std_ready, 1)
                eng.wait_ge(xn_ready, (g * 2 + i + 1) * GT)
                eng.dma_start(xn_v[ds(g * 2 + i, 1)].rearrange("o p t c -> (o p) t c"), xno[i][:, :, :]).then_inc(xn_stored[i], 16)
                for c in range(DC):
                    eng.wait_ge(tr_ready, (g * 2 + i) * 4 + c + 1 + 8)
                    eng.activation(xnT[:, c, ds((g * 2 + i) * HALF, HALF)], ptr[c][:, :], ACT.Copy).then_inc(tr_copied, 1)
                eng.wait_ge(xnT_stored[i], g * 16 + 16)
                eng.wait_ge(tr_copied, (g * 2 + i) * 4 + 8)
                eng.dma_start(d["xnT"][ds(g, 1), :, :, i * HALF:(i + 1) * HALF].rearrange("o p c n -> (o p) c n"),
                              xnT[:, :, ds((g * 2 + i) * HALF, HALF)]).then_inc(xnT_stored[i], 16)

            def logits(g, i):
                eng.wait_ge(lgT_ready, g * 2 + i + 1)
                eng.activation(lgT[:, ds((g * 2 + i) * HALF, HALF)], plg[i][0:E, :], ACT.Copy).then_inc(lgT_copied, 1)

            one_behind(eng, group, logits)
            for i in range(2):
                eng.wait_ge(xn_stored[i], NG * 8 + 16)
                eng.wait_ge(xnT_stored[i], NG * 8 + 16)

        @block.tensor
        def _(eng):
            for i in range(2):
                eng.sem_inc(xn_stored[i], 16)
                eng.sem_inc(xnT_stored[i], 16)
            eng.sem_inc(tr_ready, 8)
            eng.sem_inc(lgT_copied, 2)
            eng.sem_inc(tr_copied, 4)
            eng.wait_ge(t.const_ready, 6)
            eng.wait_ge(t.gate_in, 16)

            def group(g, i):
                eng.wait_ge(xn_ready, (g * 2 + i + 1) * GT)
                for c in range(DC):
                    eng.wait_ge(tr_copied, (g * 2 + i) * 4 + c + 1)
                    for k in range(GT):
                        last = eng.transpose(ptr[c][:, k * P:(k + 1) * P], xno[i][:, k, c * P:(c + 1) * P], t.ident[:, :])
                    last.then_inc(tr_ready, 1)

            def logits(g, i):
                eng.wait_ge(tr_copied, (g * 2 + i) * 4 + 8)
                eng.wait_ge(lgT_copied, g * 2 + i + 1)
                for c in range(DC):
                    last = eng.matmul(plg[i][0:E, :], t.gate[:, c, :], xnT[:, c, ds((g * 2 + i) * HALF, HALF)],
                                      start=(c == 0), stop=(c == DC - 1))
                last.then_inc(lgT_ready, 1)

            one_behind(eng, group, logits)
            eng.wait_ge(lgT_copied, NG + 2)
            for i in range(TT):
                last = eng.transpose(t.ps_lg[:, i * E:(i + 1) * E], lgT[:, i * P:(i + 1) * P], t.ident[0:E, 0:E])
            last.then_inc(t.logits_ready, 1)


def mamba_front(nc, t, d):
    JOBS = 36
    RING = 6
    XC_X = 4
    with ExitStack() as ctx:
        sb = lambda n, s, dt=F32: ctx.enter_context(nc.sbuf_tensor(n, s, dt))
        sem = lambda n: ctx.enter_context(nc.semaphore(n))
        conv_hi = sb("conv_hi", [P, KC, CC, DIN], F32R)
        conv_lo = sb("conv_lo", [P, KC, CC, DIN], F32R)
        xc_hi = sb("xc_hi", [P, CC, SEQ + KC - 1], F32R)
        xc_lo = sb("xc_lo", [P, CC, SEQ + KC - 1], F32R)
        u2 = sb("u2", [P, CC, SEQ])
        din = sb("din", [P, SEQ])
        bcT = sb("bcT", [2 * NST, SEQ])
        th = [sb(f"th_r{i}", [P, HALF]) for i in range(2)]
        th2 = [sb(f"th_x{i}", [P, HALF]) for i in range(2)]
        srp = [sb(f"sr_piece{i}", [P, HALF]) for i in range(2)]
        xsp = [sb(f"xs_piece{i}", [P, HALF]) for i in range(2)]
        udp = [sb(f"ud_piece{i}", [P, HALF]) for i in range(2)]
        dlp = [sb(f"delta_piece{i}", [P, HALF]) for i in range(4)]
        dup = [sb(f"du_piece{i}", [P, HALF]) for i in range(4)]
        raw = dlp + dup
        ez = th + th2
        w1m = t.hot[:, :, :, :].rearrange("p k i e -> p (k i e)")
        ring = [ctx.enter_context(nc.psum_tensor(f"front{i}", [P, HALF], F32)) for i in range(RING)]
        ps_rt = ctx.enter_context(nc.psum_tensor("ps_rt", [P, HALF], F32))
        bank_full = sem("bank_full")
        act_freed = sem("act_freed")
        xh_ready = sem("xh_ready")
        xl_ready = sem("xl_ready")
        sp_sync = sem("sp_sync")
        cw_in = sem("cw_in")
        cw_lo = sem("cw_lo")
        cw_hi = sem("cw_hi")
        th_r = sem("th_r")
        sr_ready = sem("sr_ready")
        sr_out = [sem(f"sr_out{i}") for i in range(2)]
        xs_ready = sem("xs_ready")
        xs_out = [sem(f"xs_out{i}") for i in range(2)]
        th_x = sem("th_x")
        u_ready = sem("u_ready")
        ud_ready = sem("ud_ready")
        ud_out = [sem(f"ud_out{i}") for i in range(2)]
        bc_out = sem("bc_out")
        abs_ready = sem("abs_ready")
        exp_ready = sem("exp_ready")
        z_ready = sem("z_ready")
        ln_ready = sem("ln_ready")
        sp_step = sem("softplus_step")
        delta_ready = sem("delta_ready")
        delta_out = [sem(f"delta_out{i}") for i in range(4)]
        du_ready = sem("du_ready")
        du_out = [sem(f"du_out{i}") for i in range(4)]
        r_step = sem("route_step")
        r_exp = sem("route_exp")
        r_max = sem("route_max")
        r_mask = sem("route_mask")
        r_count = sem("route_count")
        slots_ready = sem("slots_ready")
        block = ctx.enter_context(nc.Block())

        pieces = [(c, h) for c in range(CC) for h in range(NH)]

        def row(name, b, c, h):
            return d[name][ds(b * PAIRS + c // 2, 1), :, c % 2, h * HALF:(h + 1) * HALF].rearrange("o p n -> (o p) n")

        @block.tensor
        def _(eng):
            eng.wait_ge(r_mask, 1)
            eng.matmul(ps_rt[:, 0:TT * E], t.tri[:, :], t.mask[:, :, :].rearrange("p i e -> p (i e)"), start=True, stop=True)
            eng.matmul(ps_rt[:, TT * E:2 * TT * E], t.ones[:, :], t.mask[:, :, :].rearrange("p i e -> p (i e)"),
                       start=False, stop=True, skip_group_check=True).then_inc(r_count, 1)
            eng.wait_ge(t.w_in, 48)
            with eng.Fori(0, BATCH) as b:
                q = 0
                owner = ([(xl_ready, 8, n + 1 + 8) for n in range(8)]
                         + [(sr_ready, 8, n + 1 + 2) for n in range(8)]
                         + [(xs_ready, 8, n + 1) for n in range(8)]
                         + [(act_freed, XC_X, n + 1) for n in range(XC_X)]
                         + [(z_ready, 8, n + 1 + 8) for n in range(8)])

                def bank():
                    s, per, n = owner[(q - RING) % JOBS]
                    eng.wait_ge(s, b * per + n - (per if q < RING else 0))
                    return ring[q % RING]

                eng.wait_ge(t.xn_in, b * 16 + 16)
                for m in range(2 * CC):
                    for h in range(NH):
                        o = bank()
                        for c in range(DC):
                            last = eng.matmul(o[:, :], t.W_in[:, c, m * P:(m + 1) * P],
                                              t.xn_b[:, c, h * HALF:(h + 1) * HALF], start=(c == 0), stop=(c == DC - 1))
                        last.then_inc(bank_full, 1)
                        q += 1
                for m, h in pieces:
                    o = bank()
                    if m == 0 and h == 0:
                        eng.wait_ge(cw_lo, KC * CC)
                        eng.wait_ge(xl_ready, b * 8 + 8 + 8)
                    for k in range(KC):
                        for c in range(CC):
                            for p, (w, x) in enumerate(((conv_hi, xc_hi), (conv_hi, xc_lo), (conv_lo, xc_hi))):
                                last = eng.matmul(o[:, :], w[:, k, c, m * P:(m + 1) * P],
                                                  x[:, c, h * HALF + k:h * HALF + k + HALF],
                                                  start=(k == 0 and c == 0 and p == 0),
                                                  stop=(k == KC - 1 and c == CC - 1 and p == 2))
                    last.then_inc(bank_full, 1)
                    q += 1
                for part in range(2):
                    for h in range(NH):
                        o = bank()
                        eng.wait_ge(u_ready, b * 8 + 8 + 2)
                        lo, hi = (0, DTR) if part == 0 else (DTR, NX)
                        for c in range(CC):
                            last = eng.matmul(o[0:hi - lo, :], t.W_x[:, c, lo:hi], u2[:, c, h * HALF:(h + 1) * HALF],
                                              start=(c == 0), stop=(c == CC - 1))
                        last.then_inc(bank_full, 1)
                        q += 1
                for m, h in pieces:
                    o = bank()
                    eng.wait_ge(act_freed, b * XC_X + 2)
                    eng.matmul(o[:, :], t.W_dt[:, m * P:(m + 1) * P], din[:, h * HALF:(h + 1) * HALF],
                               start=True, stop=True).then_inc(bank_full, 1)
                    q += 1

        @block.scalar
        def _(eng):
            eng.wait_ge(t.a_step, 1)
            eng.activation(t.A[:, :].rearrange("p (c n) -> p c n", n=NST), t.A_log[:, :, :], ACT.Exp).then_inc(t.a_step, 1)
            eng.wait_ge(t.a_step, 2)
            eng.activation(t.A[:, :], t.A[:, :], ACT.Copy, scale=-1.0).then_inc(t.a_step, 1)
            eng.wait_ge(r_max, 1)
            eng.activation(t.prob[:, :, :], t.prob[:, :, :], ACT.Exp).then_inc(r_exp, 1)
            for x in (xc_hi, xc_lo):
                eng.activation(x[:, :, 0:KC - 1], t.ones[:, 0:CC * (KC - 1)].rearrange("p (c k) -> p c k", k=KC - 1),
                               ACT.Copy, scale=0.0)
            for i in range(KC * CC):
                eng.wait_ge(cw_in, (i // len(raw) + 1) * len(raw) * 16)
                eng.activation(conv_hi[:, i // CC, i % CC, :], raw[i % len(raw)][:, :], ACT.Copy).then_inc(cw_hi, 1)
            with eng.Fori(0, BATCH) as b:
                q = 0
                for m, h in pieces:
                    eng.wait_ge(bank_full, b * JOBS + q + 1)
                    eng.activation(xc_hi[:, m, KC - 1 + h * HALF:KC - 1 + (h + 1) * HALF], ring[q % RING][:, :],
                                   ACT.Copy).then_inc(xh_ready, 1)
                    q += 1
                eng.wait_ge(delta_ready, b * 8 + 4)
                for i in range(8):
                    eng.wait_ge(bank_full, b * JOBS + q + 1)
                    eng.wait_ge(sr_ready, b * 8 + i + 1)
                    eng.activation(th[i % 2][:, :], ring[q % RING][:, :], ACT.Tanh, scale=0.5).then_inc(th_r, 1)
                    q += 1
                for i in range(8):
                    eng.wait_ge(xs_ready, b * 8 + i + 1)
                    eng.wait_ge(u_ready, b * 8 + i + 1)
                    eng.activation(th2[i % 2][:, :], xsp[i % 2][:, :], ACT.Tanh, scale=0.5).then_inc(th_x, 1)
                    q += 1
                for h in range(NH):
                    eng.wait_ge(bank_full, b * JOBS + q + 1)
                    eng.activation(din[:, h * HALF:(h + 1) * HALF], ring[q % RING][:, :], ACT.Copy,
                                   scale=0.5).then_inc(act_freed, 1)
                    q += 1
                for h in range(NH):
                    eng.wait_ge(bank_full, b * JOBS + q + 1)
                    eng.wait_ge(bc_out, b * 64 + 64)
                    eng.activation(bcT[:, h * HALF:(h + 1) * HALF], ring[q % RING][0:2 * NST, :], ACT.Copy,
                                   scale=0.5).then_inc(act_freed, 1)
                    q += 1
                for quad in range(0, 8, 4):
                    for i in range(quad, quad + 4):
                        m = pieces[i][0]
                        eng.wait_ge(bank_full, b * JOBS + q + 1)
                        eng.wait_ge(delta_ready, b * 8 + i + 1)
                        eng.activation(ez[i % 4][:, :], ring[q % RING][:, :], ACT.Abs,
                                       bias=t.b_dt[:, m:m + 1]).then_inc(abs_ready, 1)
                        q += 1
                    for i in range(quad, quad + 4):
                        eng.wait_ge(abs_ready, b * 8 + i + 1)
                        eng.activation(ez[i % 4][:, :], ez[i % 4][:, :], ACT.Exp, scale=-1.0).then_inc(exp_ready, 1)
                    for i in range(quad, quad + 4):
                        eng.wait_ge(exp_ready, b * 8 + i + 1)
                        eng.wait_ge(delta_out[i % 4], (b * 2 + i // 4 + 1) * 16)
                        eng.wait_ge(du_ready, b * 8 + i + 1)
                        eng.activation(dlp[i % 4][:, :], ez[i % 4][:, :], ACT.Ln, bias=1.0).then_inc(ln_ready, 1)

        @block.vector
        def _(eng):
            for out in (sr_out, xs_out, ud_out, delta_out, du_out):
                for o in out:
                    eng.sem_inc(o, 16)
            eng.sem_inc(bc_out, 64)
            eng.sem_inc(sr_ready, 2)
            eng.sem_inc(du_ready, 4)
            eng.sem_inc(u_ready, 2)
            eng.sem_inc(z_ready, 8)
            eng.sem_inc(xl_ready, 8)
            eng.sem_inc(delta_ready, 4)
            eng.wait_ge(t.small_in, 64)
            eng.tensor_scalar(t.A_log[:, :, :], t.A_log[:, :, :], LOG_MAX, None, ALU.min).then_inc(t.a_step, 1)
            step = [0]

            def link(ins):
                step[0] += 1
                ins.then_inc(r_step, 1)
                eng.wait_ge(r_step, step[0])

            link(eng.tensor_copy(t.prob[:, :, :].rearrange("p i e -> p (i e)"), t.ps_lg[:, 0:TT * E]))
            link(eng.tensor_reduce(t.red[:, :], t.prob[:, :, :], AX.X, ALU.max))
            eng.tensor_tensor(t.prob[:, :, :], t.prob[:, :, :], bcast(t.red[:, :].unsqueeze(2), [P, TT, E]),
                              ALU.subtract).then_inc(r_max, 1)
            eng.wait_ge(r_exp, 1)
            link(eng.tensor_reduce(t.red[:, :], t.prob[:, :, :], AX.X, ALU.add))
            link(eng.reciprocal(t.red2[:, :], t.red[:, :]))
            link(eng.tensor_tensor(t.prob[:, :, :], t.prob[:, :, :], bcast(t.red2[:, :].unsqueeze(2), [P, TT, E]), ALU.mult))
            for i in range(TT):
                eng.max(t.top[:, i, :], t.prob[:, i, :]).then_inc(r_step, 1)
            step[0] += TT
            eng.wait_ge(r_step, step[0])
            for i in range(TT):
                eng.max_index(t.topi[:, i, :], t.top[:, i, :], t.prob[:, i, :]).then_inc(r_step, 1)
            step[0] += TT
            eng.wait_ge(r_step, step[0])
            link(eng.tensor_tensor(t.red[:, :], t.top[:, :, 0], t.top[:, :, 1], ALU.add))
            link(eng.reciprocal(t.red2[:, :], t.red[:, :]))
            for k in range(TOP):
                link(eng.tensor_tensor(t.wgt[:, k, :], t.top[:, :, k], t.red2[:, :], ALU.mult))
                link(eng.tensor_copy(t.topf[:, k, :], t.topi[:, :, k]))
            eng.wait_ge(t.const_ready, 6)
            link(eng.tensor_copy(t.num[:, :], t.num_i[:, :]))
            for k in range(TOP):
                link(eng.tensor_tensor(t.hot[:, k, :, :], bcast(t.num[:, 0:E].unsqueeze(1), [P, TT, E]),
                                       bcast(t.topf[:, k, :].unsqueeze(2), [P, TT, E]), ALU.is_equal))
            eng.tensor_tensor(t.mask[:, :, :], t.hot[:, 0, :, :], t.hot[:, 1, :, :], ALU.add).then_inc(r_mask, 1)
            for i in range(KC * CC):
                eng.wait_ge(cw_hi, i + 1)
                eng.tensor_tensor(conv_lo[:, i // CC, i % CC, :], raw[i % len(raw)][:, :],
                                  conv_hi[:, i // CC, i % CC, :].bitcast(F32), ALU.subtract).then_inc(cw_lo, 1)
            eng.wait_ge(r_count, 1)
            rank = ps_rt[:, 0:TT * E].rearrange("p (i e) -> p i e", e=E)
            total = ps_rt[:, TT * E:2 * TT * E].rearrange("p (i e) -> p e i", e=E)
            link(eng.tensor_copy(t.tot[:, :, :], total))
            for e in range(E):
                link(eng.tensor_tensor_scan(t.cum[:, e, :], t.ones[:, 0:TT], t.tot[:, e, :], 0.0, ALU.mult, ALU.add))
            link(eng.tensor_scalar(t.cnt_i[:, :], t.cum[:, :, TT - 1], float(SLOTS - 1), None, ALU.add))
            link(eng.tensor_scalar(t.cnt_i[:, :], t.cnt_i[:, :], SHIFT, None, ALU.arith_shift_right))
            link(eng.tensor_copy(t.ntile[:, :], t.cnt_i[:, :]))
            link(eng.tensor_tensor_scan(t.last_tile[:, :], t.ones[:, 0:E], t.ntile[:, :], 0.0, ALU.mult, ALU.add))
            link(eng.tensor_tensor(t.base[:, :], t.last_tile[:, :], t.ntile[:, :], ALU.subtract))
            link(eng.tensor_scalar(t.base[:, :], t.base[:, :], float(SLOTS), None, ALU.mult))
            link(eng.tensor_tensor(t.cum[:, :, :], t.cum[:, :, :], t.tot[:, :, :], ALU.subtract))
            link(eng.tensor_tensor(t.cum[:, :, :], t.cum[:, :, :], bcast(t.base[:, :].unsqueeze(2), [P, E, TT]), ALU.add))
            link(eng.tensor_tensor(t.prob[:, :, :], t.cum[:, :, :].rearrange("p e i -> p i e"), rank, ALU.add))
            for k in range(TOP):
                link(eng.tensor_tensor(t.hot[:, k, :, :], t.hot[:, k, :, :], t.prob[:, :, :], ALU.mult))
                link(eng.tensor_reduce(t.topf[:, k, :], t.hot[:, k, :, :], AX.X, ALU.add))
            link(eng.tensor_copy(t.slot[:, :, :], t.topf[:, :, :]))
            link(eng.tensor_scalar(t.place[:, :, :], t.slot[:, :, :], P - 1, None, ALU.bitwise_and))
            link(eng.tensor_scalar(t.place2[:, :, :], t.slot[:, :, :], 7, None, ALU.logical_shift_right))
            eng.scalar_tensor_tensor(out=t.place[:, :, :], in0=t.place[:, :, :], scalar=float(IDW),
                                     in1=t.place2[:, :, :], op0=ALU.mult, op1=ALU.add).then_inc(slots_ready, 1)
            step_no = t.num[:, :]
            last2, cmp_buf = t.base[:, :], u2[:, 0, 0:(NK + 2) * E].rearrange("p (k e) -> p k e", e=E)
            expert, first, count, within, half, live, tmp, fresh = (u2[:, 1, i * 128:i * 128 + NK + 2] for i in range(8))
            by_step = lambda v, n: bcast(v.unsqueeze(2), [P, NK + 2, n])
            by_expert = lambda v, n: bcast(v[:, 0:n].unsqueeze(1), [P, NK + 2, n])
            past = cmp_buf[:, :, 0:E - 1]
            link(eng.tensor_scalar(last2, t.last_tile[:, :], 2.0, None, ALU.mult))
            link(eng.tensor_tensor(past, by_step(step_no, E - 1), by_expert(last2, E - 1), ALU.is_ge))
            link(eng.tensor_reduce(expert, past, AX.X, ALU.add))
            link(eng.tensor_tensor(past, past, by_expert(t.ntile[:, :], E - 1), ALU.mult))
            link(eng.tensor_reduce(first, past, AX.X, ALU.add))
            link(eng.tensor_tensor(cmp_buf, by_expert(t.num[:, :], E), by_step(expert, E), ALU.is_equal))
            link(eng.tensor_tensor(cmp_buf, cmp_buf, by_expert(t.ntile[:, :], E), ALU.mult))
            link(eng.tensor_reduce(count, cmp_buf, AX.X, ALU.add))
            link(eng.scalar_tensor_tensor(out=within, in0=first, scalar=-2.0, in1=step_no, op0=ALU.mult, op1=ALU.add))
            link(eng.tensor_tensor(half, within, count, ALU.is_ge))
            link(eng.tensor_tensor(live, step_no, bcast(last2[:, E - 1:E], [P, NK + 2]), ALU.is_lt))
            link(eng.tensor_tensor(tmp, within, count, ALU.is_equal))
            link(eng.scalar_tensor_tensor(out=tmp, in0=within, scalar=0.0, in1=tmp, op0=ALU.is_equal, op1=ALU.add))
            link(eng.tensor_tensor(fresh, tmp, live, ALU.mult))
            link(eng.tensor_copy(t.meta[:, 1, :], fresh))
            link(eng.scalar_tensor_tensor(out=fresh, in0=live, scalar=-2.0, in1=fresh, op0=ALU.mult, op1=ALU.add))
            link(eng.tensor_scalar(t.meta[:, 5, :], fresh, 2.0, None, ALU.add))
            link(eng.tensor_tensor(tmp, half, count, ALU.mult))
            link(eng.tensor_tensor(within, within, tmp, ALU.subtract))
            link(eng.scalar_tensor_tensor(out=within, in0=within, scalar=float(1 - NT), in1=first, op0=ALU.add, op1=ALU.add))
            link(eng.tensor_tensor(within, within, live, ALU.mult))
            link(eng.tensor_scalar(t.meta[:, 4, :], within, float(NT - 1), None, ALU.add))
            link(eng.tensor_copy(t.meta[:, 0, :], expert))
            link(eng.tensor_copy(t.meta[:, 2, :], live))
            link(eng.tensor_tensor(t.meta[:, 3, :], half, live, ALU.mult))

            eng.wait_ge(t.small_in, 64)
            with eng.Fori(0, BATCH) as b:
                for i, (m, h) in enumerate(pieces):
                    eng.wait_ge(xh_ready, b * 8 + i + 1)
                    at = KC - 1 + h * HALF
                    eng.tensor_tensor(xc_lo[:, m, at:at + HALF], ring[i % RING][:, :], xc_hi[:, m, at:at + HALF].bitcast(F32),
                                      ALU.subtract).then_inc(xl_ready, 1)
                q = 8
                for i in range(8):
                    eng.wait_ge(th_r, b * 8 + i + 1)
                    eng.wait_ge(sr_out[i % 2], (b * 4 + i // 2 + 1) * 16)
                    eng.scalar_tensor_tensor(out=srp[i % 2][:, :], in0=th[i % 2][:, :], scalar=1.0,
                                             in1=ring[q % RING][:, :], op0=ALU.add, op1=ALU.mult).then_inc(sr_ready, 1)
                    q += 1

                def silu(i):
                    m, h = pieces[i]
                    eng.wait_ge(th_x, b * 8 + i + 1)
                    eng.scalar_tensor_tensor(out=u2[:, m, h * HALF:(h + 1) * HALF], in0=th2[i % 2][:, :], scalar=1.0,
                                             in1=xsp[i % 2][:, :], op0=ALU.add, op1=ALU.mult).then_inc(u_ready, 1)
                    eng.wait_ge(u_ready, b * 8 + i + 1 + 2)
                    eng.wait_ge(ud_out[i % 2], (b * 4 + i // 2 + 1) * 16)
                    eng.tensor_scalar(udp[i % 2][:, :], u2[:, m, h * HALF:(h + 1) * HALF], t.D[:, m:m + 1], 0.5,
                                      ALU.mult, ALU.mult).then_inc(ud_ready, 1)

                for i, (m, h) in enumerate(pieces):
                    eng.wait_ge(bank_full, b * JOBS + q + 1)
                    eng.wait_ge(xs_out[i % 2], (b * 4 + i // 2 + 1) * 16)
                    eng.wait_ge(u_ready, b * 8 + i + 1)
                    eng.tensor_scalar(xsp[i % 2][:, :], ring[q % RING][:, :], t.conv_b[:, m:m + 1], None,
                                      ALU.add).then_inc(xs_ready, 1)
                    if i >= 1:
                        silu(i - 1)
                    q += 1
                silu(7)
                q = JOBS - 8
                for quad in range(0, 8, 4):
                    for i in range(quad, quad + 4):
                        m = pieces[i][0]
                        eng.wait_ge(abs_ready, b * 8 + i + 1)
                        eng.wait_ge(du_out[i % 4], (b * 2 + i // 4 + 1) * 16)
                        eng.tensor_scalar(dup[i % 4][:, :], ring[q % RING][:, :], t.b_dt[:, m:m + 1], 0.0,
                                          ALU.add, ALU.max).then_inc(z_ready, 1)
                        q += 1
                    for i in range(quad, quad + 4):
                        m, h = pieces[i]
                        at = b * 24 + i * 3
                        e, dl, z = ez[i % 4], dlp[i % 4], dup[i % 4]
                        eng.wait_ge(exp_ready, b * 8 + i + 1)
                        eng.tensor_scalar(w1m, e[:, :], 1.0, -1.0, ALU.add, ALU.add).then_inc(sp_step, 1)
                        eng.wait_ge(ln_ready, b * 8 + i + 1)
                        eng.wait_ge(sp_step, at + 1)
                        eng.tensor_tensor(e[:, :], e[:, :], w1m, ALU.subtract).then_inc(sp_step, 1)
                        eng.wait_ge(sp_step, at + 2)
                        eng.tensor_tensor(e[:, :], e[:, :], dl[:, :], ALU.add).then_inc(sp_step, 1)
                        eng.wait_ge(sp_step, at + 3)
                        eng.wait_ge(z_ready, b * 8 + i + 1 + 8)
                        eng.tensor_tensor(dl[:, :], e[:, :], z[:, :], ALU.add).then_inc(delta_ready, 1)
                        eng.wait_ge(delta_ready, b * 8 + i + 1 + 4)
                        eng.scalar_tensor_tensor(out=z[:, :], in0=dl[:, :], scalar=0.5,
                                                 in1=u2[:, m, h * HALF:(h + 1) * HALF], op0=ALU.mult,
                                                 op1=ALU.mult).then_inc(du_ready, 1)

        @block.sync
        def _(eng):
            for i in range(KC * CC):
                if i >= len(raw):
                    eng.wait_ge(cw_lo, i // len(raw) * len(raw))
                eng.dma_start(raw[i % len(raw)][:, :], d["conv_w"][i // CC, i % CC * P:(i % CC + 1) * P, :]).then_inc(cw_in, 16)
            with eng.Fori(0, BATCH) as b:
                for i, (m, h) in enumerate(pieces):
                    eng.wait_ge(sr_ready, b * 8 + i + 3)
                    eng.dma_start(row("sr", b, m, h), srp[i % 2][:, :]).then_inc(sr_out[i % 2], 16)
                for i, (m, h) in enumerate(pieces):
                    eng.wait_ge(xs_ready, b * 8 + i + 1)
                    eng.dma_start(row("xs", b, m, h), xsp[i % 2][:, :]).then_inc(xs_out[i % 2], 16)
                    if i >= 1:
                        eng.wait_ge(ud_ready, b * 8 + i)
                        eng.dma_start(row("ud", b, *pieces[i - 1]), udp[(i - 1) % 2][:, :]).then_inc(ud_out[(i - 1) % 2], 16)
                eng.wait_ge(bank_full, b * JOBS + 16)
                eng.sem_inc(sp_sync, 1)
                with eng.If(b < BATCH - 1):
                    eng.dma_start(t.xn_b[:, :, :], d["xnT"][ds(b + 1, 1), :, :, :].rearrange("o p c n -> (o p) c n")).then_inc(t.xn_in, 16)
                eng.wait_ge(ud_ready, b * 8 + 8)
                eng.dma_start(row("ud", b, *pieces[7]), udp[1][:, :]).then_inc(ud_out[1], 16)
                eng.wait_ge(act_freed, b * XC_X + XC_X)
                for r in range(PAIRS):
                    for s in range(2):
                        eng.dma_start(d["bc"][ds((b * PAIRS + r) * NST, NST), s, :],
                                      bcT[s * NST:(s + 1) * NST, :]).then_inc(bc_out, 16)
                for i, (m, h) in enumerate(pieces):
                    eng.wait_ge(delta_ready, b * 8 + i + 1 + 4)
                    eng.dma_start(row("delta", b, m, h), dlp[i % 4][:, :]).then_inc(delta_out[i % 4], 16)
                    eng.wait_ge(du_ready, b * 8 + i + 5)
                    eng.dma_start(row("du", b, m, h), dup[i % 4][:, :]).then_inc(du_out[i % 4], 16)
            eng.dma_start(d["bc"][ROWS * NST:ROWS * NST + 2, 0, :], bcT[0:2, :]).then_inc(bc_out, 16)
            eng.dma_start(d["bc"][ROWS * NST:ROWS * NST + 2, 1, :], bcT[2:4, :]).then_inc(bc_out, 16)
            for out in (sr_out, xs_out, ud_out, delta_out, du_out):
                for o in out:
                    eng.wait_ge(o, BATCH * 8 * 16 // len(out) + 16)
            eng.wait_ge(bc_out, BATCH * 64 + 96)

        @block.gpsimd
        def _(eng):
            eng.wait_ge(slots_ready, 1)
            eng.wait_ge(t.ids_zeroed, 16)
            n = 0
            for k in range(TOP):
                for i in range(TT):
                    eng.indirect_dma_start(out=d["ids"], out_offset=bass.IndirectOffsetOnAxis(ap=t.place[:, k, i:i + 1], axis=0),
                                           in_=t.tok_id[:, i:i + 1], in_offset=None).then_inc(t.ids_written, 16)
                    n += 16
            eng.wait_ge(t.ids_written, n)
            eng.dma_start(t.ids[:, :], d["ids"].rearrange("(p w) o -> p (w o)", p=P)).then_inc(t.ids_loaded, 16)
            eng.wait_ge(t.ids_loaded, 16)


def experts_and_scan(nc, t, d):
    LAG = 3
    ORDER = [("up", 3), ("down", 0), ("up", 4), ("down", 1), ("turn", 0), ("up", 5), ("down", 2), ("up", 6), ("down", 3),
             ("down", 4), ("next up", 0), ("down", 5), ("next up", 1), ("down", 6), ("next up", 2)]
    assert sorted(f for what, f in ORDER if what == "down") == list(range(NF)) and LAG == 3
    HR = 4
    RING3 = [0, 1, 2, 0, 1, 2, 1]
    RING4 = [f % HR for f in range(NF)]
    CHUNK = 3 * DM
    AHEAD = 3
    SCAN = [("p", 0, 0), ("s", 0, 0), ("s", 0, 1), ("p", 1, 0), ("q", 0, 0), ("s", 1, 0), ("r", 0, 0), ("s", 1, 1),
            ("q", 1, 0), ("r", 1, 0)]
    NS = len(SCAN)
    STEPS = [2, 2, 2, 1, 1, 1, 1]
    assert sum(STEPS) == NS and len(STEPS) == NF
    done = {key: n + 1 for n, key in enumerate(SCAN)}
    with ExitStack() as ctx:
        sb = lambda n, s, dt=F32: ctx.enter_context(nc.sbuf_tensor(n, s, dt))
        sem = lambda n: ctx.enter_context(nc.semaphore(n))
        ps = lambda n: ctx.enter_context(nc.psum_tensor(n, [P, HALF], F32))
        raw = [sb(f"w_raw{i}", [P, CHUNK]) for i in range(3)]
        whi = [sb(f"w_hi{f}", [P, CHUNK], F32R) for f in range(NF)]
        wlo = [sb(f"w_lo{f}", [P, CHUNK], F32R) for f in range(NF)]
        delta = sb("delta_b", [P, 2, SEQ])
        du = sb("du_b", [P, 2, SEQ])
        y = sb("y_b", [P, 2, SEQ])
        dA = [sb(f"dA{i}", [P, 2, SEQ]) for i in range(2)]
        hs = [sb(f"h_states{i}", [P, 2, SEQ]) for i in range(2)]
        bc = [sb(f"bc{i}", [P, 2, SEQ]) for i in range(2)]
        xg = sb("xg", [P, SH, DM])
        xhi = sb("x_hi", [P, DC, SLOTS], F32R)
        xlo = sb("x_lo", [P, DC, SLOTS], F32R)
        hid = [sb(f"hidden{i}", [P, SLOTS]) for i in range(3)]
        hhi = [sb(f"h_hi{i}", [P, SLOTS], F32R) for i in range(HR)]
        hlo = [sb(f"h_lo{i}", [P, SLOTS], F32R) for i in range(HR)]
        og = sb("og", [P, SH, DM])
        idc = sb("ids_now", [P, SH], U32)
        warm = sb("table_warm", [P, 1])
        ph = [ps(f"ph{i}") for i in range(HR)]
        po = [ps(f"po{i}") for i in range(SH)]
        px = [ps(f"px{i}") for i in range(2)]
        raw_in = [sem(f"raw_in{f}") for f in range(NF)]
        whi_done = sem("whi_done")
        w_ready = sem("w_ready")
        xg_in = sem("xg_in")
        xg_turned = sem("xg_turned")
        xhi_ready = sem("xhi_ready")
        xT_ready = sem("xT_ready")
        up_done = sem("up_done")
        tanh_done = sem("tanh_done")
        gate_step = sem("gate_step")
        val_done = sem("val_done")
        hhi_done = sem("hhi_done")
        hid_done = sem("hid_done")
        down_done = sem("down_done")
        out_copied = sem("out_copied")
        og_free = sem("og_free")
        ys_out = sem("ys_out")
        ids_now = sem("ids_now_ready")
        row_in = sem("row_in")
        y_in = sem("y_in")
        sr_in = sem("sr_in")
        bc_in = [sem(f"bc_in{i}") for i in range(2)]
        dA_ready = sem("dA_ready")
        scan_step = sem("scan_step")
        y_final = sem("y_final")
        y_out = sem("y_out")
        act_sync = sem("act_sync")
        pool_sync = sem("pool_sync")
        block = ctx.enter_context(nc.Block())

        def before(f, ring):
            same = [g for g in range(f) if ring[g] == ring[f]]
            if same:
                return same[-1] + NF
            return max(g for g in range(NF) if ring[g] == ring[f])

        def meta(eng, what, k, most):
            return eng.value_load(t.meta[0:1, what, ds(k, 1)], min_val=0, max_val=most)

        def all_steps(eng, body, between=None):
            with eng.Fori(0, BATCH) as b:
                with eng.Fori(0, PAIRS) as r:
                    row = b * PAIRS + r
                    with eng.Fori(0, GROUP - 1) as j:
                        body(row * GROUP + j, (row, r, j), False, False)
                    body(row * GROUP + GROUP - 1, None, row, False)
            if between:
                between()
            with eng.Fori(0, PLAIN) as j:
                live = meta(eng, 2, ROWS * GROUP + j, 1)
                with eng.If(live > 0):
                    body(ROWS * GROUP + j, None, False, True)

        @block.sync
        def _(eng):
            def chunk(e, h, f):
                dst = raw[RING3[f]]
                at = h * HM + f * P
                for n, name in enumerate(("w1", "w3")):
                    eng.dma_start(dst[:, n * DM:(n + 1) * DM].rearrange("p (k m) -> p k m", m=P),
                                  d[name][ds(e, 1), :, ds(at, P)].rearrange("o (k p) m -> (o p) k m", p=P)).then_inc(raw_in[f], 16)
                eng.dma_start(dst[:, 2 * DM:3 * DM], d["w2"][ds(e, 1), ds(at, P), :].rearrange("o p n -> (o p) n")).then_inc(raw_in[f], 16)

            def weights(k, chunks):
                again = meta(eng, 1, k, 2)
                for f in chunks:
                    prev = before(f, RING3)
                    free = (k * NF + prev - NF if prev >= NF else (k - 1) * NF + prev) + 1 + 1
                    with eng.If(again > 0):
                        e = meta(eng, 0, k, E - 1)
                        h = meta(eng, 3, k, 1)
                        eng.wait_ge(w_ready, free)
                        chunk(e, h, f)
                    with eng.Else():
                        eng.wait_ge(w_ready, free)
                        eng.sem_inc(raw_in[f], 48)

            def bc_load(m, i):
                eng.dma_start(bc[i][:, :, :].rearrange("p s n -> p (s n)"),
                              bcast(d["bc"][ds(m, 1), :, :].rearrange("o s n -> o (s n)"), [P, 2 * SEQ])).then_inc(bc_in[i], 16)

            def body(k, scan, final, plain):
                weights(k, [NF - 1])
                if scan is None:
                    weights(k + 1, range(NF - 1))
                    return
                row, r, j = scan
                at = (row * (GROUP - 1) + j) * NS + NS
                for chunks, i in (((0, 1, 2), 0), ((3, 4), 1), ((5,), None)):
                    if i is not None:
                        weights(k + 1, chunks)
                        eng.wait_ge(scan_step, at + done["q", i, 0])
                        bc_load(row * NST + j * 2 + 2 + i, i)
                    else:
                        weights(k + 1, chunks)

            e0 = meta(eng, 0, 0, E - 1)
            for f in range(NF - 1):
                if f >= 3:
                    eng.wait_ge(w_ready, before(f, RING3) - NF + 1 + 1)
                chunk(e0, 0, f)
                if f == 2:
                    for i in range(2):
                        bc_load(i, i)
            all_steps(eng, body)
            for i in range(2):
                eng.wait_ge(bc_in[i], 16 * (ROWS * NST // 2 + 1))

        @block.gpsimd
        def _(eng):
            def gather(k):
                tile = meta(eng, 4, k, NT - 1)
                eng.tensor_copy(idc[:, :], t.ids[:, ds(tile * SH, SH)]).then_inc(ids_now, 1)
                eng.wait_ge(ids_now, k + 1)
                eng.sem_inc(pool_sync, 1)
                for s in range(SH):
                    eng.indirect_dma_start(out=xg[:, s, :], out_offset=None, in_=d["xn"],
                                           in_offset=bass.IndirectOffsetOnAxis(ap=idc[:, s:s + 1], axis=0)).then_inc(xg_in, 16)

            def outputs(k):
                tile = meta(eng, 4, k, NT - 1)
                half = meta(eng, 3, k, 1)
                eng.wait_ge(out_copied, k * SH + 2 * SH)
                eng.sem_inc(pool_sync, 1)
                out = d["ys"][ds(tile, 1), :, :].rearrange("o (s p) n -> (o p) s n", p=P)
                with eng.If(half > 0):
                    eng.dma_start(out, og[:, :, :], accum_op=ALU.add).then_inc(ys_out, 16)
                with eng.Else():
                    eng.dma_start(out, og[:, :, :]).then_inc(ys_out, 16)
                eng.wait_ge(ys_out, k * 16 + 16)
                eng.sem_inc(og_free, 1)

            def load(buf, name, row):
                return eng.dma_start(buf[:, :, :], d[name][ds(row, 1), :, :, :].rearrange("o p c n -> (o p) c n"))

            def body(k, scan, final, plain):
                if final is not False:
                    eng.wait_ge(scan_step, (final + 1) * (GROUP - 1) * NS + NS)
                    eng.sem_inc(pool_sync, 1)
                    load(dA[0], "sr", final).then_inc(sr_in, 16)
                    with eng.If(final < ROWS - 1):
                        load(delta, "delta", final + 1).then_inc(row_in, 16)
                        load(du, "du", final + 1).then_inc(row_in, 16)
                eng.wait_ge(xg_turned, k + 2)
                eng.sem_inc(pool_sync, 1)
                gather(k + 2)
                if final is not False:
                    eng.wait_ge(y_final, final + 2)
                    eng.sem_inc(pool_sync, 1)
                    eng.dma_start(d["yg"][ds(final, 1), :, :, :].rearrange("o p c n -> (o p) c n"), y[:, :, :]).then_inc(y_out, 16)
                    eng.wait_ge(y_out, final * 16 + 16)
                    eng.sem_inc(pool_sync, 1)
                    with eng.If(final < ROWS - 1):
                        load(y, "ud", final + 1).then_inc(y_in, 16)
                outputs(k)
                if plain:
                    eng.wait_ge(xg_in, k * 32 + 96)
                    eng.sem_inc(pool_sync, 1)

            gather(0)
            load(delta, "delta", 0).then_inc(row_in, 16)
            load(du, "du", 0).then_inc(row_in, 16)
            load(y, "ud", 0).then_inc(y_in, 16)
            eng.wait_ge(xg_turned, 1)
            eng.sem_inc(pool_sync, 1)
            gather(1)
            all_steps(eng, body)
            eng.wait_ge(xg_in, (ROWS * GROUP + 2) * 32)

        @block.tensor
        def _(eng):
            eng.sem_inc(down_done, NF)

            def turn(k):
                eng.wait_ge(xg_in, k * 32 + 32)
                for c in range(DC):
                    for s in range(SH):
                        last = eng.transpose(px[c // 2][:, (c % 2) * SLOTS + s * P:(c % 2) * SLOTS + (s + 1) * P],
                                             xg[:, s, c * P:(c + 1) * P], t.ident[:, :])
                last.then_inc(xg_turned, 1)

            def up_waits(k, f):
                if f == 0:
                    eng.wait_ge(xT_ready, k * 2 + 1)
                eng.wait_ge(w_ready, k * NF + f + 1 + 1)
                eng.wait_ge(val_done, k * NF + before(f, RING4) + 1)

            def up(k, f):
                up_waits(k, f)
                for c in range(DC):
                    if f == 0 and c == DC // 2:
                        eng.wait_ge(xT_ready, k * 2 + 2)
                    for n in range(2):
                        at = n * DM + c * P
                        for p, (w, x) in enumerate(((whi, xhi), (whi, xlo), (wlo, xhi))):
                            last = eng.matmul(ph[RING4[f]][:, n * SLOTS:(n + 1) * SLOTS], w[f][:, at:at + P], x[:, c, :],
                                              start=(n == 0 and c == 0 and p == 0), stop=(c == DC - 1 and p == 2),
                                              skip_group_check=True)
                last.then_inc(up_done, 1)

            def down_waits(k, f):
                eng.wait_ge(hid_done, k * NF + NF + f + 1)
                if f == 0:
                    eng.wait_ge(out_copied, k * SH + SH)

            def down(k, f):
                down_waits(k, f)
                for s in range(SH):
                    for p, (h, w) in enumerate(((hhi, whi), (hhi, wlo), (hlo, whi))):
                        last = eng.matmul(po[s][:, :], h[RING4[f]][:, s * P:(s + 1) * P], w[f][:, 2 * DM:3 * DM],
                                          start=(f == 0 and p == 0), stop=(f == NF - 1 and p == 2))
                last.then_inc(down_done, 1)

            def work(k):
                for what, f in ORDER:
                    if what == "up":
                        up(k, f)
                    elif what == "next up":
                        up(k + 1, f)
                    elif what == "down":
                        down(k, f)
                    else:
                        turn(k + 1)

            def body(k, scan, final, plain):
                if plain:
                    work(k)
                    return
                live = meta(eng, 2, k, 1)
                with eng.If(live > 0):
                    work(k)
                with eng.Else():
                    eng.drain()
                    for what, f in ORDER:
                        if what == "turn":
                            eng.wait_ge(xg_in, k * 32 + 64)
                            eng.sem_inc(xg_turned, 1)
                        elif what == "down":
                            down_waits(k, f)
                            eng.sem_inc(down_done, 1)
                        else:
                            up_waits(k if what == "up" else k + 1, f)
                            if f == 0:
                                eng.wait_ge(xT_ready, k * 2 + 4)
                            eng.sem_inc(up_done, 1)

            turn(0)
            for f in range(LAG):
                up(0, f)
            all_steps(eng, body)

        @block.scalar
        def _(eng):
            def split(k, f):
                eng.wait_ge(raw_in[f], k * 48 + 48)
                eng.wait_ge(down_done, k * NF + f + 1)
                eng.activation(whi[f][:, :], raw[RING3[f]][:, :], ACT.Copy).then_inc(whi_done, 1)

            def kept(k, f, count):
                eng.wait_ge(whi_done, k * NF + f + 1)
                eng.sem_inc(whi_done, count)

            def turned(k):
                eng.wait_ge(xg_turned, k + 1)
                eng.wait_ge(up_done, k * NF + 1)
                for i in range(2):
                    eng.activation(xhi[:, 2 * i:2 * i + 2, :].rearrange("p c n -> p (c n)"), px[i][:, :],
                                   ACT.Copy).then_inc(xhi_ready, 1)

            def tanh(k, f):
                eng.wait_ge(up_done, k * NF + f + 1 + 1)
                eng.wait_ge(hid_done, k * NF + before(f, RING3) + 1)
                eng.activation(hid[RING3[f]][:, :], ph[RING4[f]][:, 0:SLOTS], ACT.Tanh, scale=0.5).then_inc(tanh_done, 1)

            def hidden_hi(k, f):
                eng.wait_ge(val_done, k * NF + NF + f + 1)
                eng.wait_ge(down_done, k * NF + before(f, RING4) + 1)
                eng.activation(hhi[RING4[f]][:, :], hid[RING3[f]][:, :], ACT.Copy).then_inc(hhi_done, 1)

            def decay(scan, i, c):
                row, r, j = scan
                at = (row * (GROUP - 1) + j) * NS
                eng.wait_ge(scan_step, at + done["s", i, c])
                if i == 0 and c == 0:
                    eng.sem_inc(act_sync, 1)
                    eng.wait_ge(row_in, row * 32 + 32)
                    eng.sem_inc(act_sync, 1)
                    eng.wait_ge(y_final, row + 1)
                eng.sem_inc(act_sync, 1)
                eng.activation(dA[i][:, c, :], delta[:, c, :], ACT.Exp,
                               scale=t.A[:, ds((r * 2 + c) * NST + j * 2 + i, 1)]).then_inc(dA_ready, 1)

            def outputs(k):
                eng.wait_ge(down_done, k * NF + 2 * NF)
                eng.wait_ge(og_free, k + 1)
                for s in range(SH):
                    eng.activation(og[:, s, :], po[s][:, :], ACT.Copy).then_inc(out_copied, 1)

            WHEN = {2: (1, 0), 3: (1, 1)}

            def body(k, scan, final, plain):
                def chunks(fs, fresh):
                    for f in fs:
                        if f == NF - 1:
                            turned(k + 1)
                        if 1 < f < NF:
                            tanh(k, f)
                        elif f == NF:
                            tanh(k + 1, 0)
                        if fresh:
                            if f + AHEAD < NF:
                                split(k, f + AHEAD)
                            else:
                                split(k + 1, f + AHEAD - NF)
                        if scan is not None and f in WHEN:
                            decay(scan, *WHEN[f])
                        if f < NF:
                            hidden_hi(k, f)

                def work(fresh):
                    hidden_hi(k, 0)
                    tanh(k, 1)
                    if not plain:
                        with eng.If(k > 0):
                            outputs(k - 1)
                    if not fresh:
                        kept(k, AHEAD + 1, NF - AHEAD - 1)
                    chunks(range(1, NF - AHEAD), fresh)
                    then = meta(eng, 1, k + 1, 2)
                    with eng.If(then > 0):
                        chunks(range(NF - AHEAD, NF + 1), True)
                    with eng.Else():
                        kept(k + 1, 0, AHEAD + 1)
                        chunks(range(NF - AHEAD, NF + 1), False)

                def no_rows():
                    outputs(k - 1)
                    eng.wait_ge(tanh_done, k * NF + 1)
                    eng.wait_ge(xhi_ready, k * 2 + 2)
                    eng.sem_inc(tanh_done, NF)
                    eng.sem_inc(hhi_done, NF)
                    eng.sem_inc(xhi_ready, 2)
                    kept(k, AHEAD + 1, NF - AHEAD - 1)
                    kept(k + 1, 0, AHEAD + 1)
                    if scan is not None:
                        for f in WHEN:
                            decay(scan, *WHEN[f])

                kind = meta(eng, 5, k, 2)
                if scan is not None:
                    decay(scan, 0, 0)
                    decay(scan, 0, 1)
                with eng.If(kind > 0):
                    if plain:
                        work(True)
                    else:
                        with eng.If(kind > 1):
                            no_rows()
                        with eng.Else():
                            work(True)
                with eng.Else():
                    work(False)
                if plain:
                    outputs(k)

            eng.activation(warm[:, :], t.A[:, 0:1], ACT.Exp)
            turned(0)
            for f in range(AHEAD):
                split(0, f)
            tanh(0, 0)
            split(0, AHEAD)
            all_steps(eng, body, between=lambda: outputs(ROWS * GROUP - 1))

        @block.vector
        def _(eng):
            eng.sem_inc(val_done, NF)
            eng.sem_inc(hid_done, NF)
            eng.sem_inc(scan_step, NS)
            eng.sem_inc(out_copied, SH)
            eng.sem_inc(og_free, 1)
            eng.sem_inc(y_final, 1)
            eng.sem_inc(up_done, 1)
            eng.sem_inc(whi_done, 1)
            eng.sem_inc(w_ready, 1)

            def split(k, f):
                eng.wait_ge(whi_done, k * NF + f + 1 + 1)
                eng.tensor_tensor(wlo[f][:, :], raw[RING3[f]][:, :], whi[f][:, :].bitcast(F32), ALU.subtract).then_inc(w_ready, 1)

            def kept(k, f, count):
                eng.wait_ge(w_ready, k * NF + f + 1)
                eng.sem_inc(w_ready, count)

            def turned(k):
                for i in range(2):
                    eng.wait_ge(xhi_ready, k * 2 + i + 1)
                    eng.tensor_tensor(xlo[:, 2 * i:2 * i + 2, :].rearrange("p c n -> p (c n)"), px[i][:, :],
                                      xhi[:, 2 * i:2 * i + 2, :].rearrange("p c n -> p (c n)").bitcast(F32),
                                      ALU.subtract).then_inc(xT_ready, 1)

            def gate(k, f):
                eng.wait_ge(tanh_done, k * NF + f + 1)
                eng.scalar_tensor_tensor(out=hid[RING3[f]][:, :], in0=hid[RING3[f]][:, :], scalar=1.0,
                                         in1=ph[RING4[f]][:, 0:SLOTS], op0=ALU.add, op1=ALU.mult).then_inc(gate_step, 1)

            def value(k, f):
                eng.wait_ge(gate_step, k * NF + f + 1)
                eng.scalar_tensor_tensor(out=hid[RING3[f]][:, :], in0=hid[RING3[f]][:, :], scalar=0.5,
                                         in1=ph[RING4[f]][:, SLOTS:2 * SLOTS], op0=ALU.mult, op1=ALU.mult).then_inc(val_done, 1)

            def hidden_lo(k, f):
                eng.wait_ge(hhi_done, k * NF + f + 1)
                eng.tensor_tensor(hlo[RING4[f]][:, :], hid[RING3[f]][:, :], hhi[RING4[f]][:, :].bitcast(F32),
                                  ALU.subtract).then_inc(hid_done, 1)

            def scan_one(scan, n):
                row, r, j = scan
                kind, i, c = SCAN[n]
                m = row * (GROUP - 1) + j
                at = m * NS + NS
                need = lambda *key: eng.wait_ge(scan_step, at + done[key])
                if kind == "p":
                    if i == 0:
                        eng.wait_ge(row_in, row * 32 + 32)
                    eng.wait_ge(bc_in[i], m * 16 + 16)
                    eng.wait_ge(scan_step, at - NS + done["r", i, 0])
                    ins = eng.tensor_tensor(hs[i][:, :, :], du[:, :, :], bcast(bc[i][:, 0:1, :], [P, 2, SEQ]), ALU.mult)
                elif kind == "s":
                    need("p", i, 0)
                    eng.wait_ge(dA_ready, m * 4 + i * 2 + c + 1)
                    ins = eng.tensor_tensor_scan(hs[i][:, c, :], dA[i][:, c, :], hs[i][:, c, :], 0.0, ALU.mult, ALU.add)
                elif kind == "q":
                    need("s", i, 1)
                    ins = eng.tensor_tensor(hs[i][:, :, :], hs[i][:, :, :], bcast(bc[i][:, 1:2, :], [P, 2, SEQ]), ALU.mult)
                else:
                    if i == 0:
                        eng.wait_ge(y_in, row * 16 + 16)
                    need("q", i, 0)
                    ins = eng.tensor_tensor(y[:, :, :], y[:, :, :], hs[i][:, :, :], ALU.add)
                ins.then_inc(scan_step, 1)

            def gate_y(row):
                eng.wait_ge(sr_in, row * 16 + 16)
                flat = lambda v: v[:, :, :].rearrange("p c n -> p (c n)")
                eng.scalar_tensor_tensor(out=flat(y), in0=flat(y), scalar=0.5, in1=flat(dA[0]),
                                         op0=ALU.mult, op1=ALU.mult).then_inc(y_final, 1)

            def body(k, scan, final, plain):
                def chunks(fs, fresh):
                    for f in fs:
                        if f == NF - 1:
                            hidden_lo(k, f - 1)
                            turned(k + 1)
                        gate(k, f)
                        if 0 < f < NF - 1:
                            hidden_lo(k, f - 1)
                        value(k, f)
                        if f == NF - 1:
                            hidden_lo(k, f)
                        if fresh:
                            if f + AHEAD < NF:
                                split(k, f + AHEAD)
                            else:
                                split(k + 1, f + AHEAD - NF)
                        if scan is not None:
                            for n in range(sum(STEPS[:f]), sum(STEPS[:f + 1])):
                                scan_one(scan, n)
                        if final is not False and f == NF - 3:
                            gate_y(final)

                def work(fresh):
                    if not fresh:
                        kept(k, AHEAD, NF - AHEAD)
                    chunks(range(NF - AHEAD), fresh)
                    then = meta(eng, 1, k + 1, 2)
                    with eng.If(then > 0):
                        chunks(range(NF - AHEAD, NF), True)
                    with eng.Else():
                        kept(k + 1, 0, AHEAD)
                        chunks(range(NF - AHEAD, NF), False)

                def no_rows():
                    kept(k, AHEAD, NF - AHEAD)
                    kept(k + 1, 0, AHEAD)
                    eng.wait_ge(val_done, k * NF + NF)
                    eng.wait_ge(hid_done, k * NF + NF)
                    eng.wait_ge(xT_ready, k * 2 + 2)
                    eng.sem_inc(gate_step, NF)
                    eng.sem_inc(val_done, NF)
                    eng.sem_inc(hid_done, NF)
                    eng.sem_inc(xT_ready, 2)
                    if scan is not None:
                        for n in range(NS):
                            scan_one(scan, n)
                    if final is not False:
                        gate_y(final)

                kind = meta(eng, 5, k, 2)
                with eng.If(kind > 0):
                    if plain:
                        work(True)
                    else:
                        with eng.If(kind > 1):
                            no_rows()
                        with eng.Else():
                            work(True)
                with eng.Else():
                    work(False)

            turned(0)
            for f in range(AHEAD):
                split(0, f)
            all_steps(eng, body)

def mamba_out_and_combine(nc, t, d):
    with ExitStack() as ctx:
        sb = lambda n, s, dt=F32: ctx.enter_context(nc.sbuf_tensor(n, s, dt))
        sem = lambda n: ctx.enter_context(nc.semaphore(n))
        NB = 4
        wo = sb("W_out", [P, CC, DM])
        yg = [sb(f"yg{i}", [P, CC, P]) for i in range(NB)]
        xs = [sb(f"xs{i}", [P, CC, P]) for i in range(NB)]
        xr = [sb(f"xr{i}", [P, DM]) for i in range(NB)]
        e1 = [sb(f"e1_{i}", [P, DM]) for i in range(NB)]
        e2 = [sb(f"e2_{i}", [P, DM]) for i in range(NB)]
        acc = [sb(f"acc{i}", [P, DM]) for i in range(NB)]
        sl = [sb(f"slot_now{i}", [P, TOP], U32) for i in range(NB)]
        wg = [sb(f"weight_now{i}", [P, TOP]) for i in range(NB)]
        pz = [ctx.enter_context(nc.psum_tensor(f"pz{i}", [P, DM], F32)) for i in range(NB)]
        wo_in = sem("wo_in")
        mm_in = [sem(f"mm_in{i}") for i in range(NB)]
        e_in = [sem(f"e_in{i}") for i in range(NB)]
        out_st = [sem(f"out_stored{i}") for i in range(NB)]
        proj = sem("proj")
        summed = sem("summed")
        sum_step = sem("sum_step")
        now = sem("slots_now")
        pool_sync = sem("pool_sync4")
        block = ctx.enter_context(nc.Block())
        ROUNDS = TT // NB

        @block.sync
        def _(eng):
            eng.dma_start(wo[:, :, :], d["W_out"].rearrange("(c p) n -> p c n", p=P)).then_inc(wo_in, 16)
            with eng.Fori(0, BATCH) as b:
                for k in range(TPB):
                    i = k % NB
                    tile = b * TPB + k
                    eng.wait_ge(summed, tile + 1)
                    for buf, name in ((yg, "yg"), (xs, "xs")):
                        for r in range(PAIRS):
                            eng.dma_start(buf[i][:, 2 * r:2 * r + 2, :], d[name][ds(b * PAIRS + r, 1), :, :, k * P:(k + 1) * P].rearrange(
                                "o p c n -> (o p) c n")).then_inc(mm_in[i], 16)
                    eng.dma_start(xr[i][:, :], d["x"][ds(tile * P, P), :]).then_inc(mm_in[i], 16)

        @block.gpsimd
        def _(eng):
            with eng.Fori(0, ROUNDS) as r:
                for i in range(NB):
                    tile = r * NB + i
                    eng.wait_ge(summed, tile + 1)
                    eng.sem_inc(pool_sync, 1)
                    eng.tensor_copy(sl[i][:, :], t.slot[:, :, ds(tile, 1)].rearrange("p k o -> p (k o)")).then_inc(now, 1)
                    eng.tensor_copy(wg[i][:, :], t.wgt[:, :, ds(tile, 1)].rearrange("p k o -> p (k o)")).then_inc(now, 1)
                    eng.wait_ge(now, tile * 2 + 2)
                    eng.sem_inc(pool_sync, 1)
                    for k, buf in enumerate((e1, e2)):
                        eng.indirect_dma_start(out=buf[i][:, :], out_offset=None, in_=d["ys"].rearrange("t s n -> (t s) n"),
                                               in_offset=bass.IndirectOffsetOnAxis(ap=sl[i][:, k:k + 1], axis=0)).then_inc(e_in[i], 16)

        @block.tensor
        def _(eng):
            eng.sem_inc(summed, NB)
            for i in range(NB):
                eng.sem_inc(out_st[i], 16)
            eng.wait_ge(wo_in, 16)
            with eng.Fori(0, ROUNDS) as r:
                for i in range(NB):
                    eng.wait_ge(mm_in[i], r * 80 + 80)
                    eng.wait_ge(summed, r * NB + i + 1)
                    for c in range(CC):
                        eng.matmul(pz[i][:, :], yg[i][:, c, :], wo[:, c, :], start=(c == 0), stop=False, skip_group_check=True)
                    for c in range(CC):
                        last = eng.matmul(pz[i][:, c * P:(c + 1) * P], xs[i][:, c, :], t.ident[:, :], start=False,
                                          stop=(c == CC - 1), skip_group_check=True)
                    last.then_inc(proj, 1)

        @block.vector
        def _(eng):
            with eng.Fori(0, ROUNDS) as r:
                for i in range(NB):
                    tile = r * NB + i
                    eng.wait_ge(proj, tile + 1)
                    eng.wait_ge(mm_in[i], r * 80 + 80)
                    eng.wait_ge(out_st[i], r * 16 + 16)
                    eng.tensor_tensor(acc[i][:, :], xr[i][:, :], pz[i][:, :], ALU.add).then_inc(sum_step, 1)
                    eng.wait_ge(e_in[i], r * 32 + 32)
                    eng.wait_ge(now, tile * 2 + 2)
                    for n, buf in enumerate((e1, e2)):
                        eng.wait_ge(sum_step, tile * 2 + n + 1)
                        ins = eng.scalar_tensor_tensor(out=acc[i][:, :], in0=buf[i][:, :], scalar=wg[i][:, n:n + 1],
                                                       in1=acc[i][:, :], op0=ALU.mult, op1=ALU.add)
                        ins.then_inc(sum_step if n < 1 else summed, 1)

        @block.scalar
        def _(eng):
            with eng.Fori(0, ROUNDS) as r:
                for i in range(NB):
                    tile = r * NB + i
                    eng.wait_ge(summed, tile + 1 + NB)
                    eng.dma_start(d["out"][ds(tile * P, P), :], acc[i][:, :]).then_inc(out_st[i], 16)
            for i in range(NB):
                eng.wait_ge(out_st[i], ROUNDS * 16 + 16)


class Shared:
    pass


def build(nc, d):
    d["xn"] = dram(nc, "xn_d", [TOKENS, DM])
    for name in ("sr", "xs", "ud", "delta", "du", "yg"):
        d[name] = dram(nc, f"{name}_d", [ROWS + 1, P, 2, SEQ])
    d["bc"] = dram(nc, "bc_d", [ROWS * NST + 2, 2, SEQ])
    d["xnT"] = dram(nc, "xnT_d", [BATCH + 1, P, DC, SEQ])
    d["ids"] = dram(nc, "ids_d", [P * IDW, 1], U32)
    d["ys"] = dram(nc, "ys_d", [NT, SLOTS, DM])
    with ExitStack() as ctx:
        sem = lambda n: ctx.enter_context(nc.semaphore(n))
        sb = lambda n, s, dt=F32: ctx.enter_context(nc.sbuf_tensor(n, s, dt))
        t = Shared()
        t.ident = sb("ident", [P, P])
        t.ones = sb("ones", [P, P])
        t.A = sb("A", [P, CC * NST])
        t.ids = sb("ids", [P, IDW], U32)
        t.slot = sb("slot", [P, TOP, TT], U32)
        t.wgt = sb("wgt", [P, TOP, TT])
        t.meta = sb("meta", [P, 6, NK + 2], I32)
        t.gate_in = sem("gate_in")
        t.small_in = sem("small_in")
        t.w_in = sem("w_in")
        t.xn_in = sem("xn_in")
        t.const_ready = sem("const_ready")
        t.ids_zeroed = sem("ids_zeroed")
        t.ids_written = sem("ids_written")
        t.ids_loaded = sem("ids_loaded")
        t.logits_ready = sem("logits_ready")
        t.a_step = sem("a_step")
        with ExitStack() as front:
            fsb = lambda n, s, dt=F32: front.enter_context(nc.sbuf_tensor(n, s, dt))
            t.xn_b = fsb("xn_b", [P, DC, SEQ])
            t.W_in = fsb("W_in", [P, DC, 2 * DIN])
            t.W_x = fsb("W_x", [P, CC, NX])
            t.W_dt = fsb("W_dt", [P, DIN])
            t.gate = fsb("gate", [P, DC, E])
            t.conv_b = fsb("conv_b", [P, CC])
            t.b_dt = fsb("b_dt", [P, CC])
            t.D = fsb("D", [P, CC])
            t.A_log = fsb("A_log", [P, CC, NST])
            t.tri = fsb("tri", [P, P])
            t.tok_id = fsb("tok_id", [P, TT], U32)
            t.num_i = fsb("num_i", [P, NK + 2], I32)
            t.num = fsb("num", [P, NK + 2])
            t.zero_ids = fsb("zero_ids", [P, IDW], U32)
            t.prob = fsb("prob", [P, TT, E])
            t.red = fsb("red", [P, TT])
            t.red2 = fsb("red2", [P, TT])
            t.top = fsb("top", [P, TT, 8])
            t.topi = fsb("topi", [P, TT, 8], U32)
            t.topf = fsb("topf", [P, TOP, TT])
            t.hot = fsb("hot", [P, TOP, TT, E])
            t.mask = fsb("mask", [P, TT, E])
            t.tot = fsb("tot", [P, E, TT])
            t.cum = fsb("cum", [P, E, TT])
            t.cnt_i = fsb("cnt_i", [P, E], I32)
            t.ntile = fsb("ntile", [P, E])
            t.last_tile = fsb("last_tile", [P, E])
            t.base = fsb("base", [P, E])
            t.place = fsb("place", [P, TOP, TT], U32)
            t.place2 = fsb("place2", [P, TOP, TT], U32)
            t.ps_lg = front.enter_context(nc.psum_tensor("ps_lg", [P, HALF], F32))
            norm_and_route_logits(nc, t, d)
            mamba_front(nc, t, d)
        experts_and_scan(nc, t, d)
        mamba_out_and_combine(nc, t, d)


def kernel(**inputs):
    import numpy as np
    import concourse.bacc as bacc
    from concourse.bass_utils import run_bass_kernel_spmd

    lay = {
        "x": inputs["L0_attn_x"].reshape(TOKENS, DM),
        "W_in": inputs["L0_attn_W_in"],
        "conv_w": np.transpose(np.asarray(inputs["L0_attn_conv_w"]), (2, 1, 0)),
        "conv_b": np.asarray(inputs["L0_attn_conv_b"]).reshape(CC, P).T,
        "W_x": inputs["L0_attn_W_x"],
        "W_dt": inputs["L0_attn_W_dt"],
        "b_dt": np.asarray(inputs["L0_attn_b_dt"]).reshape(CC, P).T,
        "A_log": inputs["L0_attn_A_log"],
        "D": np.asarray(inputs["L0_attn_D"]).reshape(CC, P).T,
        "W_out": inputs["L0_attn_W_out"],
        "gate_w": inputs["L0_ffn_gate_w"],
        "w1": inputs["L0_ffn_w1"],
        "w2": inputs["L0_ffn_w2"],
        "w3": inputs["L0_ffn_w3"],
    }
    nc = bacc.Bacc("TRN2", target_bir_lowering=False, num_devices=1)
    arrays, d = {}, {}
    for name, a in lay.items():
        a = np.ascontiguousarray(a)
        arrays[f"in_{name}"] = a
        d[name] = nc.dram_tensor(f"in_{name}", a.shape, mybir.dt.from_np(a.dtype), kind="ExternalInput").ap()
    d["out"] = nc.dram_tensor("out_0", (TOKENS, DM), F32, kind="ExternalOutput").ap()
    build(nc, d)
    r = run_bass_kernel_spmd(nc, [arrays], core_ids=[0])
    return r.results[0]["out_0"].reshape(BATCH, SEQ, DM)
```
